# Optimizing a Trainium2 kernel written in Bass

```python
import numpy as np
import jax
import jax.numpy as jnp

def _softmax(x, axis=-1):
    return jax.nn.softmax(x, axis=axis)

def _gelu(x):
    return jax.nn.gelu(x, approximate=True)

def _silu(x):
    return jax.nn.silu(x)

def _sigmoid(x):
    return jax.nn.sigmoid(x)

def _layernorm(x, axis=-1, eps=1e-05):
    m = jnp.mean(x, axis=axis, keepdims=True)
    v = jnp.var(x, axis=axis, keepdims=True)
    return (x - m) / jnp.sqrt(v + eps)

def _scatter_add(tgt, idx, src, axis=0):
    return tgt.at[idx].add(src)

def _segment_sum(src, seg, n):
    return jax.ops.segment_sum(src, seg, n)
kernel_name = 'mk_hybrid_d1_jaxref_r8_3946aa'

def setup_inputs(seed: int=0):
    np.random.seed(seed)
    _w = jnp.asarray

    def _L0_attn_a_setup():
        import jax, jax.numpy as jnp
        import numpy as np
        GAMMA = 0.9
        SCALE_BASE = 512.0

        def _xpos(x, downscale=False):
            B, L, D = x.shape
            half = D // 2
            scale_vec = (jnp.arange(0, D, 2, dtype=jnp.float32) + 0.4 * D) / (1.4 * D)
            power = jnp.arange(L, dtype=jnp.float32) / SCALE_BASE
            scale = scale_vec[None, :] ** power[:, None]
            if downscale:
                scale = 1.0 / scale
            inv_freq = 1.0 / 10000.0 ** (jnp.arange(half, dtype=jnp.float32) / half)
            sinusoid = jnp.arange(L, dtype=jnp.float32)[:, None] * inv_freq[None, :]
            sin = jnp.repeat(jnp.sin(sinusoid) * scale, 2, axis=-1)
            cos = jnp.repeat(jnp.cos(sinusoid) * scale, 2, axis=-1)
            x_even = x[..., 0::2]
            x_odd = x[..., 1::2]
            rot = jnp.stack((-x_odd, x_even), axis=-1).reshape(x.shape)
            return x * cos + rot * sin

        def _get_D(seq_len):
            n = jnp.arange(seq_len, dtype=jnp.float32)[:, None]
            m = jnp.arange(seq_len, dtype=jnp.float32)[None, :]
            D = GAMMA ** jnp.abs(n - m)
            return D
        key = jax.random.key(seed)
        k1, k2, k3, k4 = jax.random.split(key, 4)
        B, L, H, Dh = (8, 256, 128, 128)
        X = jax.random.normal(k1, (B, L, H), dtype=jnp.float32)
        W_Q = jax.random.normal(k2, (H, Dh), dtype=jnp.float32) / H
        W_K = jax.random.normal(k3, (H, Dh), dtype=jnp.float32) / H
        W_V = jax.random.normal(k4, (H, Dh), dtype=jnp.float32) / H
        return {'X': X, 'W_Q': W_Q, 'W_K': W_K, 'W_V': W_V}
    _L0_attn_a_in = _L0_attn_a_setup()

    def _L0_attn_b_setup():
        import jax, jax.numpy as jnp
        import numpy as np
        B, T, NE, H = (4, 128, 128, 16)
        HS = NE // H
        EPS = 0.00064

        def _forward(x, time_maa_x, time_maa, maa_w1, maa_w2, decay_w1, decay_w2, aaa_w1, aaa_w2, kkk_w1, kkk_w2, gate_w1, gate_w2, ma_w1, ma_w2, mk_w1, mk_w2, time_decay, time_faaaa, time_aaaaa, time_misc_a, time_misc_k, Wr, Wk, Wv, Wo, ln_w, ln_b):
            Bx, Tx, C = x.shape
            xx = jnp.pad(x, ((0, 0), (1, 0), (0, 0)))[:, :Tx] - x
            mix = x + xx * time_maa_x
            lo = jnp.tanh(jnp.einsum('btc,dc->btd', mix, maa_w1)).reshape(Bx, Tx, 4, 32)
            lo = jnp.einsum('btgk,gkc->gbtc', lo, maa_w2)
            xm = x[None] + xx[None] * (lo + time_maa)
            xrg, xwa, xk, xv = (xm[0], xm[1], xm[2], xm[3])
            r = xrg @ Wr.T
            g = jnp.tanh(xrg @ gate_w1.T) @ gate_w2
            k = xk @ Wk.T
            v = xv @ Wv.T
            w2 = jnp.tanh(xwa @ decay_w1.T) @ decay_w2
            w = -jax.nn.softplus(-(time_decay + w2)) - 0.5
            kk = k + jnp.tanh(xk @ kkk_w1.T) @ kkk_w2
            kkh = kk.reshape(Bx, Tx, H, HS)
            kk = (kkh / jnp.maximum(jnp.linalg.norm(kkh, axis=-1, keepdims=True), 1e-12)).reshape(Bx, Tx, C)
            a = jax.nn.sigmoid(time_aaaaa + xwa @ aaa_w1.T @ aaa_w2)
            ma = jax.nn.sigmoid(time_misc_a + xwa @ ma_w1.T @ ma_w2)
            k = k * ma + k * a * (1.0 - ma)
            mk = jax.nn.sigmoid(time_misc_k + xk @ mk_w1.T @ mk_w2)
            k = k * jnp.exp(w * mk)
            b = -kk * a

            def to_th(t):
                return t.reshape(Bx, Tx, H, HS).transpose(1, 0, 2, 3)
            qt, wt, kt, vt, at, bt = map(to_th, (r, w, k, v, kk, b))
            wt = jnp.exp(-jnp.exp(wt))

            def step(s, inp):
                q_, w_, k_, v_, a_, b_ = inp
                sa = jnp.einsum('bhij,bhj->bhi', s, a_)
                s = s * w_[:, :, None, :] + sa[..., None] * b_[:, :, None, :] + v_[..., None] * k_[:, :, None, :]
                return (s, jnp.einsum('bhij,bhj->bhi', s, q_))
            s0 = jnp.zeros((Bx, H, HS, HS), x.dtype)
            _, y = jax.lax.scan(step, s0, (qt, wt, kt, vt, at, bt))
            y = y.transpose(1, 0, 2, 3).reshape(Bx, Tx, C)
            yg = y.reshape(Bx, Tx, H, HS)
            mu = yg.mean(-1, keepdims=True)
            var = ((yg - mu) ** 2).mean(-1, keepdims=True)
            y = ((yg - mu) / jnp.sqrt(var + EPS)).reshape(Bx, Tx, C) * ln_w + ln_b
            rk = (r.reshape(Bx, Tx, H, HS) * k.reshape(Bx, Tx, H, HS) * time_faaaa.reshape(H, HS)).sum(-1, keepdims=True)
            y = y + (rk * v.reshape(Bx, Tx, H, HS)).reshape(Bx, Tx, C)
            return y * g @ Wo.T
        key = jax.random.key(seed)
        ks = jax.random.split(key, 30)

        def rn(k, shape, s):
            return jax.random.normal(k, shape, jnp.float32) * s
        d = {}
        d['x'] = jax.random.normal(ks[0], (B, T, NE), jnp.float32)
        d['time_maa_x'] = jax.random.uniform(ks[1], (NE,), jnp.float32)
        d['time_maa'] = jax.random.uniform(ks[2], (4, 1, 1, NE), jnp.float32)
        d['maa_w1'] = rn(ks[3], (128, NE), 0.02)
        d['maa_w2'] = rn(ks[4], (4, 32, NE), 0.02)
        d['decay_w1'] = rn(ks[5], (64, NE), 0.02)
        d['decay_w2'] = rn(ks[6], (64, NE), 0.02)
        d['aaa_w1'] = rn(ks[7], (16, NE), 0.02)
        d['aaa_w2'] = rn(ks[8], (16, NE), 0.02)
        d['kkk_w1'] = rn(ks[9], (16, NE), 0.02)
        d['kkk_w2'] = rn(ks[10], (16, NE), 0.02)
        d['gate_w1'] = rn(ks[11], (128, NE), 0.02)
        d['gate_w2'] = rn(ks[12], (128, NE), 0.02)
        d['ma_w1'] = rn(ks[13], (16, NE), 0.02)
        d['ma_w2'] = rn(ks[14], (16, NE), 0.02)
        d['mk_w1'] = rn(ks[15], (16, NE), 0.02)
        d['mk_w2'] = rn(ks[16], (16, NE), 0.02)
        d['time_decay'] = jnp.linspace(-6.5, -1.5, NE, dtype=jnp.float32)
        d['time_faaaa'] = rn(ks[17], (NE,), 0.02)
        d['time_aaaaa'] = rn(ks[18], (NE,), 0.02)
        d['time_misc_a'] = rn(ks[19], (NE,), 0.02)
        d['time_misc_k'] = rn(ks[20], (NE,), 0.02)
        d['Wr'] = rn(ks[21], (NE, NE), 0.5 / NE ** 0.5)
        d['Wk'] = rn(ks[22], (NE, NE), 0.05 / NE ** 0.5)
        d['Wv'] = rn(ks[23], (NE, NE), 0.5 / NE ** 0.5)
        d['Wo'] = rn(ks[24], (NE, NE), 1.0 / NE ** 0.5)
        d['ln_w'] = jnp.ones((NE,), jnp.float32)
        d['ln_b'] = jnp.zeros((NE,), jnp.float32)
        return d
    _L0_attn_b_in = _L0_attn_b_setup()

    def _L0_ffn_setup():
        import jax, jax.numpy as jnp
        import numpy as np
        DIM = 128
        DEPTH = 6
        HEADS = 16
        DIM_HEAD = 64
        WINDOW = 32
        INNER = HEADS * DIM_HEAD
        DIM_INNER = int(DIM * 4 * 2 / 3)
        QK_SCALE = 8.0

        def shift_tokens(t):
            a, s = jnp.split(t, 2, -1)
            s = jnp.pad(s, ((0, 0), (1, 0), (0, 0)))[:, :-1]
            return jnp.concatenate([a, s], -1)

        def l2norm(t):
            return t / jnp.maximum(jnp.linalg.norm(t, axis=-1, keepdims=True), 1e-12)

        def rotate_half(x):
            x1, x2 = jnp.split(x, 2, -1)
            return jnp.concatenate([-x2, x1], -1)

        def rotary_tables(n):
            half = jnp.arange(0, DIM_HEAD, 2, dtype=jnp.float32)
            inv_freq = 1.0 / 10000.0 ** (half / DIM_HEAD)
            t = jnp.arange(n, dtype=jnp.float32)
            freqs = t[:, None] * inv_freq[None, :]
            freqs = jnp.concatenate([freqs, freqs], -1)
            base_scale = (half + 0.4 * DIM_HEAD) / (1.4 * DIM_HEAD)
            power = (t - n // 2) / (WINDOW // 2)
            scale = base_scale[None, :] ** power[:, None]
            scale = jnp.concatenate([scale, scale], -1)
            return (freqs, scale)

        def local_attention(q, k, v):
            b, h, n, d = q.shape
            w = WINDOW
            nw = n // w
            bq = q.reshape(b, h, nw, w, d)
            bk = k.reshape(b, h, nw, w, d)
            bv = v.reshape(b, h, nw, w, d)

            def look(t):
                p = jnp.pad(t, ((0, 0), (0, 0), (1, 0), (0, 0), (0, 0)))
                return jnp.concatenate([p[:, :, :nw], p[:, :, 1:]], axis=3)
            bk2, bv2 = (look(bk), look(bv))
            seq = jnp.arange(n).reshape(nw, w)
            seq_p = jnp.pad(seq, ((1, 0), (0, 0)), constant_values=-1)
            jt = jnp.concatenate([seq_p[:nw], seq_p[1:]], axis=1)
            it = seq[:, :, None]
            jb = jt[:, None, :]
            mask = (it < jb) | (it > jb + w) | (jb == -1)
            sim = jnp.einsum('bhwie,bhwje->bhwij', bq, bk2) * QK_SCALE
            sim = jnp.where(mask, -jnp.finfo(sim.dtype).max, sim)
            attn = jax.nn.softmax(sim, -1)
            out = jnp.einsum('bhwij,bhwje->bhwie', attn, bv2)
            return out.reshape(b, h, n, d)

        def attn_layer(x, Wqkv, qs, ksc, Wo):
            b, n, _ = x.shape
            qkv = x @ Wqkv
            q, k, v = jnp.split(qkv, 3, -1)
            sh = lambda t: t.reshape(b, n, HEADS, DIM_HEAD).transpose(0, 2, 1, 3)
            q, k, v = (sh(q), sh(k), sh(v))
            q = l2norm(q) * qs
            k = l2norm(k) * ksc
            freqs, scale = rotary_tables(n)
            cos, sin = (jnp.cos(freqs), jnp.sin(freqs))
            q = q * cos * scale + rotate_half(q) * sin * scale
            inv = 1.0 / scale
            k = k * cos * inv + rotate_half(k) * sin * inv
            out = local_attention(q, k, v)
            out = out.transpose(0, 2, 1, 3).reshape(b, n, INNER)
            return out @ Wo

        def ffn_layer(x, g, bln, W1, b1, W2, b2):
            mu = x.mean(-1, keepdims=True)
            var = ((x - mu) ** 2).mean(-1, keepdims=True)
            xn = (x - mu) / jnp.sqrt(var + 1e-05) * g + bln
            hg = xn @ W1 + b1
            a, gate = jnp.split(hg, 2, -1)
            return a * jax.nn.gelu(gate, approximate=False) @ W2 + b2
        key = jax.random.key(seed)
        ks = jax.random.split(key, 8)
        B, N = (2, 256)
        init = lambda k, shape: jax.random.normal(k, shape, jnp.float32) * 0.02
        return {'x': jax.random.normal(ks[0], (B, N, DIM), jnp.float32), 'Wqkv': init(ks[1], (DEPTH, DIM, 3 * INNER)), 'q_scale': jnp.ones((DEPTH, DIM_HEAD), jnp.float32), 'k_scale': jnp.ones((DEPTH, DIM_HEAD), jnp.float32), 'Wo': init(ks[2], (DEPTH, INNER, DIM)), 'ln_g': jnp.ones((DEPTH, DIM), jnp.float32), 'ln_b': jnp.zeros((DEPTH, DIM), jnp.float32), 'W1': init(ks[3], (DEPTH, DIM, 2 * DIM_INNER)), 'b1': jnp.zeros((DEPTH, 2 * DIM_INNER), jnp.float32), 'W2': init(ks[4], (DEPTH, DIM_INNER, DIM)), 'b2': jnp.zeros((DEPTH, DIM), jnp.float32)}
    _L0_ffn_in = _L0_ffn_setup()
    _d = {'L0_attn_a_X': _L0_attn_a_in['X'], 'L0_attn_a_W_Q': _L0_attn_a_in['W_Q'], 'L0_attn_a_W_K': _L0_attn_a_in['W_K'], 'L0_attn_a_W_V': _L0_attn_a_in['W_V'], 'L0_attn_b_time_maa_x': _L0_attn_b_in['time_maa_x'], 'L0_attn_b_time_maa': _L0_attn_b_in['time_maa'], 'L0_attn_b_maa_w1': _L0_attn_b_in['maa_w1'], 'L0_attn_b_maa_w2': _L0_attn_b_in['maa_w2'], 'L0_attn_b_decay_w1': _L0_attn_b_in['decay_w1'], 'L0_attn_b_decay_w2': _L0_attn_b_in['decay_w2'], 'L0_attn_b_aaa_w1': _L0_attn_b_in['aaa_w1'], 'L0_attn_b_aaa_w2': _L0_attn_b_in['aaa_w2'], 'L0_attn_b_kkk_w1': _L0_attn_b_in['kkk_w1'], 'L0_attn_b_kkk_w2': _L0_attn_b_in['kkk_w2'], 'L0_attn_b_gate_w1': _L0_attn_b_in['gate_w1'], 'L0_attn_b_gate_w2': _L0_attn_b_in['gate_w2'], 'L0_attn_b_ma_w1': _L0_attn_b_in['ma_w1'], 'L0_attn_b_ma_w2': _L0_attn_b_in['ma_w2'], 'L0_attn_b_mk_w1': _L0_attn_b_in['mk_w1'], 'L0_attn_b_mk_w2': _L0_attn_b_in['mk_w2'], 'L0_attn_b_time_decay': _L0_attn_b_in['time_decay'], 'L0_attn_b_time_faaaa': _L0_attn_b_in['time_faaaa'], 'L0_attn_b_time_aaaaa': _L0_attn_b_in['time_aaaaa'], 'L0_attn_b_time_misc_a': _L0_attn_b_in['time_misc_a'], 'L0_attn_b_time_misc_k': _L0_attn_b_in['time_misc_k'], 'L0_attn_b_Wr': _L0_attn_b_in['Wr'], 'L0_attn_b_Wk': _L0_attn_b_in['Wk'], 'L0_attn_b_Wv': _L0_attn_b_in['Wv'], 'L0_attn_b_Wo': _L0_attn_b_in['Wo'], 'L0_attn_b_ln_w': _L0_attn_b_in['ln_w'], 'L0_attn_b_ln_b': _L0_attn_b_in['ln_b'], 'L0_ffn_Wqkv': _L0_ffn_in['Wqkv'], 'L0_ffn_q_scale': _L0_ffn_in['q_scale'], 'L0_ffn_k_scale': _L0_ffn_in['k_scale'], 'L0_ffn_Wo': _L0_ffn_in['Wo'], 'L0_ffn_ln_g': _L0_ffn_in['ln_g'], 'L0_ffn_ln_b': _L0_ffn_in['ln_b'], 'L0_ffn_W1': _L0_ffn_in['W1'], 'L0_ffn_b1': _L0_ffn_in['b1'], 'L0_ffn_W2': _L0_ffn_in['W2'], 'L0_ffn_b2': _L0_ffn_in['b2']}
    _x0 = _d['L0_attn_a_X']
    _d['L0_attn_a_X'] = jax.random.normal(jax.random.fold_in(jax.random.key(seed), 1), (4, 512, 128), dtype=_x0.dtype)
    del _x0
    return _d

def reference(L0_attn_a_X, L0_attn_a_W_Q, L0_attn_a_W_K, L0_attn_a_W_V, L0_attn_b_time_maa_x, L0_attn_b_time_maa, L0_attn_b_maa_w1, L0_attn_b_maa_w2, L0_attn_b_decay_w1, L0_attn_b_decay_w2, L0_attn_b_aaa_w1, L0_attn_b_aaa_w2, L0_attn_b_kkk_w1, L0_attn_b_kkk_w2, L0_attn_b_gate_w1, L0_attn_b_gate_w2, L0_attn_b_ma_w1, L0_attn_b_ma_w2, L0_attn_b_mk_w1, L0_attn_b_mk_w2, L0_attn_b_time_decay, L0_attn_b_time_faaaa, L0_attn_b_time_aaaaa, L0_attn_b_time_misc_a, L0_attn_b_time_misc_k, L0_attn_b_Wr, L0_attn_b_Wk, L0_attn_b_Wv, L0_attn_b_Wo, L0_attn_b_ln_w, L0_attn_b_ln_b, L0_ffn_Wqkv, L0_ffn_q_scale, L0_ffn_k_scale, L0_ffn_Wo, L0_ffn_ln_g, L0_ffn_ln_b, L0_ffn_W1, L0_ffn_b1, L0_ffn_W2, L0_ffn_b2):

    def _L0_attn_a_ref(X, W_Q, W_K, W_V):
        import jax, jax.numpy as jnp
        import numpy as np
        GAMMA = 0.9
        SCALE_BASE = 512.0

        def _xpos(x, downscale=False):
            B, L, D = x.shape
            half = D // 2
            scale_vec = (jnp.arange(0, D, 2, dtype=jnp.float32) + 0.4 * D) / (1.4 * D)
            power = jnp.arange(L, dtype=jnp.float32) / SCALE_BASE
            scale = scale_vec[None, :] ** power[:, None]
            if downscale:
                scale = 1.0 / scale
            inv_freq = 1.0 / 10000.0 ** (jnp.arange(half, dtype=jnp.float32) / half)
            sinusoid = jnp.arange(L, dtype=jnp.float32)[:, None] * inv_freq[None, :]
            sin = jnp.repeat(jnp.sin(sinusoid) * scale, 2, axis=-1)
            cos = jnp.repeat(jnp.cos(sinusoid) * scale, 2, axis=-1)
            x_even = x[..., 0::2]
            x_odd = x[..., 1::2]
            rot = jnp.stack((-x_odd, x_even), axis=-1).reshape(x.shape)
            return x * cos + rot * sin

        def _get_D(seq_len):
            n = jnp.arange(seq_len, dtype=jnp.float32)[:, None]
            m = jnp.arange(seq_len, dtype=jnp.float32)[None, :]
            D = GAMMA ** jnp.abs(n - m)
            return D
        B, L, H = X.shape
        D = _get_D(L)
        Q = _xpos(X @ W_Q)
        K = _xpos(X @ W_K, downscale=True)
        V = X @ W_V
        scores = jnp.einsum('bqd,bkd->bqk', Q, K)
        p_attn = jax.nn.softmax(scores, axis=-1)
        p_attn = p_attn * D[None, :, :]
        return jnp.einsum('bqk,bkv->bqv', p_attn, V)

    def _L0_attn_b_ref(x, time_maa_x, time_maa, maa_w1, maa_w2, decay_w1, decay_w2, aaa_w1, aaa_w2, kkk_w1, kkk_w2, gate_w1, gate_w2, ma_w1, ma_w2, mk_w1, mk_w2, time_decay, time_faaaa, time_aaaaa, time_misc_a, time_misc_k, Wr, Wk, Wv, Wo, ln_w, ln_b):
        import jax, jax.numpy as jnp
        import numpy as np
        B, T, NE, H = (4, 128, 128, 16)
        HS = NE // H
        EPS = 0.00064

        def _forward(x, time_maa_x, time_maa, maa_w1, maa_w2, decay_w1, decay_w2, aaa_w1, aaa_w2, kkk_w1, kkk_w2, gate_w1, gate_w2, ma_w1, ma_w2, mk_w1, mk_w2, time_decay, time_faaaa, time_aaaaa, time_misc_a, time_misc_k, Wr, Wk, Wv, Wo, ln_w, ln_b):
            Bx, Tx, C = x.shape
            xx = jnp.pad(x, ((0, 0), (1, 0), (0, 0)))[:, :Tx] - x
            mix = x + xx * time_maa_x
            lo = jnp.tanh(jnp.einsum('btc,dc->btd', mix, maa_w1)).reshape(Bx, Tx, 4, 32)
            lo = jnp.einsum('btgk,gkc->gbtc', lo, maa_w2)
            xm = x[None] + xx[None] * (lo + time_maa)
            xrg, xwa, xk, xv = (xm[0], xm[1], xm[2], xm[3])
            r = xrg @ Wr.T
            g = jnp.tanh(xrg @ gate_w1.T) @ gate_w2
            k = xk @ Wk.T
            v = xv @ Wv.T
            w2 = jnp.tanh(xwa @ decay_w1.T) @ decay_w2
            w = -jax.nn.softplus(-(time_decay + w2)) - 0.5
            kk = k + jnp.tanh(xk @ kkk_w1.T) @ kkk_w2
            kkh = kk.reshape(Bx, Tx, H, HS)
            kk = (kkh / jnp.maximum(jnp.linalg.norm(kkh, axis=-1, keepdims=True), 1e-12)).reshape(Bx, Tx, C)
            a = jax.nn.sigmoid(time_aaaaa + xwa @ aaa_w1.T @ aaa_w2)
            ma = jax.nn.sigmoid(time_misc_a + xwa @ ma_w1.T @ ma_w2)
            k = k * ma + k * a * (1.0 - ma)
            mk = jax.nn.sigmoid(time_misc_k + xk @ mk_w1.T @ mk_w2)
            k = k * jnp.exp(w * mk)
            b = -kk * a

            def to_th(t):
                return t.reshape(Bx, Tx, H, HS).transpose(1, 0, 2, 3)
            qt, wt, kt, vt, at, bt = map(to_th, (r, w, k, v, kk, b))
            wt = jnp.exp(-jnp.exp(wt))

            def step(s, inp):
                q_, w_, k_, v_, a_, b_ = inp
                sa = jnp.einsum('bhij,bhj->bhi', s, a_)
                s = s * w_[:, :, None, :] + sa[..., None] * b_[:, :, None, :] + v_[..., None] * k_[:, :, None, :]
                return (s, jnp.einsum('bhij,bhj->bhi', s, q_))
            s0 = jnp.zeros((Bx, H, HS, HS), x.dtype)
            _, y = jax.lax.scan(step, s0, (qt, wt, kt, vt, at, bt))
            y = y.transpose(1, 0, 2, 3).reshape(Bx, Tx, C)
            yg = y.reshape(Bx, Tx, H, HS)
            mu = yg.mean(-1, keepdims=True)
            var = ((yg - mu) ** 2).mean(-1, keepdims=True)
            y = ((yg - mu) / jnp.sqrt(var + EPS)).reshape(Bx, Tx, C) * ln_w + ln_b
            rk = (r.reshape(Bx, Tx, H, HS) * k.reshape(Bx, Tx, H, HS) * time_faaaa.reshape(H, HS)).sum(-1, keepdims=True)
            y = y + (rk * v.reshape(Bx, Tx, H, HS)).reshape(Bx, Tx, C)
            return y * g @ Wo.T
        return _forward(x, time_maa_x, time_maa, maa_w1, maa_w2, decay_w1, decay_w2, aaa_w1, aaa_w2, kkk_w1, kkk_w2, gate_w1, gate_w2, ma_w1, ma_w2, mk_w1, mk_w2, time_decay, time_faaaa, time_aaaaa, time_misc_a, time_misc_k, Wr, Wk, Wv, Wo, ln_w, ln_b)

    def _L0_ffn_ref(x, Wqkv, q_scale, k_scale, Wo, ln_g, ln_b, W1, b1, W2, b2):
        import jax, jax.numpy as jnp
        import numpy as np
        DIM = 128
        DEPTH = 6
        HEADS = 16
        DIM_HEAD = 64
        WINDOW = 32
        INNER = HEADS * DIM_HEAD
        DIM_INNER = int(DIM * 4 * 2 / 3)
        QK_SCALE = 8.0

        def shift_tokens(t):
            a, s = jnp.split(t, 2, -1)
            s = jnp.pad(s, ((0, 0), (1, 0), (0, 0)))[:, :-1]
            return jnp.concatenate([a, s], -1)

        def l2norm(t):
            return t / jnp.maximum(jnp.linalg.norm(t, axis=-1, keepdims=True), 1e-12)

        def rotate_half(x):
            x1, x2 = jnp.split(x, 2, -1)
            return jnp.concatenate([-x2, x1], -1)

        def rotary_tables(n):
            half = jnp.arange(0, DIM_HEAD, 2, dtype=jnp.float32)
            inv_freq = 1.0 / 10000.0 ** (half / DIM_HEAD)
            t = jnp.arange(n, dtype=jnp.float32)
            freqs = t[:, None] * inv_freq[None, :]
            freqs = jnp.concatenate([freqs, freqs], -1)
            base_scale = (half + 0.4 * DIM_HEAD) / (1.4 * DIM_HEAD)
            power = (t - n // 2) / (WINDOW // 2)
            scale = base_scale[None, :] ** power[:, None]
            scale = jnp.concatenate([scale, scale], -1)
            return (freqs, scale)

        def local_attention(q, k, v):
            b, h, n, d = q.shape
            w = WINDOW
            nw = n // w
            bq = q.reshape(b, h, nw, w, d)
            bk = k.reshape(b, h, nw, w, d)
            bv = v.reshape(b, h, nw, w, d)

            def look(t):
                p = jnp.pad(t, ((0, 0), (0, 0), (1, 0), (0, 0), (0, 0)))
                return jnp.concatenate([p[:, :, :nw], p[:, :, 1:]], axis=3)
            bk2, bv2 = (look(bk), look(bv))
            seq = jnp.arange(n).reshape(nw, w)
            seq_p = jnp.pad(seq, ((1, 0), (0, 0)), constant_values=-1)
            jt = jnp.concatenate([seq_p[:nw], seq_p[1:]], axis=1)
            it = seq[:, :, None]
            jb = jt[:, None, :]
            mask = (it < jb) | (it > jb + w) | (jb == -1)
            sim = jnp.einsum('bhwie,bhwje->bhwij', bq, bk2) * QK_SCALE
            sim = jnp.where(mask, -jnp.finfo(sim.dtype).max, sim)
            attn = jax.nn.softmax(sim, -1)
            out = jnp.einsum('bhwij,bhwje->bhwie', attn, bv2)
            return out.reshape(b, h, n, d)

        def attn_layer(x, Wqkv, qs, ksc, Wo):
            b, n, _ = x.shape
            qkv = x @ Wqkv
            q, k, v = jnp.split(qkv, 3, -1)
            sh = lambda t: t.reshape(b, n, HEADS, DIM_HEAD).transpose(0, 2, 1, 3)
            q, k, v = (sh(q), sh(k), sh(v))
            q = l2norm(q) * qs
            k = l2norm(k) * ksc
            freqs, scale = rotary_tables(n)
            cos, sin = (jnp.cos(freqs), jnp.sin(freqs))
            q = q * cos * scale + rotate_half(q) * sin * scale
            inv = 1.0 / scale
            k = k * cos * inv + rotate_half(k) * sin * inv
            out = local_attention(q, k, v)
            out = out.transpose(0, 2, 1, 3).reshape(b, n, INNER)
            return out @ Wo

        def ffn_layer(x, g, bln, W1, b1, W2, b2):
            mu = x.mean(-1, keepdims=True)
            var = ((x - mu) ** 2).mean(-1, keepdims=True)
            xn = (x - mu) / jnp.sqrt(var + 1e-05) * g + bln
            hg = xn @ W1 + b1
            a, gate = jnp.split(hg, 2, -1)
            return a * jax.nn.gelu(gate, approximate=False) @ W2 + b2
        for i in range(DEPTH):
            x = attn_layer(shift_tokens(x), Wqkv[i], q_scale[i], k_scale[i], Wo[i]) + x
            x = ffn_layer(shift_tokens(x), ln_g[i], ln_b[i], W1[i], b1[i], W2[i], b2[i]) + x
        return x
    x = L0_attn_a_X
    x = x + _L0_attn_a_ref(_layernorm(x, axis=-1), L0_attn_a_W_Q, L0_attn_a_W_K, L0_attn_a_W_V)
    x = x + _L0_ffn_ref(_layernorm(x, axis=-1), L0_ffn_Wqkv, L0_ffn_q_scale, L0_ffn_k_scale, L0_ffn_Wo, L0_ffn_ln_g, L0_ffn_ln_b, L0_ffn_W1, L0_ffn_b1, L0_ffn_W2, L0_ffn_b2)
    x = x + _L0_attn_b_ref(_layernorm(x, axis=-1), L0_attn_b_time_maa_x, L0_attn_b_time_maa, L0_attn_b_maa_w1, L0_attn_b_maa_w2, L0_attn_b_decay_w1, L0_attn_b_decay_w2, L0_attn_b_aaa_w1, L0_attn_b_aaa_w2, L0_attn_b_kkk_w1, L0_attn_b_kkk_w2, L0_attn_b_gate_w1, L0_attn_b_gate_w2, L0_attn_b_ma_w1, L0_attn_b_ma_w2, L0_attn_b_mk_w1, L0_attn_b_mk_w2, L0_attn_b_time_decay, L0_attn_b_time_faaaa, L0_attn_b_time_aaaaa, L0_attn_b_time_misc_a, L0_attn_b_time_misc_k, L0_attn_b_Wr, L0_attn_b_Wk, L0_attn_b_Wv, L0_attn_b_Wo, L0_attn_b_ln_w, L0_attn_b_ln_b)
    x = x + _L0_ffn_ref(_layernorm(x, axis=-1), L0_ffn_Wqkv, L0_ffn_q_scale, L0_ffn_k_scale, L0_ffn_Wo, L0_ffn_ln_g, L0_ffn_ln_b, L0_ffn_W1, L0_ffn_b1, L0_ffn_W2, L0_ffn_b2)
    return x

_drawn_inputs = setup_inputs


def setup_inputs(seed=0):
    import zlib

    import numpy as np

    out = dict(_drawn_inputs(seed))
    spreads = {'L0_attn_b_ln_w': (1.0, 0.2),
     'L0_attn_b_ln_b': (0.0, 0.1),
     'L0_ffn_q_scale': (1.0, 0.2),
     'L0_ffn_k_scale': (1.0, 0.2),
     'L0_ffn_ln_g': (1.0, 0.2),
     'L0_ffn_ln_b': (0.0, 0.1),
     'L0_ffn_b1': (0.0, 0.1),
     'L0_ffn_b2': (0.0, 0.1)}
    factors = {}
    for name, (base, spread) in spreads.items():
        noise = np.random.default_rng([zlib.crc32(name.encode()), seed]).standard_normal(out[name].shape)
        drawn = base * np.exp(spread * noise) if base else spread * noise
        out[name] = jnp.asarray(drawn.astype(out[name].dtype))
    for name, factor in factors.items():
        out[name] = (out[name] * factor).astype(out[name].dtype)
    return out
```

```python
from contextlib import ExitStack

import numpy as np

import concourse.bass as bass
from concourse import mybir

F32 = mybir.dt.float32
ALU = mybir.AluOpType
ACT = mybir.ActivationFunctionType
AX = mybir.AxisListType

P = 128
DIM = 128
BATCH, SEQ = 4, 512
EPS = 1e-5
LOWEST = -3.0e38
DEPTH, HEADS, HD, WINDOW = 6, 16, 64, 32
INNER = HEADS * HD
PAIRS = HEADS // 2
HID = DIM * 4 * 2 // 3
TILES = DEPTH * BATCH * SEQ // P
N_LOADS = 9
N_CONSTS = 6




def layernorm_rows(eng_wait, dve, stats, meanvar, src, n, stats_sem):
    dve.bn_stats(stats[:, n, :], src).then_inc(stats_sem, 1)
    dve.wait_ge(stats_sem, eng_wait)
    dve.bn_aggr(meanvar[:, n, :], stats[:, n, :]).then_inc(stats_sem, 1)


def retention(nc, shared, ins):
    x, ident = shared["x"], shared["ident"]
    with ExitStack() as ctx:
        def sb(name, shape):
            return ctx.enter_context(nc.sbuf_tensor("ret_" + name, shape, F32))

        def ps(name):
            return ctx.enter_context(nc.psum_tensor("ret_" + name, [P, 512], F32))

        def sem(name):
            return ctx.enter_context(nc.semaphore("ret_" + name))

        w_qkv = sb("w_qkv", [P, 3 * DIM])
        xpos = sb("xpos", [P, 4, 2, 2 * DIM])
        decay = sb("decay", [P, 7 * P])
        mhalf = sb("mhalf", [P, 16])
        stats = sb("stats", [P, 16, 6])
        meanvar = sb("meanvar", [P, 16, 2])
        rstd = sb("rstd", [P, 16])
        x_n = sb("x_n", [P, 4, DIM])
        xn_t = sb("xn_t", [P, 4, P])
        cosined = sb("cosined", [P, 4, 2 * DIM])
        sined = sb("sined", [P, 4, 2 * DIM])
        q_k = sb("q_k", [P, 4, 2 * DIM])
        v = sb("v", [P, 3, 4, DIM])
        q_t = sb("q_t", [P, 2, 4, P])
        k_t = sb("k_t", [P, 2, 4, P])
        row_max = sb("row_max", [P, 4])
        neg_max = sb("neg_max", [P, 4])
        row_sum = sb("row_sum", [P, 4])
        inv_sum = sb("inv_sum", [P, 4])
        e = sb("e", [P, 2, SEQ])
        prob = sb("prob", [P, 2, SEQ])
        p_t = sb("p_t", [P, 2, SEQ])

        bank_x = ps("bank_x")
        bank_qkv = [ps("bank_qkv0"), ps("bank_qkv1")]
        bank_turn = ps("bank_turn")
        bank_s = [ps("bank_s0"), ps("bank_s1")]
        bank_pt = ps("bank_pt")
        bank_o = ps("bank_o")

        loaded = sem("loaded")
        half_set = sem("half_set")
        stats_set = sem("stats_set")
        var_set = sem("var_set")
        rstd_set = sem("rstd_set")
        xn_set = sem("xn_set")
        pe_xn = sem("pe_xn")
        xn_turned = sem("xn_turned")
        pe_qkv = sem("pe_qkv")
        v_set = sem("v_set")
        rotated = sem("rotated")
        qk_set = sem("qk_set")
        pe_qk = sem("pe_qk")
        qk_turned = sem("qk_turned")
        pe_s = sem("pe_s")
        max_set = sem("max_set")
        e_set = sem("e_set")
        inv_set = sem("inv_set")
        prob_set = sem("prob_set")
        pe_pt = sem("pe_pt")
        pt_set = sem("pt_set")
        pe_o = sem("pe_o")
        x_set = sem("x_set")

        block = ctx.enter_context(nc.Block())

        @block.sync
        def _(sp):
            for n, name in enumerate(("W_Q", "W_K", "W_V")):
                sp.dma_start(w_qkv[:, n * DIM:(n + 1) * DIM], ins["L0_attn_a_" + name]).then_inc(loaded, 16)
            sp.dma_start(xpos[:, :, :, :], ins["table_xpos"]).then_inc(loaded, 16)
            sp.dma_start(decay[:, :], ins["table_decay"]).then_inc(loaded, 16)

        @block.tensor
        def _(pe):
            pe.wait_ge(loaded, 16 * 5)

            def project(n):
                T = n % 4
                pe.wait_ge(xn_set, n + 1)
                if n:
                    pe.wait_ge(xn_turned, n)
                pe.transpose(bank_x[:, 0:P], x_n[:, T, :], ident[:, :]).then_inc(pe_xn, 1)
                pe.wait_ge(xn_turned, n + 1)
                if n >= 2:
                    pe.wait_ge(v_set, n - 1)
                pe.matmul(bank_qkv[n % 2][:, 0:3 * DIM], xn_t[:, T, :], w_qkv[:, :],
                          start=True, stop=True).then_inc(pe_qkv, 1)

            def turn(n):
                T = n % 4
                pe.wait_ge(qk_set, n + 1)
                if n:
                    pe.wait_ge(qk_turned, n)
                pe.transpose(bank_turn[:, 0:P], q_k[:, T, 0:P], ident[:, :])
                pe.transpose(bank_turn[:, P:2 * P], q_k[:, T, P:2 * P], ident[:, :]).then_inc(pe_qk, 1)

            def scores(n):
                b, T = n // 4 % 2, n % 4
                pe.wait_ge(qk_turned, n - T + 4)
                if n >= 2:
                    pe.wait_ge(e_set, n - 1)
                pe.matmul(bank_s[n % 2][:, :], q_t[:, b, T, :], k_t[:, b, :, :], start=True, stop=True
                          ).then_inc(pe_s, 1)

            def attend(n):
                pe.wait_ge(prob_set, n + 1)
                if n:
                    pe.wait_ge(pt_set, n)
                for j in range(4):
                    last = pe.transpose(bank_pt[:, j * P:(j + 1) * P], prob[:, n % 2, j * P:(j + 1) * P], ident[:, :])
                last.then_inc(pe_pt, 1)
                pe.wait_ge(pt_set, n + 1)
                if n:
                    pe.wait_ge(x_set, n)
                for j in range(4):
                    last = pe.matmul(bank_o[:, 0:DIM], p_t[:, n % 2, j * P:(j + 1) * P], v[:, n // 4 % 3, j, :],
                                     start=j == 0, stop=j == 3)
                last.then_inc(pe_o, 1)

            for n in range(4 * BATCH + 6):
                if n < 4 * BATCH:
                    project(n)
                if 1 <= n <= 4 * BATCH:
                    turn(n - 1)
                if 4 <= n < 4 * BATCH + 4:
                    scores(n - 4)
                if 5 <= n < 4 * BATCH + 5:
                    attend(n - 5)

        @block.scalar
        def _(act):
            for n in range(4 * BATCH + 6):
                if n < 4 * BATCH:
                    T, b = n % 4, n // 4 % 2
                    act.wait_ge(pe_xn, n + 1)
                    act.copy(xn_t[:, T, :], bank_x[:, 0:P]).then_inc(xn_turned, 1)
                    act.wait_ge(rotated, n + 1)
                    if n >= 12:
                        act.wait_ge(pe_o, n - n % 4 - 8)
                    act.copy(v[:, n // 4 % 3, T, :], bank_qkv[n % 2][:, 2 * DIM:3 * DIM]).then_inc(v_set, 1)
                if 1 <= n <= 4 * BATCH:
                    m = n - 1
                    act.wait_ge(pe_qk, m + 1)
                    act.copy(q_t[:, m // 4 % 2, m % 4, :], bank_turn[:, 0:P])
                    act.copy(k_t[:, m // 4 % 2, m % 4, :], bank_turn[:, P:2 * P]).then_inc(qk_turned, 1)
                if 4 <= n < 4 * BATCH + 4:
                    m = n - 4
                    act.wait_ge(max_set, 2 * m + 2)
                    if m >= 2:
                        act.wait_ge(prob_set, m - 1)
                    act.activation(e[:, m % 2, :], bank_s[m % 2][:, :], ACT.Exp, bias=neg_max[:, m % 4:m % 4 + 1],
                                   accum_out=row_sum[:, m % 4:m % 4 + 1]).then_inc(e_set, 1)
                if 5 <= n < 4 * BATCH + 5:
                    m = n - 5
                    act.wait_ge(pe_pt, m + 1)
                    if m >= 2:
                        act.wait_ge(pe_o, m - 1)
                    act.copy(p_t[:, m % 2, :], bank_pt[:, :]).then_inc(pt_set, 1)

        @block.vector
        def _(dve):
            dve.memset(mhalf[:, :], -0.5).then_inc(half_set, 1)
            for n in range(16):
                layernorm_rows(2 * n + 1, dve, stats, meanvar, x[:, n, :], n, stats_set)
            dve.wait_ge(rstd_set, 1)
            dve.wait_ge(loaded, 16 * 5)
            for n in range(4 * BATCH + 6):
                if n < 4 * BATCH:
                    T = n % 4
                    if n >= 4:
                        dve.wait_ge(pe_xn, n - 3)
                    dve.tensor_scalar(x_n[:, T, :], x[:, n, :], meanvar[:, n, 0:1], rstd[:, n:n + 1],
                                      ALU.subtract, ALU.mult).then_inc(xn_set, 1)
                    dve.wait_ge(pe_qkv, n + 1)
                    if n >= 4:
                        dve.wait_ge(qk_set, n - 3)
                    src = bank_qkv[n % 2][:, 0:2 * DIM]
                    dve.tensor_tensor(cosined[:, T, :], src, xpos[:, T, 0, :], ALU.mult)
                    dve.tensor_tensor(sined[:, T, :].rearrange("p (n f) -> p n f", f=2),
                                      src.rearrange("p (n f) -> p n f", f=2)[:, :, ::-1],
                                      xpos[:, T, 1, :].rearrange("p (n f) -> p n f", f=2),
                                      ALU.mult).then_inc(rotated, 1)
                if 4 <= n < 4 * BATCH + 4:
                    m = n - 4
                    c = m % 4
                    dve.wait_ge(pe_s, m + 1)
                    dve.tensor_reduce(row_max[:, c:c + 1], bank_s[m % 2][:, :], AX.X, ALU.max).then_inc(max_set, 1)
                    dve.wait_ge(max_set, 2 * m + 1)
                    dve.tensor_scalar(neg_max[:, c:c + 1], row_max[:, c:c + 1], -1.0, None, ALU.mult
                                      ).then_inc(max_set, 1)
                    dve.wait_ge(e_set, m + 1)
                    dve.reciprocal(inv_sum[:, c:c + 1], row_sum[:, c:c + 1]).then_inc(inv_set, 1)
                    dve.wait_ge(inv_set, m + 1)
                    if m >= 2:
                        dve.wait_ge(pe_pt, m - 1)
                    d = (3 - m % 4) * P
                    dve.scalar_tensor_tensor(prob[:, m % 2, :], e[:, m % 2, :], inv_sum[:, c:c + 1],
                                             decay[:, d:d + SEQ], ALU.mult, ALU.mult).then_inc(prob_set, 1)
                if 5 <= n < 4 * BATCH + 5:
                    m = n - 5
                    dve.wait_ge(pe_o, m + 1)
                    dve.tensor_tensor(x[:, m, :], bank_o[:, 0:DIM], x[:, m, :], ALU.add).then_inc(x_set, 1)

        @block.gpsimd
        def _(pool):
            pool.wait_ge(stats_set, 32)
            pool.wait_ge(half_set, 1)
            pool.tensor_scalar(rstd[:, :], meanvar[:, :, 1], EPS, 1.0, ALU.add, ALU.mult).then_inc(var_set, 1)
            pool.wait_ge(var_set, 1)
            pool.tensor_tensor(rstd[:, :], rstd[:, :], mhalf[:, :], ALU.pow).then_inc(rstd_set, 1)
            for n in range(4 * BATCH):
                T = n % 4
                pool.wait_ge(rotated, n + 1)
                if n >= 4:
                    pool.wait_ge(pe_qk, n - 3)
                pool.tensor_tensor(q_k[:, T, :], cosined[:, T, :], sined[:, T, :], ALU.add).then_inc(qk_set, 1)
def ffn_stack(nc, shared, w):
    xo, ident, rot, mask = shared["x"], shared["ident"], shared["rot"], shared["mask"]
    with ExitStack() as ctx:
        def sb(name, shape):
            return ctx.enter_context(nc.sbuf_tensor(shared["tag"] + name, shape, F32))

        def ps(name):
            return ctx.enter_context(nc.psum_tensor(shared["tag"] + name, [P, 512], F32))

        def sem(name):
            return ctx.enter_context(nc.semaphore(shared["tag"] + name))

        w_qkv = sb("w_qkv", [P, 2, 3 * INNER])
        w_o = sb("w_o", [P, 2, PAIRS, DIM])
        w_1 = sb("w_1", [P, 2, 2 * HID])
        w_2 = sb("w_2", [P, 2, 3, DIM])
        b_1 = sb("b_1", [P, 2, 2 * HID])
        b_2 = sb("b_2", [P, 2, DIM])
        ln_gb = sb("ln_gb", [P, 2, 2])
        xres = sb("xres", [P, 16, DIM])
        xin = sb("xin", [P, 4, DIM])
        xmid = sb("xmid", [P, 4, DIM])
        xmid_b = sb("xmid_b", [P, 4, DIM])
        xshift = sb("xshift", [P, 4 * P + 1])
        mshift = sb("mshift", [P, 4 * P + 1])
        sq = sb("sq", [P, 2, 512])
        rot_c = sb("rot_c", [P, 2, 512])
        rot_s = sb("rot_s", [P, 2, 512])
        roped = sb("roped", [P, 2, 512])
        ssq = sb("ssq", [P, 4, 4, 8])
        rnorm = sb("rnorm", [P, 4, 4, 8])
        nrn8 = sb("nrn8", [P, 4, HEADS])
        q_t = sb("q_t", [P, 2, PAIRS, P])
        k_z = sb("k_z", [P, 4, PAIRS, 2, P])
        v_n = sb("v_n", [P, 4, INNER])
        s_m = sb("s_m", [P, 4, 2, 160])
        prob = sb("prob", [P, 4, 2, 256])
        smax = sb("smax", [P, 4, HEADS])
        nbias = sb("nbias", [P, 4, HEADS])
        psums = sb("psums", [P, 4, HEADS])
        prec = sb("prec", [P, 4, HEADS])
        p_t = sb("p_t", [P, 2, 320])
        o_t = sb("o_t", [P, 2, PAIRS, P])
        stats = sb("stats", [P, 16, 6])
        meanvar = sb("meanvar", [P, 16, 2])
        rstd = sb("rstd", [P, 16, 1])
        mhalf = sb("mhalf", [P, 16])
        x_n = sb("x_n", [P, 2, DIM])
        xn_t = sb("xn_t", [P, 2, DIM])
        h_gate = sb("h_gate", [P, HID])
        h_act = sb("h_act", [P, HID])
        h_lin = sb("h_lin", [P, HID])
        h = sb("h", [P, HID])
        h_t = sb("h_t", [P, 3, P])

        bank_proj = [ps("bank_proj0"), ps("bank_proj1")]
        bank_turn = ps("bank_turn")
        bank_s = [ps("bank_s0"), ps("bank_s1")]
        bank_pt = ps("bank_pt")
        bank_o = ps("bank_o")
        bank_misc = ps("bank_misc")

        passed = {e.engine: sem(f"passed_{n}") for n, e in enumerate((nc.scalar, nc.vector, nc.gpsimd))}
        weights_in = sem("weights_in")
        consts_set = sem("consts_set")
        x_var = sem("x_var")
        x_stats = sem("x_stats")
        x_rstd = sem("x_rstd")
        x_ready = sem("x_ready")
        xin_set = sem("xin_set")
        pe_x = sem("pe_x")
        x_turned = sem("x_turned")
        proj_done = sem("proj_done")
        rot_read = sem("rot_read")
        sq_done = sem("sq_done")
        ssq_done = sem("ssq_done")
        rope_chain = sem("rope_chain")
        ln_chain = sem("ln_chain")
        roped_set = sem("roped_set")
        rn8_set = sem("rn8_set")
        pe_turn = sem("pe_turn")
        turned = sem("turned")
        v_set = sem("v_set")
        pe_s = sem("pe_s")
        masked = sem("masked")
        nbias_set = sem("nbias_set")
        exp_done = sem("exp_done")
        prec_set = sem("prec_set")
        normed = sem("normed")
        pe_pt = sem("pe_pt")
        pt_set = sem("pt_set")
        pe_pv = sem("pe_pv")
        o_set = sem("o_set")
        pe_wo = sem("pe_wo")
        xmid_set = sem("xmid_set")
        xmid_b_set = sem("xmid_b_set")
        pe_m = sem("pe_m")
        m_turned = sem("m_turned")
        pe_ms = sem("pe_ms")
        ln_stats = sem("ln_stats")
        ln_rstd = sem("ln_rstd")
        xn_set = sem("xn_set")
        pe_xn = sem("pe_xn")
        xn_turned = sem("xn_turned")
        pe_w1 = sem("pe_w1")
        hid_read = sem("hid_read")
        gelu_done = sem("gelu_done")
        h_set = sem("h_set")
        pe_h = sem("pe_h")
        h_turned = sem("h_turned")
        pe_w2 = sem("pe_w2")

        def wait(eng, s, per_tile, tile, c):
            n = tile * per_tile + c
            if isinstance(n, int) and (n <= 0 or tile >= TILES):
                return
            eng.wait_ge(s, n)

        def wait_apart(eng, s, per_tile, tile, c):
            wait(eng, s, per_tile, tile, c)
            if not isinstance(tile, int):
                eng.sem_inc(passed[eng.engine], 1)

        def slots(eng, body):
            def where(i, T):
                def tile(lag):
                    return 4 * i + (T - lag)

                def ahead(lag):
                    return i + (T - lag) // 4
                return tile, ahead

            def static(N):
                tile, ahead = where(N // 4, N % 4)
                body(N, N % 4, lambda lag: (N - lag) // 16 % 2, lambda lag: (N - lag) // 4 % 4,
                     lambda lag: 0 <= N - lag < TILES)

            for N in range(4):
                static(N)
            with eng.Fori(1, TILES // 4) as i:
                for T in range(4):
                    def parity(lag, T=T):
                        return (i + (T - lag) // 4) // 4 % 2

                    def row(lag, T=T):
                        return (i + (T - lag) // 4) % 4
                    body(4 * i + T, T, parity, row, lambda lag: True)
            for N in range(TILES, TILES + 3):
                static(N)

        CHUNKS = {0: 0, 1: 1, 3: 2, 4: 3, 5: 4, 6: 5}
        CHUNK_COLS = [INNER, 0, INNER + 512, 512, 2 * INNER, 2 * INNER + 512]
        TURNS = {3: 0, 4: 1, 6: 2, 7: 3}

        block = ctx.enter_context(nc.Block())

        @block.sync
        def _(sp):
            for layer in range(DEPTH):
                half = layer % 2
                if layer >= 1:
                    sp.wait_ge(weights_in, 16 * N_LOADS * layer)
                if layer >= 2:
                    sp.wait_ge(x_ready, 16 * layer)
                sp.dma_start(w_qkv[:, half, :], w["Wqkv"][layer]).then_inc(weights_in, 16)
                sp.dma_start(w_o[:, half, :, :], w["Wo"][layer].rearrange("(g p) n -> p g n", p=P)
                             ).then_inc(weights_in, 16)
                sp.dma_start(w_1[:, half, :], w["W1"][layer]).then_inc(weights_in, 16)
                sp.dma_start(w_2[:, half, 0:2, :], w["W2"][layer, 0:2 * P, :].rearrange("(g p) n -> p g n", p=P)
                             ).then_inc(weights_in, 16)
                sp.dma_start(w_2[0:HID - 2 * P, half, 2, :], w["W2"][layer, 2 * P:HID, :]).then_inc(weights_in, 16)
                sp.dma_start(b_1[:, half, :], w["b1"][layer].partition_broadcast(P)).then_inc(weights_in, 16)
                sp.dma_start(b_2[:, half, :], w["b2"][layer].partition_broadcast(P)).then_inc(weights_in, 16)
                sp.dma_start(ln_gb[:, half, 0:1], w["ln_g"][layer].unsqueeze(1)).then_inc(weights_in, 16)
                sp.dma_start(ln_gb[:, half, 1:2], w["ln_b"][layer].unsqueeze(1)).then_inc(weights_in, 16)
            sp.wait_ge(weights_in, 16 * N_LOADS * DEPTH)

        @block.tensor
        def _(pe):
            def turn_x(t, T):
                wait(pe, xin_set, 1, t, 1)
                wait(pe, turned, 4, t - 1, 0)
                pe.transpose(bank_turn[:, 0:P], xin[:, T, :], ident[:, :]).then_inc(pe_x, 1)

            def project(t, T, c, half):
                if c == 0:
                    wait(pe, x_turned, 1, t, 1)
                if c in (0, 1):
                    wait(pe, v_set, 2, t - 1, c + 1)
                elif c in (2, 3):
                    wait(pe, hid_read, 2, t - 3, c - 1)
                    wait(pe, sq_done, 4, t, c - 1)
                else:
                    wait(pe, sq_done, 4, t, c - 1)
                pe.matmul(bank_proj[c % 2][:, :], xshift[:, T * P:(T + 1) * P],
                          w_qkv[:, half, CHUNK_COLS[c]:CHUNK_COLS[c] + 512],
                          start=True, stop=True).then_inc(proj_done, 1)

            def turn_chunk(t, c):
                wait(pe, roped_set, 4, t, c + 1)
                if c == 0:
                    wait(pe, x_turned, 1, t, 2)
                elif c == 2:
                    wait(pe, h_turned, 1, t - 3, 1)
                    wait(pe, turned, 4, t, c)
                else:
                    wait(pe, turned, 4, t, c)
                for g in range(4):
                    last = pe.transpose(bank_turn[:, g * P:(g + 1) * P], roped[:, c % 2, g * P:(g + 1) * P],
                                        ident[:, :])
                last.then_inc(pe_turn, 1)

            def scores(t, T, hp):
                wait(pe, turned, 4, t, 2 if hp < 4 else 4)
                wait(pe, masked, 8, t, hp - 1)
                out = bank_s[hp % 2][:, 0:320].rearrange("p (h c) -> p h c", h=2)
                last = pe.matmul(out[:, :, 32:160], q_t[:, T % 2, hp, :], k_z[:, T, hp, :, :], start=True, stop=True)
                if T > 0:
                    last = pe.matmul(out[:, :, 0:32], q_t[:, T % 2, hp, :], k_z[:, T - 1, hp, :, 96:128],
                                     start=True, stop=True)
                last.then_inc(pe_s, 1)

            def turn_probs(t, T, hp):
                wait(pe, normed, 8, t, hp + 1)
                wait(pe, pt_set, 8, t, hp)
                for j in range(2):
                    last = pe.transpose(bank_pt[:, 160 * j:160 * j + P], prob[:, hp % 4, j, P:2 * P], ident[:, :])
                    if T > 0:
                        last = pe.transpose(bank_pt[:, 160 * j + P:160 * j + 160], prob[0:32, hp % 4, j, 0:P],
                                            ident[0:32, 0:32])
                last.then_inc(pe_pt, 1)

            def weigh_values(t, T, hp):
                wait(pe, pt_set, 8, t, hp + 1)
                if hp == 0:
                    wait(pe, v_set, 2, t, 2)
                if hp % 4 == 0:
                    wait(pe, o_set, 2, t, hp // 4)
                for j in range(2):
                    head = 2 * hp + j
                    out = bank_o[64 * j:64 * j + 64, (hp % 4) * P:(hp % 4 + 1) * P]
                    last = pe.matmul(out, v_n[:, T, 64 * head:64 * head + 64], p_t[:, hp % 2, 160 * j:160 * j + P],
                                     start=True, stop=True)
                    if T > 0:
                        last = pe.matmul(out[:, 0:32], v_n[:, T - 1, 64 * head:64 * head + 64],
                                         p_t[:, hp % 2, 160 * j + P:160 * j + 160], start=False, stop=True,
                                         skip_group_check=True)
                last.then_inc(pe_pv, 1)

            def project_out(t, T, half):
                wait(pe, o_set, 2, t, 2)
                wait(pe, xn_turned, 1, t - 1, 1)
                for g in range(PAIRS):
                    last = pe.matmul(bank_misc[:, 0:DIM], o_t[:, T % 2, g, :], w_o[:, half, g, :],
                                     start=g == 0, stop=g == PAIRS - 1)
                last.then_inc(pe_wo, 1)

            def turn_mid(t, T):
                wait(pe, xmid_set, 1, t, 1)
                pe.transpose(bank_misc[:, 0:P], xmid[:, T, :], ident[:, :]).then_inc(pe_m, 1)

            def turn_mid_back(t, T):
                wait(pe, m_turned, 1, t, 1)
                wait(pe, x_ready, 1, t - 1, 17)
                pe.transpose(bank_misc[:, 0:P], mshift[:, T * P:(T + 1) * P], ident[:, :]).then_inc(pe_ms, 1)

            def turn_xn(t, T):
                wait(pe, xn_set, 1, t, 1)
                pe.transpose(bank_misc[:, 0:P], x_n[:, T % 2, :], ident[:, :]).then_inc(pe_xn, 1)

            def mlp_up(t, T, half):
                wait(pe, xn_turned, 1, t, 1)
                for c in range(2):
                    wait(pe, sq_done, 4, t + 3, c + 1)
                    if isinstance(t, int) and t + 3 >= TILES:
                        wait(pe, v_set, 2, TILES - 1, 2)
                        wait(pe, hid_read, 2, t - 1, c + 1)
                    col = HID * (1 - c)
                    pe.matmul(bank_proj[c][:, 0:HID], xn_t[:, T % 2, :], w_1[:, half, col:col + HID],
                              start=True, stop=True).then_inc(pe_w1, 1)

            def turn_h(t):
                wait(pe, h_set, 1, t, 1)
                wait(pe, turned, 4, t + 3, 2)
                if isinstance(t, int) and t + 3 >= TILES:
                    wait(pe, turned, 4, TILES - 1, 4)
                    wait(pe, x_turned, 1, TILES - 1, 2)
                    wait(pe, h_turned, 1, t - 1, 1)
                for g in range(3):
                    n = min(P, HID - g * P)
                    last = pe.transpose(bank_turn[0:n, g * P:(g + 1) * P], h[:, g * P:g * P + n], ident[:, :])
                last.then_inc(pe_h, 1)

            def mlp_down(t, half):
                wait(pe, h_turned, 1, t, 1)
                wait(pe, m_turned, 1, t + 1, 1)
                for g in range(3):
                    n = min(P, HID - g * P)
                    last = pe.matmul(bank_misc[:, 0:DIM], h_t[0:n, g, :], w_2[0:n, half, g, :],
                                     start=g == 0, stop=g == 2)
                last.then_inc(pe_w2, 1)

            def slot(N, T, parity, row, runs):
                for s in range(8):
                    if runs(1):
                        scores(N - 1, (T - 1) % 4, s)
                    if runs(0) and s in CHUNKS:
                        if s == 0 and T == 0:
                            pe.wait_ge(weights_in, (N // 16 + 1) * (16 * N_LOADS))
                        project(N, T, CHUNKS[s], parity(0))
                    if s == 1 and runs(3):
                        turn_xn(N - 3, (T - 3) % 4)
                    if s == 2 and runs(-1):
                        turn_x(N + 1, (T + 1) % 4)
                    pt_tile = 2 if s < 2 else 1
                    if runs(pt_tile):
                        turn_probs(N - pt_tile, (T - pt_tile) % 4, (s - 2) % 8)
                    if s == 2 and runs(3):
                        mlp_up(N - 3, (T - 3) % 4, parity(3))
                    pv_tile = 2 if s < 3 else 1
                    if runs(pv_tile):
                        weigh_values(N - pv_tile, (T - pv_tile) % 4, (s - 3) % 8)
                    if s == 4 and runs(2):
                        project_out(N - 2, (T - 2) % 4, parity(2))
                    if s in TURNS and runs(0):
                        turn_chunk(N, TURNS[s])
                    if s == 5 and runs(3):
                        turn_h(N - 3)
                    if s == 5 and runs(2):
                        turn_mid(N - 2, (T - 2) % 4)
                    if s == 6 and runs(3):
                        mlp_down(N - 3, parity(3))
                    if s == 7 and runs(2):
                        turn_mid_back(N - 2, (T - 2) % 4)

            pe.wait_ge(consts_set, N_CONSTS)
            turn_x(0, 0)
            slots(pe, slot)

        @block.scalar
        def _(act):
            def x_out(t, T):
                wait(act, pe_x, 1, t, 1)
                wait(act, proj_done, 6, t - 3, 6)
                act.copy(xshift[0:64, T * P:(T + 1) * P], bank_turn[0:64, 0:P])
                act.copy(xshift[64:P, T * P + 1:(T + 1) * P + 1], bank_turn[64:P, 0:P]).then_inc(x_turned, 1)

            def square(t, c):
                wait(act, rot_read, 4, t, c + 1)
                wait(act, ssq_done, 4, t, c - 1)
                act.activation(sq[:, c % 2, :], bank_proj[c % 2][:, :], ACT.Square).then_inc(sq_done, 1)

            def turned_out(t, T, c):
                wait(act, pe_turn, 4, t, c + 1)
                g = 4 * (c // 2)
                src = bank_turn[:, :].rearrange("p (g n) -> p g n", g=4)
                if c % 2 == 0:
                    wait(act, pe_s, 8, t - 3, 8)
                    act.copy(k_z[0:64, T, g:g + 4, 0, :], src[0:64])
                    act.copy(k_z[64:P, T, g:g + 4, 1, :], src[64:P]).then_inc(turned, 1)
                else:
                    wait(act, pe_s, 8, t - 2, 8)
                    act.copy(q_t[:, T % 2, g:g + 4, :], src).then_inc(turned, 1)

            def values_out(t, T, c):
                wait(act, proj_done, 6, t, 5 + c)
                wait(act, pe_pv, 8, t - 3, 8)
                act.copy(v_n[:, T, 512 * c:512 * c + 512], bank_proj[c][:, :]).then_inc(v_set, 1)

            def exponent(t, T, hp):
                wait(act, nbias_set, 8, t, hp + 1)
                wait(act, pe_pt, 8, t, hp - 3)
                lo = 0 if T > 0 else 32
                for j in range(2):
                    head = 2 * hp + j
                    last = act.activation(prob[:, hp % 4, j, 96 + lo:256], s_m[:, hp % 4, j, lo:160], ACT.Exp,
                                          bias=nbias[:, T, head:head + 1],
                                          scale=rnorm[:, T, 1 + 2 * (hp // 4), head % 8:head % 8 + 1],
                                          accum_out=psums[:, T, head:head + 1])
                last.then_inc(exp_done, 1)

            def probs_out(t, T, hp):
                wait(act, pe_pt, 8, t, hp + 1)
                wait(act, pe_pv, 8, t, hp - 1)
                if T > 0:
                    act.copy(p_t[:, hp % 2, :], bank_pt[:, 0:320]).then_inc(pt_set, 1)
                else:
                    act.copy(p_t[:, hp % 2, :].rearrange("p (h c) -> p h c", h=2)[:, :, 0:P],
                             bank_pt[:, 0:320].rearrange("p (h c) -> p h c", h=2)[:, :, 0:P]).then_inc(pt_set, 1)

            def heads_out(t, T, c):
                wait(act, pe_pv, 8, t, 4 * c + 4)
                wait(act, pe_wo, 1, t - 2, 1)
                act.copy(o_t[:, T % 2, 4 * c:4 * c + 4, :],
                         bank_o[:, :].rearrange("p (g n) -> p g n", g=4)).then_inc(o_set, 1)

            def mid_out(t, T):
                wait(act, pe_m, 1, t, 1)
                act.copy(mshift[0:64, T * P:(T + 1) * P], bank_misc[0:64, 0:P])
                act.copy(mshift[64:P, T * P + 1:(T + 1) * P + 1], bank_misc[64:P, 0:P]).then_inc(m_turned, 1)

            def xn_out(t, T, half):
                wait_apart(act, pe_xn, 1, t, 1)
                act.activation(xn_t[:, T % 2, :], bank_misc[:, 0:P], ACT.Identity,
                               bias=ln_gb[:, half, 1:2], scale=ln_gb[:, half, 0:1]).then_inc(xn_turned, 1)

            def gelu(t):
                wait(act, hid_read, 2, t, 1)
                act.activation(h_act[:, :], h_gate[:, :], ACT.Gelu).then_inc(gelu_done, 1)

            def h_out(t):
                wait(act, pe_h, 1, t, 1)
                act.copy(h_t[:, 0:2, :], bank_turn[:, 0:2 * P].rearrange("p (g n) -> p g n", g=2))
                act.copy(h_t[0:HID - 2 * P, 2, :], bank_turn[0:HID - 2 * P, 2 * P:3 * P]).then_inc(h_turned, 1)

            def slot(N, T, parity, row, runs):
                for s in range(8):
                    pt_tile = 2 if s < 2 else 1
                    if s == 0 and runs(1):
                        turned_out(N - 1, (T - 1) % 4, 3)
                    if s == 2 and runs(3):
                        xn_out(N - 3, (T - 3) % 4, parity(3))
                    if s == 3 and runs(2):
                        heads_out(N - 2, (T - 2) % 4, 1)
                    if s == 7 and runs(1):
                        heads_out(N - 1, (T - 1) % 4, 0)
                    if runs(pt_tile):
                        probs_out(N - pt_tile, (T - pt_tile) % 4, (s - 2) % 8)
                    if runs(1):
                        exponent(N - 1, (T - 1) % 4, s)
                    if s in (1, 2, 4, 5) and runs(0):
                        square(N, {1: 0, 2: 1, 4: 2, 5: 3}[s])
                    if s == 3 and runs(-1):
                        x_out(N + 1, (T + 1) % 4)
                    if s in (4, 5, 7) and runs(0):
                        turned_out(N, T, {4: 0, 5: 1, 7: 2}[s])
                    if s == 3 and runs(3):
                        gelu(N - 3)
                    if s == 6 and runs(2):
                        mid_out(N - 2, (T - 2) % 4)
                    if s == 6 and runs(3):
                        h_out(N - 3)
                    if s in (6, 7) and runs(0):
                        values_out(N, T, s - 6)

            act.wait_ge(consts_set, N_CONSTS)
            x_out(0, 0)
            slots(act, slot)

        @block.vector
        def _(dve):
            def rotate(t, T, c, table):
                wait(dve, proj_done, 6, t, c + 1)
                wait(dve, roped_set, 4, t, c - 1)
                kind = 0 if c % 2 else 2
                src = bank_proj[c % 2][:, :]
                cosine = table[:, kind, :].unsqueeze(1).broadcast_to([P, 8, HD])
                sine = table[:, kind + 1, :].rearrange("p (f d) -> p f d", f=2).unsqueeze(1).broadcast_to([P, 8, 2, HD // 2])
                dve.tensor_tensor(rot_c[:, c % 2, :].rearrange("p (h d) -> p h d", h=8),
                                  src.rearrange("p (h d) -> p h d", h=8), cosine, ALU.mult)
                dve.tensor_tensor(rot_s[:, c % 2, :].rearrange("p (h f d) -> p h f d", h=8, f=2),
                                  src.rearrange("p (h f d) -> p h f d", h=8, f=2)[:, :, ::-1, :], sine,
                                  ALU.mult).then_inc(rot_read, 1)

            def sum_squares(t, T, c):
                wait(dve, sq_done, 4, t, c + 1)
                dve.tensor_reduce(ssq[:, T, c, :], sq[:, c % 2, :].rearrange("p (h d) -> p h d", h=8),
                                  AX.X, ALU.add).then_inc(ssq_done, 1)

            def mask_max(t, T, hp):
                wait(dve, pe_s, 8, t, hp + 1)
                wait_apart(dve, exp_done, 8, t, hp - 3)
                lo = 0 if T > 0 else 32
                for j in range(2):
                    head = 2 * hp + j
                    last = dve.tensor_tensor_reduce(s_m[:, hp % 4, j, lo:160],
                                                    bank_s[hp % 2][:, 160 * j + lo:160 * j + 160], mask[:, lo:160],
                                                    1.0, LOWEST, ALU.add, ALU.max, smax[:, T, head:head + 1])
                last.then_inc(masked, 1)

            def reciprocal(t, T, hp):
                wait(dve, exp_done, 8, t, hp + 1)
                dve.reciprocal(prec[:, T, 2 * hp:2 * hp + 2], psums[:, T, 2 * hp:2 * hp + 2]).then_inc(prec_set, 1)

            def normalise(t, T, hp):
                wait(dve, prec_set, 8, t, hp + 1)
                lo = 96 if T > 0 else 128
                for j in range(2):
                    head = 2 * hp + j
                    p = prob[:, hp % 4, j, lo:256]
                    last = dve.tensor_scalar(p, p, prec[:, T, head:head + 1], None, ALU.mult)
                last.then_inc(normed, 1)

            def mid(t, T):
                wait(dve, pe_wo, 1, t, 1)
                dve.tensor_tensor(xmid[:, T, :], bank_misc[:, 0:DIM], xin[:, T, :], ALU.add).then_inc(xmid_set, 1)

            def mid_stats(t, T):
                wait(dve, pe_ms, 1, t, 1)
                dve.bn_stats(stats[:, T, :], bank_misc[:, 0:P]).then_inc(ln_stats, 1)
                wait_apart(dve, ln_stats, 2, t, 1)
                dve.bn_aggr(meanvar[:, T, :], stats[:, T, :]).then_inc(ln_stats, 1)

            def mid_norm(t, T):
                wait(dve, ln_rstd, 1, t, 1)
                dve.tensor_scalar(x_n[:, T % 2, :], bank_misc[:, 0:P], meanvar[:, T, 0:1], rstd[:, T, :],
                                  ALU.subtract, ALU.mult).then_inc(xn_set, 1)

            def hidden(t, half):
                for c, (out, col) in enumerate(((h_gate, HID), (h_lin, 0))):
                    wait(dve, pe_w1, 2, t, c + 1)
                    dve.tensor_tensor(out[:, :], bank_proj[c][:, 0:HID], b_1[:, half, col:col + HID],
                                      ALU.add).then_inc(hid_read, 1)

            def finish(t, T, r):
                wait(dve, pe_w2, 1, t, 1)
                wait(dve, xmid_b_set, 1, t, 1)
                dve.tensor_tensor(xres[:, r * 4 + T, :], bank_misc[:, 0:DIM], xmid_b[:, T, :],
                                  ALU.add).then_inc(x_ready, 1)

            def slot(N, T, parity, row, runs):
                for s in range(8):
                    late = 2 if s == 0 else 1
                    if s == 0 and runs(3):
                        mid_stats(N - 3, (T - 3) % 4)
                    if runs(late):
                        reciprocal(N - late, (T - late) % 4, (s - 1) % 8)
                    if runs(1):
                        mask_max(N - 1, (T - 1) % 4, s)
                    if runs(late):
                        normalise(N - late, (T - late) % 4, (s - 1) % 8)
                    if s == 1 and runs(3):
                        mid_norm(N - 3, (T - 3) % 4)
                    if s in (0, 1, 3, 4) and runs(0):
                        rotate(N, T, {0: 0, 1: 1, 3: 2, 4: 3}[s], rot[:, N // 16, T, :, :])
                    if s in (1, 2, 4, 5) and runs(0):
                        sum_squares(N, T, {1: 0, 2: 1, 4: 2, 5: 3}[s])
                    if s == 2 and runs(3):
                        hidden(N - 3, parity(3))
                    if s == 4 and runs(2):
                        mid(N - 2, (T - 2) % 4)
                    if s == 6 and runs(3):
                        finish(N - 3, (T - 3) % 4, row(3))

            dve.memset(mhalf[:, :], -0.5).then_inc(consts_set, 1)
            dve.memset(k_z[0:64, :, :, 1, :], 0.0).then_inc(consts_set, 1)
            dve.memset(k_z[64:P, :, :, 0, :], 0.0).then_inc(consts_set, 1)
            dve.memset(prob[0:32, :, :, 0:96], 0.0).then_inc(consts_set, 1)
            dve.memset(xshift[64:P, 0:1], 0.0).then_inc(consts_set, 1)
            dve.memset(mshift[64:P, 0:1], 0.0).then_inc(consts_set, 1)
            for n in range(16):
                dve.bn_stats(stats[:, n, :], xo[:, n, :]).then_inc(x_stats, 1)
            dve.wait_ge(x_stats, 16)
            for n in range(16):
                dve.bn_aggr(meanvar[:, n, :], stats[:, n, :]).then_inc(x_stats, 1)
            dve.wait_ge(x_rstd, 1)
            for n in range(16):
                dve.tensor_scalar(xres[:, n, :], xo[:, n, :], meanvar[:, n, 0:1], rstd[:, n, :],
                                  ALU.subtract, ALU.mult).then_inc(x_ready, 1)
            slots(dve, slot)
            dve.wait_ge(x_ready, 16 + TILES)
            dve.tensor_tensor(xo[:, :, :], xo[:, :, :], xres[:, :, :], ALU.add)

        @block.gpsimd
        def _(pool):
            def link(t, c, ins):
                ins.then_inc(rope_chain, 1)
                wait_apart(pool, rope_chain, 10, t, c)

            def copy_in(t, T, r):
                wait_apart(pool, x_ready, 1, t, 1)
                pool.tensor_copy(xin[:, T, :], xres[:, r * 4 + T, :]).then_inc(xin_set, 1)

            def rope(t, T, c):
                wait(pool, rot_read, 4, t, c + 1)
                wait(pool, pe_turn, 4, t, c - 1)
                ins = pool.tensor_tensor(roped[:, c % 2, :], rot_c[:, c % 2, :], rot_s[:, c % 2, :], ALU.add)
                if c % 2:
                    ins.then_inc(roped_set, 1)
                else:
                    link(t, 1 if c == 0 else 6, ins)

            def norms(t, T, c):
                wait_apart(pool, ssq_done, 4, t, c + 1)
                n = (2, 4, 7, 9)[c]
                link(t, n, pool.tensor_scalar(ssq[:, T, c, :], ssq[:, T, c, :], 1e-24, 1.0 / 64 if c % 2 else 1.0,
                                              ALU.max, ALU.mult))
                ins = pool.tensor_tensor(rnorm[:, T, c, :], ssq[:, T, c, :], mhalf[:, 0:8], ALU.pow)
                link(t, n + 1, ins)
                if c % 2:
                    head = 8 * (c // 2)
                    pool.tensor_scalar(nrn8[:, T, head:head + 8], rnorm[:, T, c, :], -1.0, 1.0,
                                       ALU.mult, ALU.mult).then_inc(rn8_set, 1)
                else:
                    k = roped[:, c % 2, :].rearrange("p (h d) -> p h d", h=8)
                    pool.tensor_tensor(k, k, rnorm[:, T, c, :].unsqueeze(2).broadcast_to([P, 8, HD]),
                                       ALU.mult).then_inc(roped_set, 1)

            def biases(t, T, hp):
                wait(pool, masked, 8, t, hp + 1)
                wait(pool, rn8_set, 2, t, 1 + hp // 4)
                pool.tensor_tensor(nbias[:, T, 2 * hp:2 * hp + 2], smax[:, T, 2 * hp:2 * hp + 2],
                                   nrn8[:, T, 2 * hp:2 * hp + 2], ALU.mult).then_inc(nbias_set, 1)

            def mid_rstd(t, T):
                wait_apart(pool, ln_stats, 2, t, 2)
                pool.tensor_scalar(rstd[:, T, :], meanvar[:, T, 1:2], EPS, 1.0, ALU.add, ALU.mult).then_inc(ln_chain, 1)
                wait(pool, ln_chain, 1, t, 1)
                pool.tensor_tensor(rstd[:, T, :], rstd[:, T, :], mhalf[:, 0:1], ALU.pow).then_inc(ln_rstd, 1)

            def mid_bias(t, T, half):
                wait_apart(pool, xmid_set, 1, t, 1)
                pool.tensor_tensor(xmid_b[:, T, :], xmid[:, T, :], b_2[:, half, :], ALU.add).then_inc(xmid_b_set, 1)

            def gate(t):
                wait(pool, gelu_done, 1, t, 1)
                wait(pool, hid_read, 2, t, 2)
                pool.tensor_tensor(h[:, :], h_act[:, :], h_lin[:, :], ALU.mult).then_inc(h_set, 1)

            def slot(N, T, parity, row, runs):
                for s in range(8):
                    if s == 0 and runs(3):
                        mid_rstd(N - 3, (T - 3) % 4)
                    if runs(1):
                        biases(N - 1, (T - 1) % 4, s)
                    if s == 1 and runs(-1):
                        copy_in(N + 1, (T + 1) % 4, row(-1))
                    if s in (2, 3, 5, 6) and runs(0):
                        norms(N, T, {2: 0, 3: 1, 5: 2, 6: 3}[s])
                    if s in (1, 2, 4, 5) and runs(0):
                        rope(N, T, {1: 0, 2: 1, 4: 2, 5: 3}[s])
                    if s == 4 and runs(3):
                        gate(N - 3)
                    if s == 6 and runs(2):
                        mid_bias(N - 2, (T - 2) % 4, parity(2))

            pool.wait_ge(consts_set, N_CONSTS)
            pool.wait_ge(x_stats, 32)
            pool.tensor_scalar(rstd[:, :, 0], meanvar[:, :, 1], EPS, 1.0, ALU.add, ALU.mult).then_inc(x_var, 1)
            pool.wait_ge(x_var, 1)
            pool.tensor_tensor(rstd[:, :, 0], rstd[:, :, 0], mhalf[:, :], ALU.pow).then_inc(x_rstd, 1)
            copy_in(0, 0, 0)
            slots(pool, slot)

MATS = ("maa1", "maa2", "r", "k", "v", "o", "gate1", "gate2", "wa1", "wa2", "k1", "k2", "ones", "mean")
VECS = ("maa_x", "maa0", "maa1", "maa2", "maa3", "decay", "faaaa", "aaaaa", "misc_a", "misc_k", "ln_w", "ln_b")
HS = 8
EPS_HEAD = 0.00064
CHUNK = 128
GROUP = 8


def mixer(nc, shared, ins):
    with ExitStack() as ctx:
        def sb(name, shape):
            return ctx.enter_context(nc.sbuf_tensor("mix_" + name, shape, F32))

        mats = sb("mats", [P, len(MATS), P])
        vecs = sb("vecs", [P, len(VECS)])
        kept = {n: sb("kept_" + n, [P, BATCH, SEQ]) for n in ("r", "wt", "k", "v", "kk", "b", "g", "y")}
        mat = {n: mats[:, i, :] for i, n in enumerate(MATS)}
        vec = {n: vecs[:, i:i + 1] for i, n in enumerate(VECS)}
        mixer_inputs(nc, shared, ins, mats, vecs, mat, vec, kept)
        mixer_scan(nc, ins, kept)
        mixer_output(nc, shared, mat, vec, kept)


def chain_steps(ctx, nc, prefix, steps):
    where = {name: (nc_sem, i, len(names)) for nc_sem, names in (
        (ctx.enter_context(nc.semaphore(f"{prefix}_{engine}_steps")), names) for engine, names in steps.items())
        for i, name in enumerate(names)}

    def done(instruction, name):
        instruction.then_inc(where[name][0], 1)

    def need(engine, b, *names):
        for name in names:
            semaphore, i, each = where[name]
            engine.wait_ge(semaphore, b * each + (i + 1))

    return done, need


IN_STEPS = {
    "pe": ("pe_x", "pe_lo", "pe_log", "pe_r", "pe_gate1", "pe_wa1", "pe_k1", "pe_k", "pe_v", "pe_g", "pe_decay", "pe_a",
           "pe_ma", "pe_kkk", "pe_mk", "pe_ss"),
    "act": ("xc", "lo_t", "gate_t", "low_wa", "low_k", "r_out", "v_out", "g_out", "a", "ma", "mk", "ksq", "e", "ln1",
            "exp_w", "wt", "exp_wmk", "sqrt_ss"),
    "dve": ("x_n", "xx", "mix", "xm_part", "xm", "k0", "z", "nabs", "kk0", "z_min", "w", "w_mk", "a_rest", "k_factor",
            "k_part", "k_out", "ss", "inv_norm", "kk", "kkb_out"),
}
OUT_STEPS = {
    "pe": ("pe_mean", "pe_rk", "pe_var", "pe_out"),
    "act": ("ysq", "std"),
    "dve": ("rk", "yc", "bonus", "var", "inv_std", "normed", "scaled", "summed", "gated"),
}


def mixer_inputs(nc, shared, ins, mats, vecs, mat, vec, kept):
    x, ident = shared["x"], shared["ident"]
    with ExitStack() as ctx:
        def sb(name, shape):
            return ctx.enter_context(nc.sbuf_tensor("mixin_" + name, shape, F32))

        sems = {}

        def sem(name):
            if name not in sems:
                sems[name] = ctx.enter_context(nc.semaphore("mixin_" + name))
            return sems[name]

        mhalf = sb("mhalf", [P, 16])
        stats = sb("stats", [P, 16, 6])
        meanvar = sb("meanvar", [P, 16, 2])
        rstd = sb("rstd", [P, 16])
        x_n = sb("x_n", [P, 4, DIM])
        xc = sb("xc", [P, SEQ + 1])
        xx, mix, lo_t = (sb(n, [P, SEQ]) for n in ("xx", "mix", "lo_t"))
        xm = sb("xm", [P, 4, SEQ])
        gate_t, low_wa, low_k, k0, z, e, w, a, ma, mk = (
            sb(n, [P, SEQ]) for n in ("gate_t", "low_wa", "low_k", "k0", "z", "e", "w", "a", "ma", "mk"))
        nabs, ln1, kk0, ksq, knorm = (sb(n, [P, SEQ]) for n in ("nabs", "ln1", "kk0", "ksq", "knorm"))
        banks = [ctx.enter_context(nc.psum_tensor(f"mixin_bank{n}", [P, 512], F32)) for n in range(8)]

        done, need = chain_steps(ctx, nc, "mixin", IN_STEPS)
        row_free = sem("row_free")

        block = ctx.enter_context(nc.Block())

        @block.sync
        def _(sp):
            sp.dma_start(mats[:, :, :], ins["table_mix"]).then_inc(sem("loaded"), 16)
            sp.dma_start(vecs[:, :], ins["table_vec"]).then_inc(sem("loaded"), 16)

        @block.tensor
        def _(pe):
            pe.wait_ge(sem("loaded"), 32)
            with pe.Fori(0, BATCH) as b:
                pe.wait_ge(row_free, b + 1)
                need(pe, b, "x_n")
                for T in range(4):
                    last = pe.transpose(banks[0][:, T * P:(T + 1) * P], x_n[:, T, :], ident[:, :])
                done(last, "pe_x")

                def product(bank, m, rhs, name, rows=slice(0, P), *names):
                    need(pe, b, *names)
                    done(pe.matmul(banks[bank][:, :], mat[m][rows, :], rhs, start=True, stop=True), name)

                product(1, "maa1", mix[:, :], "pe_lo", slice(0, P), "mix")
                need(pe, b, "lo_t")
                for g in range(4):
                    rows = slice(32 * g, 32 * g + 32)
                    last = pe.matmul(banks[2 + g][:, :], mat["maa2"][rows, :], lo_t[rows, :], start=True, stop=True)
                done(last, "pe_log")
                everything = slice(0, P)
                product(0, "r", xm[:, 0, :], "pe_r", everything, "xm")
                product(1, "gate1", xm[:, 0, :], "pe_gate1")
                product(2, "wa1", xm[:, 1, :], "pe_wa1")
                product(3, "k1", xm[:, 2, :], "pe_k1")
                product(6, "k", xm[:, 2, :], "pe_k")
                product(7, "v", xm[:, 3, :], "pe_v")
                product(4, "gate2", gate_t[:, :], "pe_g", everything, "gate_t")
                product(5, "wa2", low_wa[0:64, :], "pe_decay", slice(0, 64), "low_wa")
                product(0, "wa2", low_wa[64:96, :], "pe_a", slice(64, 96), "r_out")
                product(1, "wa2", low_wa[96:128, :], "pe_ma", slice(96, 128))
                product(3, "k2", low_k[0:32, :], "pe_kkk", slice(0, 32), "low_k")
                product(2, "k2", low_k[32:64, :], "pe_mk", slice(32, 64))
                product(7, "ones", ksq[:, :], "pe_ss", everything, "ksq", "v_out")

        @block.scalar
        def _(act):
            with act.Fori(0, BATCH) as b:
                act.wait_ge(row_free, b + 1)
                need(act, b, "pe_x")
                done(act.copy(xc[:, 1:SEQ + 1], banks[0][:, :]), "xc")
                need(act, b, "pe_lo")
                done(act.activation(lo_t[:, :], banks[1][:, :], ACT.Tanh), "lo_t")
                need(act, b, "pe_gate1")
                done(act.activation(gate_t[:, :], banks[1][:, :], ACT.Tanh), "gate_t")
                need(act, b, "pe_wa1")
                act.activation(low_wa[0:64, :], banks[2][0:64, :], ACT.Tanh)
                done(act.copy(low_wa[64:P, :], banks[2][64:P, :]), "low_wa")
                need(act, b, "pe_k1")
                act.activation(low_k[0:32, :], banks[3][0:32, :], ACT.Tanh)
                done(act.copy(low_k[32:64, :], banks[3][32:64, :]), "low_k")
                need(act, b, "pe_r")
                done(act.copy(kept["r"][:, b, :], banks[0][:, :]), "r_out")
                need(act, b, "pe_v")
                done(act.copy(kept["v"][:, b, :], banks[7][:, :]), "v_out")
                need(act, b, "pe_g")
                done(act.copy(kept["g"][:, b, :], banks[4][:, :]), "g_out")
                for bank, out, v, name in ((0, a, "aaaaa", "a"), (1, ma, "misc_a", "ma"), (2, mk, "misc_k", "mk")):
                    need(act, b, "pe_" + name)
                    done(act.activation(out[:, :], banks[bank][:, :], ACT.Sigmoid, bias=vec[v]), name)
                need(act, b, "kk0")
                done(act.activation(ksq[:, :], kk0[:, :], ACT.Square), "ksq")
                need(act, b, "nabs")
                done(act.activation(e[:, :], nabs[:, :], ACT.Exp), "e")
                need(act, b, "e")
                done(act.activation(ln1[:, :], e[:, :], ACT.Ln, bias=1.0), "ln1")
                need(act, b, "w")
                done(act.activation(e[:, :], w[:, :], ACT.Exp), "exp_w")
                need(act, b, "exp_w")
                done(act.activation(kept["wt"][:, b, :], e[:, :], ACT.Exp, scale=-1.0), "wt")
                need(act, b, "w_mk")
                done(act.activation(mk[:, :], mk[:, :], ACT.Exp), "exp_wmk")
                need(act, b, "ss")
                done(act.activation(knorm[:, :], knorm[:, :], ACT.Sqrt), "sqrt_ss")

        @block.vector
        def _(dve):
            dve.memset(mhalf[:, :], -0.5).then_inc(sem("half"), 1)
            dve.memset(xc[:, 0:1], 0.0).then_inc(sem("half"), 1)
            for n in range(16):
                layernorm_rows(2 * n + 1, dve, stats, meanvar, x[:, n, :], n, sem("stats"))
            dve.wait_ge(sem("rstd"), 1)
            dve.wait_ge(sem("loaded"), 32)
            dve.memset(xx[:, 0:1], 0.0).then_inc(row_free, 1)
            dve.wait_ge(row_free, 1)
            with dve.Fori(0, BATCH) as b:
                def psum(bank):
                    return banks[bank][:, :]

                dve.wait_ge(row_free, b + 1)
                for T in range(4):
                    n = b * 4 + T
                    last = dve.tensor_scalar(x_n[:, T, :], x[:, n, :], meanvar[:, n, 0:1], rstd[:, bass.ds(n, 1)],
                                             ALU.subtract, ALU.mult)
                done(last, "x_n")
                need(dve, b, "xc")
                xt = xc[:, 1:SEQ + 1]
                done(dve.tensor_tensor(xx[:, :], xc[:, 0:SEQ], xt, ALU.subtract), "xx")
                need(dve, b, "xx")
                done(dve.scalar_tensor_tensor(mix[:, :], xx[:, :], vec["maa_x"], xt, ALU.mult, ALU.add), "mix")
                need(dve, b, "pe_log")
                for g in range(4):
                    last = dve.scalar_tensor_tensor(xm[:, g, :], psum(2 + g), vec[f"maa{g}"], xx[:, :],
                                                    ALU.add, ALU.mult)
                done(last, "xm_part")
                need(dve, b, "xm_part")
                done(dve.tensor_tensor(xm[:, :, :], xm[:, :, :], xt.unsqueeze(1).broadcast_to([P, 4, SEQ]), ALU.add),
                     "xm")
                need(dve, b, "pe_k")
                done(dve.tensor_copy(k0[:, :], psum(6)), "k0")
                need(dve, b, "pe_decay")
                done(dve.tensor_scalar(z[:, :], psum(5), vec["decay"], None, ALU.add), "z")
                need(dve, b, "z")
                done(dve.scalar_tensor_tensor(nabs[:, :], z[:, :], -1.0, z[:, :], ALU.mult, ALU.min), "nabs")
                need(dve, b, "pe_kkk", "k0")
                done(dve.tensor_tensor(kk0[:, :], psum(3), k0[:, :], ALU.add), "kk0")
                need(dve, b, "nabs")
                done(dve.tensor_scalar(z[:, :], z[:, :], 0.0, 0.5, ALU.min, ALU.subtract), "z_min")
                need(dve, b, "z_min", "ln1")
                done(dve.tensor_tensor(w[:, :], z[:, :], ln1[:, :], ALU.subtract), "w")
                need(dve, b, "w", "mk")
                done(dve.tensor_tensor(mk[:, :], mk[:, :], w[:, :], ALU.mult), "w_mk")
                need(dve, b, "a", "ma")
                done(dve.scalar_tensor_tensor(nabs[:, :], ma[:, :], 1.0, a[:, :], ALU.subtract, ALU.mult), "a_rest")
                need(dve, b, "a_rest")
                done(dve.tensor_tensor(ma[:, :], ma[:, :], nabs[:, :], ALU.subtract), "k_factor")
                need(dve, b, "k_factor")
                done(dve.tensor_tensor(k0[:, :], k0[:, :], ma[:, :], ALU.mult), "k_part")
                need(dve, b, "k_part", "exp_wmk")
                done(dve.tensor_tensor(kept["k"][:, b, :], k0[:, :], mk[:, :], ALU.mult), "k_out")
                need(dve, b, "pe_ss")
                done(dve.tensor_scalar(knorm[:, :], psum(7), 1e-24, None, ALU.max), "ss")
                need(dve, b, "sqrt_ss")
                done(dve.reciprocal(knorm[:, :], knorm[:, :]), "inv_norm")
                need(dve, b, "inv_norm")
                done(dve.tensor_tensor(kk0[:, :], kk0[:, :], knorm[:, :], ALU.mult), "kk")
                need(dve, b, "kk")
                dve.tensor_copy(kept["kk"][:, b, :], kk0[:, :])
                done(dve.scalar_tensor_tensor(kept["b"][:, b, :], kk0[:, :], -1.0, a[:, :], ALU.mult, ALU.mult),
                     "kkb_out")
                need(dve, b, "kkb_out", "wt", "g_out", "k_out")
                dve.memset(xx[:, 0:1], 0.0).then_inc(row_free, 1)

        @block.gpsimd
        def _(pool):
            pool.wait_ge(sem("stats"), 32)
            pool.wait_ge(sem("half"), 2)
            pool.tensor_scalar(rstd[:, :], meanvar[:, :, 1], EPS, 1.0, ALU.add, ALU.mult).then_inc(sem("var"), 1)
            pool.wait_ge(sem("var"), 1)
            pool.tensor_tensor(rstd[:, :], rstd[:, :], mhalf[:, :], ALU.pow).then_inc(sem("rstd"), 1)


def mixer_scan(nc, ins, kept):
    with ExitStack() as ctx:
        def sb(name, shape):
            return ctx.enter_context(nc.sbuf_tensor("scan_" + name, shape, F32))

        def sem(name):
            return ctx.enter_context(nc.semaphore("scan_" + name))

        spread = sb("spread", [P, HS, P])
        gather = sb("gather", [P, HS, P])
        ones = sb("ones", [P, P])
        outer = sb("outer", [P, CHUNK, BATCH, HS])
        states = sb("states", [P, CHUNK + 1, BATCH, HS])
        weighed = sb("weighed", [P, BATCH, CHUNK, HS])
        s_kk = sb("s_kk", [P, BATCH, HS])
        s_next = sb("s_next", [P, BATCH, HS])
        s_new = sb("s_new", [P, BATCH, HS])
        bank_v = [ctx.enter_context(nc.psum_tensor(f"scan_bank_v{n}", [P, 512], F32)) for n in range(2)]
        bank_sa = [ctx.enter_context(nc.psum_tensor(f"scan_bank_sa{n}", [P, 512], F32)) for n in range(2)]
        bank_y = ctx.enter_context(nc.psum_tensor("scan_bank_y", [P, 512], F32))

        loaded = sem("loaded")
        carried = sem("carried")
        pe_v = sem("pe_v")
        outer_set = sem("outer_set")
        kk_set = sem("kk_set")
        pe_sa = sem("pe_sa")
        decayed = sem("decayed")
        added = sem("added")
        rank_one = sem("rank_one")
        state_set = sem("state_set")
        weighed_set = sem("weighed_set")
        pe_y = sem("pe_y")
        y_set = sem("y_set")

        block = ctx.enter_context(nc.Block())

        @block.sync
        def _(sp):
            sp.dma_start(spread[:, :, :], ins["table_spread"]).then_inc(loaded, 16)
            sp.dma_start(gather[:, :, :], ins["table_gather"]).then_inc(loaded, 16)
            sp.dma_start(ones[:, :], ins["table_mix"][:, MATS.index("ones"), :]).then_inc(loaded, 16)

        @block.tensor
        def _(pe):
            pe.wait_ge(loaded, 48)
            with pe.Fori(0, SEQ // CHUNK) as c:
                for i in range(HS):
                    if i >= 2:
                        pe.wait_ge(outer_set, c * HS + (i - 1))
                    else:
                        pe.wait_ge(carried, c + 1)
                    pe.matmul(bank_v[i % 2][:, :], spread[:, i, :], kept["v"][:, :, bass.ds(c * CHUNK, CHUNK)],
                              start=True, stop=True).then_inc(pe_v, 1)
                with pe.Fori(0, CHUNK // GROUP) as g:
                    for u in range(GROUP):
                        n = c * CHUNK + g * GROUP + u
                        pe.wait_ge(kk_set, n + 1)
                        pe.matmul(bank_sa[u % 2][:, 0:BATCH * HS], ones[:, :], s_kk[:, :, :],
                                  start=True, stop=True).then_inc(pe_sa, 1)
                pe.wait_ge(weighed_set, (c + 1) * BATCH)
                for i in range(HS):
                    last = pe.matmul(bank_y[:, :], gather[:, i, :], weighed[:, :, :, i],
                                     start=i == 0, stop=i == HS - 1)
                last.then_inc(pe_y, 1)

        @block.scalar
        def _(act):
            with act.Fori(0, SEQ // CHUNK) as c:
                act.wait_ge(pe_y, c + 1)
                act.copy(kept["y"][:, :, bass.ds(c * CHUNK, CHUNK)],
                         bank_y[:, :].rearrange("p (b t) -> p b t", b=BATCH)).then_inc(y_set, 1)

        @block.vector
        def _(dve):
            dve.memset(states[:, 0, :, :], 0.0).then_inc(carried, 1)
            with dve.Fori(0, SEQ // CHUNK) as c:
                dve.wait_ge(carried, c + 1)
                for i in range(HS):
                    dve.wait_ge(pe_v, c * HS + (i + 1))
                    dve.tensor_tensor(outer[:, :, :, i].rearrange("p t b -> p b t"),
                                      bank_v[i % 2][:, :].rearrange("p (b t) -> p b t", b=BATCH),
                                      kept["k"][:, :, bass.ds(c * CHUNK, CHUNK)], ALU.mult).then_inc(outer_set, 1)
                with dve.Fori(0, CHUNK // GROUP) as g:
                    for u in range(GROUP):
                        local = g * GROUP + u
                        n = c * CHUNK + local

                        def at(name):
                            return kept[name][:, :, bass.ds(n, 1)].broadcast_to([P, BATCH, HS])

                        if u:
                            dve.wait_ge(state_set, n)
                        else:
                            dve.wait_ge(outer_set, (c + 1) * HS)
                            dve.wait_ge(carried, c + 1)
                            dve.wait_ge(state_set, n)
                        dve.tensor_tensor(s_kk[:, :, :], states[:, local, :, :], at("kk"), ALU.mult).then_inc(kk_set, 1)
                        dve.tensor_tensor(s_next[:, :, :], states[:, local, :, :], at("wt"), ALU.mult
                                          ).then_inc(decayed, 1)
                        dve.wait_ge(decayed, n + 1)
                        dve.tensor_tensor(s_next[:, :, :], s_next[:, :, :], outer[:, local, :, :], ALU.add
                                          ).then_inc(added, 1)
                        dve.wait_ge(pe_sa, n + 1)
                        dve.tensor_tensor(s_new[:, :, :],
                                          bank_sa[u % 2][:, 0:BATCH * HS].rearrange("p (b i) -> p b i", b=BATCH),
                                          at("b"), ALU.mult).then_inc(rank_one, 1)
                        dve.wait_ge(rank_one, n + 1)
                        dve.wait_ge(added, n + 1)
                        dve.tensor_tensor(states[:, local + 1, :, :], s_next[:, :, :], s_new[:, :, :], ALU.add
                                          ).then_inc(state_set, 1)
                dve.wait_ge(state_set, (c + 1) * CHUNK)
                for b in range(BATCH):
                    dve.tensor_tensor(weighed[:, b, :, :], states[:, 1:CHUNK + 1, b, :],
                                      kept["r"][:, b, bass.ds(c * CHUNK, CHUNK)].unsqueeze(2).broadcast_to(
                                          [P, CHUNK, HS]), ALU.mult).then_inc(weighed_set, 1)
                dve.wait_ge(y_set, c + 1)
                dve.tensor_copy(states[:, 0, :, :], states[:, CHUNK, :, :]).then_inc(carried, 1)


def mixer_output(nc, shared, mat, vec, kept):
    x = shared["x"]
    with ExitStack() as ctx:
        def sb(name):
            return ctx.enter_context(nc.sbuf_tensor("mixout_" + name, [P, SEQ], F32))

        yc, ysq, ystd, rk, out = (sb(n) for n in ("yc", "ysq", "ystd", "rk", "out"))
        banks = [ctx.enter_context(nc.psum_tensor(f"mixout_bank{n}", [P, 512], F32)) for n in range(4)]

        done, need = chain_steps(ctx, nc, "mixout", OUT_STEPS)
        row_free = ctx.enter_context(nc.semaphore("mixout_row_free"))

        block = ctx.enter_context(nc.Block())

        @block.tensor
        def _(pe):
            with pe.Fori(0, BATCH) as b:
                pe.wait_ge(row_free, b + 1)
                done(pe.matmul(banks[0][:, :], mat["mean"], kept["y"][:, b, :], start=True, stop=True), "pe_mean")
                need(pe, b, "rk")
                done(pe.matmul(banks[1][:, :], mat["ones"], rk[:, :], start=True, stop=True), "pe_rk")
                need(pe, b, "ysq")
                done(pe.matmul(banks[2][:, :], mat["mean"], ysq[:, :], start=True, stop=True), "pe_var")
                need(pe, b, "gated")
                for T in range(4):
                    last = pe.matmul(banks[3][:, T * P:(T + 1) * P], out[:, T * P:(T + 1) * P], mat["o"],
                                     start=True, stop=True)
                done(last, "pe_out")

        @block.scalar
        def _(act):
            with act.Fori(0, BATCH) as b:
                need(act, b, "yc")
                done(act.activation(ysq[:, :], yc[:, :], ACT.Square), "ysq")
                need(act, b, "var")
                done(act.activation(ystd[:, :], ystd[:, :], ACT.Sqrt), "std")

        @block.vector
        def _(dve):
            dve.memset(out[:, 0:1], 0.0).then_inc(row_free, 1)
            dve.wait_ge(row_free, 1)
            with dve.Fori(0, BATCH) as b:
                dve.wait_ge(row_free, b + 1)
                done(dve.scalar_tensor_tensor(rk[:, :], kept["r"][:, b, :], vec["faaaa"], kept["k"][:, b, :],
                                              ALU.mult, ALU.mult), "rk")
                need(dve, b, "pe_mean")
                done(dve.tensor_tensor(yc[:, :], kept["y"][:, b, :], banks[0][:, :], ALU.subtract), "yc")
                need(dve, b, "pe_rk")
                done(dve.tensor_tensor(out[:, :], banks[1][:, :], kept["v"][:, b, :], ALU.mult), "bonus")
                need(dve, b, "pe_var")
                done(dve.tensor_scalar(ystd[:, :], banks[2][:, :], EPS_HEAD, None, ALU.add), "var")
                need(dve, b, "std")
                done(dve.reciprocal(ystd[:, :], ystd[:, :]), "inv_std")
                need(dve, b, "inv_std")
                done(dve.tensor_tensor(yc[:, :], yc[:, :], ystd[:, :], ALU.mult), "normed")
                need(dve, b, "normed")
                done(dve.tensor_scalar(yc[:, :], yc[:, :], vec["ln_w"], vec["ln_b"], ALU.mult, ALU.add), "scaled")
                need(dve, b, "scaled", "bonus")
                done(dve.tensor_tensor(yc[:, :], yc[:, :], out[:, :], ALU.add), "summed")
                need(dve, b, "summed")
                done(dve.tensor_tensor(out[:, :], yc[:, :], kept["g"][:, b, :], ALU.mult), "gated")
                need(dve, b, "pe_out")
                rows = x[:, bass.ds(b * 4, 4), :]
                dve.tensor_tensor(rows, banks[3][:, :].rearrange("p (t d) -> p t d", t=4), rows, ALU.add
                                  ).then_inc(row_free, 1)


def setup(nc, shared, x_dram, tables, scales):
    with ExitStack() as ctx:
        base = ctx.enter_context(nc.sbuf_tensor("rot_base", [P, 4, 4, HD], F32))
        qk_scale = ctx.enter_context(nc.sbuf_tensor("qk_scale", [P, 2, DEPTH, HD], F32))
        loaded = ctx.enter_context(nc.semaphore("setup_loaded"))
        block = ctx.enter_context(nc.Block())

        @block.sync
        def _(sp):
            for b in range(BATCH):
                sp.dma_start(shared["x"][:, 4 * b:4 * b + 4, :], x_dram[b].rearrange("(t p) d -> p t d", p=P)
                             ).then_inc(loaded, 16)
            sp.dma_start(shared["ident"][:, :], tables["ident"]).then_inc(loaded, 16)
            sp.dma_start(shared["mask"][:, :], tables["mask"]).then_inc(loaded, 16)
            sp.dma_start(base[:, :, :, :], tables["rot"]).then_inc(loaded, 16)
            for n in range(2):
                sp.dma_start(qk_scale[:, n, :, :], scales[n].partition_broadcast(P)).then_inc(loaded, 16)

        @block.vector
        def _(dve):
            dve.wait_ge(loaded, 16 * 9)
            for layer in range(DEPTH):
                for kind in range(4):
                    s = qk_scale[:, kind // 2, layer, :].rearrange("p (f d) -> p f d", f=2)
                    if kind % 2:
                        s = s[:, ::-1, :]
                    dve.tensor_tensor(shared["rot"][:, layer, :, kind, :].rearrange("p t (f d) -> p t f d", f=2),
                                      base[:, :, kind, :].rearrange("p t (f d) -> p t f d", f=2),
                                      s.unsqueeze(1).broadcast_to([P, 4, 2, HD // 2]), ALU.mult)


def store(nc, shared, out):
    with ExitStack() as ctx:
        stored = ctx.enter_context(nc.semaphore("stored"))
        block = ctx.enter_context(nc.Block())

        @block.sync
        def _(sp):
            for b in range(BATCH):
                sp.dma_start(out[b].rearrange("(t p) d -> p t d", p=P), shared["x"][:, 4 * b:4 * b + 4, :]
                             ).then_inc(stored, 16)
            sp.wait_ge(stored, 16 * BATCH)


def program(nc, ins, out, phases=("retention", "stack0", "mixer", "stack1")):
    with ExitStack() as ctx:
        def sb(name, shape):
            return ctx.enter_context(nc.sbuf_tensor(name, shape, F32))

        shared = {
            "x": sb("x_outer", [P, 16, DIM]),
            "ident": sb("ident", [P, P]),
            "mask": sb("band", [P, 160]),
            "rot": sb("rot_tables", [P, DEPTH, 4, 4, HD]),
        }
        tables = {k: ins["table_" + k] for k in ("ident", "mask", "rot")}
        setup(nc, shared, ins["L0_attn_a_X"], tables, (ins["L0_ffn_q_scale"], ins["L0_ffn_k_scale"]))
        stack_weights = {k: ins["L0_ffn_" + k] for k in ("Wqkv", "Wo", "W1", "W2", "b1", "b2", "ln_g", "ln_b")}
        for phase in phases:
            if phase == "retention":
                retention(nc, shared, ins)
            elif phase == "mixer":
                mixer(nc, shared, ins)
            else:
                ffn_stack(nc, {**shared, "tag": phase + "_"}, stack_weights)
        store(nc, shared, out)


def shape_tables():
    f = np.float32
    t = {"ident": np.eye(P, dtype=f)}
    ahead = np.arange(P)[:, None] - (np.arange(P + WINDOW)[None, :] - WINDOW)
    t["mask"] = np.where((ahead >= 0) & (ahead <= WINDOW), f(0), f(-1e30)).astype(f)
    pos = np.arange(SEQ, dtype=f)
    half = np.arange(0, HD, 2, dtype=f)
    freq = (f(1.0) / np.power(f(10000.0), half / f(HD))).astype(f)
    angle = (pos[:, None] * freq[None, :]).astype(f)
    scale = np.power(((half + f(0.4 * HD)) / f(1.4 * HD)).astype(f)[None, :],
                     ((pos - f(SEQ // 2)) / f(WINDOW // 2)).astype(f)[:, None]).astype(f)
    cos, sin = (np.concatenate([g(angle.astype(np.float64))] * 2, -1).astype(f) for g in (np.cos, np.sin))
    scale = np.concatenate([scale, scale], -1)
    sin = sin * np.where(np.arange(HD) < HD // 2, f(-1), f(1))
    kinds = np.stack([cos * scale, sin * scale, cos / scale, sin / scale], 1).astype(f)
    t["rot"] = np.ascontiguousarray(kinds.reshape(4, P, 4, HD).transpose(1, 0, 2, 3))
    half = DIM // 2
    power = pos / f(SEQ)
    scale = np.power(((np.arange(0, DIM, 2, dtype=f) + f(0.4 * DIM)) / f(1.4 * DIM)).astype(f)[None, :],
                     power[:, None]).astype(f)
    freq = (f(1.0) / np.power(f(10000.0), (np.arange(half, dtype=f) / f(half)))).astype(f)
    angle = (pos[:, None] * freq[None, :]).astype(f).astype(np.float64)
    rows = []
    for g in (np.cos, np.sin):
        both = [np.repeat((g(angle).astype(f) * sc).astype(f), 2, -1) for sc in (scale, f(1.0) / scale)]
        rows.append(np.concatenate(both, -1))
    rows[1] = rows[1] * np.where(np.arange(2 * DIM) % 2 == 0, f(-1), f(1))
    t["xpos"] = np.ascontiguousarray(np.stack(rows, 1).reshape(4, P, 2, 2 * DIM).transpose(1, 0, 2, 3)).astype(f)
    offset = np.abs(np.arange(P)[:, None] - np.arange(7 * P)[None, :] + 3 * P)
    t["decay"] = np.power(f(0.9), offset.astype(f)).astype(f)
    head, item = np.arange(P) // HS, np.arange(P) % HS
    same = head[:, None] == head[None, :]
    t["ones"] = same.astype(f)
    t["mean"] = (same / HS).astype(f)
    t["spread"] = np.stack([same & (item[:, None] == i) for i in range(HS)], 1).astype(f)
    t["gather"] = np.stack([same & (item[None, :] == i) for i in range(HS)], 1).astype(f)
    return t


def arrange(inputs):
    f = np.float32
    got = {k: np.asarray(v) for k, v in inputs.items()}
    mixer_in = {k[len("L0_attn_b_"):]: got[k] for k in got if k.startswith("L0_attn_b_")}
    ins = {k: v for k, v in got.items() if not k.startswith("L0_attn_b_")}
    t = shape_tables()

    def placed(parts, by_column):
        m = np.zeros((P, P), f)
        for at, part in parts:
            if by_column:
                m[:, at:at + part.shape[1]] = part
            else:
                m[at:at + part.shape[0], :] = part
        return m

    w = mixer_in
    mats = {
        "maa1": w["maa_w1"].T, "maa2": w["maa_w2"].reshape(P, P),
        "r": w["Wr"].T, "k": w["Wk"].T, "v": w["Wv"].T, "o": w["Wo"].T,
        "gate1": w["gate_w1"].T, "gate2": w["gate_w2"],
        "wa1": placed(((0, w["decay_w1"].T), (64, w["aaa_w1"].T), (96, w["ma_w1"].T)), True),
        "wa2": placed(((0, w["decay_w2"]), (64, w["aaa_w2"]), (96, w["ma_w2"])), False),
        "k1": placed(((0, w["kkk_w1"].T), (32, w["mk_w1"].T)), True),
        "k2": placed(((0, w["kkk_w2"]), (32, w["mk_w2"])), False),
        "ones": t.pop("ones"), "mean": t.pop("mean"),
    }
    vecs = {
        "maa_x": w["time_maa_x"], **{f"maa{g}": w["time_maa"][g, 0, 0] for g in range(4)},
        "decay": w["time_decay"], "faaaa": w["time_faaaa"], "aaaaa": w["time_aaaaa"],
        "misc_a": w["time_misc_a"], "misc_k": w["time_misc_k"], "ln_w": w["ln_w"], "ln_b": w["ln_b"],
    }
    t["mix"] = np.stack([mats[n] for n in MATS], 1)
    t["vec"] = np.stack([vecs[n] for n in VECS], 1)
    ins.update({"table_" + k: np.ascontiguousarray(v) for k, v in t.items()})
    return ins


def kernel(**inputs):
    import concourse.bacc as bacc
    from concourse.bass_utils import run_bass_kernel_spmd

    nc = bacc.Bacc("TRN2", target_bir_lowering=False, num_devices=1)
    arrays = arrange(inputs)
    ins = {k: nc.dram_tensor(k, v.shape, mybir.dt.from_np(v.dtype), kind="ExternalInput").ap()
           for k, v in arrays.items()}
    out = nc.dram_tensor("out", (BATCH, SEQ, DIM), F32, kind="ExternalOutput").ap()
    program(nc, ins, out)
    return run_bass_kernel_spmd(nc, [arrays], core_ids=[0]).results[0]["out"]
```

```python
from contextlib import ExitStack

import numpy as np

import concourse.bass as bass
from concourse import mybir

F32 = mybir.dt.float32
ALU = mybir.AluOpType
ACT = mybir.ActivationFunctionType
AX = mybir.AxisListType

P = 128
DIM = 128
BATCH, SEQ = 4, 512
EPS = 1e-5
LOWEST = -3.0e38
DEPTH, HEADS, HD, WINDOW = 6, 16, 64, 32
INNER = HEADS * HD
PAIRS = HEADS // 2
HID = DIM * 4 * 2 // 3
TILES = DEPTH * BATCH * SEQ // P
N_LOADS = 9
N_CONSTS = 6




def layernorm_rows(eng_wait, dve, stats, meanvar, src, n, stats_sem):
    dve.bn_stats(stats[:, n, :], src).then_inc(stats_sem, 1)
    dve.wait_ge(stats_sem, eng_wait)
    dve.bn_aggr(meanvar[:, n, :], stats[:, n, :]).then_inc(stats_sem, 1)


def retention(nc, shared, ins):
    x, ident = shared["x"], shared["ident"]
    with ExitStack() as ctx:
        def sb(name, shape):
            return ctx.enter_context(nc.sbuf_tensor("ret_" + name, shape, F32))

        def ps(name):
            return ctx.enter_context(nc.psum_tensor("ret_" + name, [P, 512], F32))

        def sem(name):
            return ctx.enter_context(nc.semaphore("ret_" + name))

        w_qkv = sb("w_qkv", [P, 3 * DIM])
        xpos = sb("xpos", [P, 4, 2, 2 * DIM])
        decay = sb("decay", [P, 7 * P])
        mhalf = sb("mhalf", [P, 16])
        stats = sb("stats", [P, 16, 6])
        meanvar = sb("meanvar", [P, 16, 2])
        rstd = sb("rstd", [P, 16])
        x_n = sb("x_n", [P, 4, DIM])
        xn_t = sb("xn_t", [P, 4, P])
        cosined = sb("cosined", [P, 4, 2 * DIM])
        sined = sb("sined", [P, 4, 2 * DIM])
        q_k = sb("q_k", [P, 4, 2 * DIM])
        v = sb("v", [P, 3, 4, DIM])
        q_t = sb("q_t", [P, 2, 4, P])
        k_t = sb("k_t", [P, 2, 4, P])
        row_max = sb("row_max", [P, 4])
        neg_max = sb("neg_max", [P, 4])
        row_sum = sb("row_sum", [P, 4])
        inv_sum = sb("inv_sum", [P, 4])
        e = sb("e", [P, 2, SEQ])
        prob = sb("prob", [P, 2, SEQ])
        p_t = sb("p_t", [P, 2, SEQ])

        bank_x = ps("bank_x")
        bank_qkv = [ps("bank_qkv0"), ps("bank_qkv1")]
        bank_turn = ps("bank_turn")
        bank_s = [ps("bank_s0"), ps("bank_s1")]
        bank_pt = ps("bank_pt")
        bank_o = ps("bank_o")

        loaded = sem("loaded")
        half_set = sem("half_set")
        stats_set = sem("stats_set")
        var_set = sem("var_set")
        rstd_set = sem("rstd_set")
        xn_set = sem("xn_set")
        pe_xn = sem("pe_xn")
        xn_turned = sem("xn_turned")
        pe_qkv = sem("pe_qkv")
        v_set = sem("v_set")
        rotated = sem("rotated")
        qk_set = sem("qk_set")
        pe_qk = sem("pe_qk")
        qk_turned = sem("qk_turned")
        pe_s = sem("pe_s")
        max_set = sem("max_set")
        e_set = sem("e_set")
        inv_set = sem("inv_set")
        prob_set = sem("prob_set")
        pe_pt = sem("pe_pt")
        pt_set = sem("pt_set")
        pe_o = sem("pe_o")
        x_set = sem("x_set")

        block = ctx.enter_context(nc.Block())

        @block.sync
        def _(sp):
            for n, name in enumerate(("W_Q", "W_K", "W_V")):
                sp.dma_start(w_qkv[:, n * DIM:(n + 1) * DIM], ins["L0_attn_a_" + name]).then_inc(loaded, 16)
            sp.dma_start(xpos[:, :, :, :], ins["table_xpos"]).then_inc(loaded, 16)
            sp.dma_start(decay[:, :], ins["table_decay"]).then_inc(loaded, 16)

        @block.tensor
        def _(pe):
            pe.wait_ge(loaded, 16 * 5)

            def project(n):
                T = n % 4
                pe.wait_ge(xn_set, n + 1)
                if n:
                    pe.wait_ge(xn_turned, n)
                pe.transpose(bank_x[:, 0:P], x_n[:, T, :], ident[:, :]).then_inc(pe_xn, 1)
                pe.wait_ge(xn_turned, n + 1)
                if n >= 2:
                    pe.wait_ge(v_set, n - 1)
                pe.matmul(bank_qkv[n % 2][:, 0:3 * DIM], xn_t[:, T, :], w_qkv[:, :],
                          start=True, stop=True).then_inc(pe_qkv, 1)

            def turn(n):
                T = n % 4
                pe.wait_ge(qk_set, n + 1)
                if n:
                    pe.wait_ge(qk_turned, n)
                pe.transpose(bank_turn[:, 0:P], q_k[:, T, 0:P], ident[:, :])
                pe.transpose(bank_turn[:, P:2 * P], q_k[:, T, P:2 * P], ident[:, :]).then_inc(pe_qk, 1)

            def scores(n):
                b, T = n // 4 % 2, n % 4
                pe.wait_ge(qk_turned, n - T + 4)
                if n >= 2:
                    pe.wait_ge(e_set, n - 1)
                pe.matmul(bank_s[n % 2][:, :], q_t[:, b, T, :], k_t[:, b, :, :], start=True, stop=True
                          ).then_inc(pe_s, 1)

            def attend(n):
                pe.wait_ge(prob_set, n + 1)
                if n:
                    pe.wait_ge(pt_set, n)
                for j in range(4):
                    last = pe.transpose(bank_pt[:, j * P:(j + 1) * P], prob[:, n % 2, j * P:(j + 1) * P], ident[:, :])
                last.then_inc(pe_pt, 1)
                pe.wait_ge(pt_set, n + 1)
                if n:
                    pe.wait_ge(x_set, n)
                for j in range(4):
                    last = pe.matmul(bank_o[:, 0:DIM], p_t[:, n % 2, j * P:(j + 1) * P], v[:, n // 4 % 3, j, :],
                                     start=j == 0, stop=j == 3)
                last.then_inc(pe_o, 1)

            for n in range(4 * BATCH + 6):
                if n < 4 * BATCH:
                    project(n)
                if 1 <= n <= 4 * BATCH:
                    turn(n - 1)
                if 4 <= n < 4 * BATCH + 4:
                    scores(n - 4)
                if 5 <= n < 4 * BATCH + 5:
                    attend(n - 5)

        @block.scalar
        def _(act):
            for n in range(4 * BATCH + 6):
                if n < 4 * BATCH:
                    T, b = n % 4, n // 4 % 2
                    act.wait_ge(pe_xn, n + 1)
                    act.copy(xn_t[:, T, :], bank_x[:, 0:P]).then_inc(xn_turned, 1)
                    act.wait_ge(rotated, n + 1)
                    if n >= 12:
                        act.wait_ge(pe_o, n - n % 4 - 8)
                    act.copy(v[:, n // 4 % 3, T, :], bank_qkv[n % 2][:, 2 * DIM:3 * DIM]).then_inc(v_set, 1)
                if 1 <= n <= 4 * BATCH:
                    m = n - 1
                    act.wait_ge(pe_qk, m + 1)
                    act.copy(q_t[:, m // 4 % 2, m % 4, :], bank_turn[:, 0:P])
                    act.copy(k_t[:, m // 4 % 2, m % 4, :], bank_turn[:, P:2 * P]).then_inc(qk_turned, 1)
                if 4 <= n < 4 * BATCH + 4:
                    m = n - 4
                    act.wait_ge(max_set, 2 * m + 2)
                    if m >= 2:
                        act.wait_ge(prob_set, m - 1)
                    act.activation(e[:, m % 2, :], bank_s[m % 2][:, :], ACT.Exp, bias=neg_max[:, m % 4:m % 4 + 1],
                                   accum_out=row_sum[:, m % 4:m % 4 + 1]).then_inc(e_set, 1)
                if 5 <= n < 4 * BATCH + 5:
                    m = n - 5
                    act.wait_ge(pe_pt, m + 1)
                    if m >= 2:
                        act.wait_ge(pe_o, m - 1)
                    act.copy(p_t[:, m % 2, :], bank_pt[:, :]).then_inc(pt_set, 1)

        @block.vector
        def _(dve):
            dve.memset(mhalf[:, :], -0.5).then_inc(half_set, 1)
            for n in range(16):
                layernorm_rows(2 * n + 1, dve, stats, meanvar, x[:, n, :], n, stats_set)
            dve.wait_ge(rstd_set, 1)
            dve.wait_ge(loaded, 16 * 5)
            for n in range(4 * BATCH + 6):
                if n < 4 * BATCH:
                    T = n % 4
                    if n >= 4:
                        dve.wait_ge(pe_xn, n - 3)
                    dve.tensor_scalar(x_n[:, T, :], x[:, n, :], meanvar[:, n, 0:1], rstd[:, n:n + 1],
                                      ALU.subtract, ALU.mult).then_inc(xn_set, 1)
                    dve.wait_ge(pe_qkv, n + 1)
                    if n >= 4:
                        dve.wait_ge(qk_set, n - 3)
                    src = bank_qkv[n % 2][:, 0:2 * DIM]
                    dve.tensor_tensor(cosined[:, T, :], src, xpos[:, T, 0, :], ALU.mult)
                    dve.tensor_tensor(sined[:, T, :].rearrange("p (n f) -> p n f", f=2),
                                      src.rearrange("p (n f) -> p n f", f=2)[:, :, ::-1],
                                      xpos[:, T, 1, :].rearrange("p (n f) -> p n f", f=2),
                                      ALU.mult).then_inc(rotated, 1)
                if 4 <= n < 4 * BATCH + 4:
                    m = n - 4
                    c = m % 4
                    dve.wait_ge(pe_s, m + 1)
                    dve.tensor_reduce(row_max[:, c:c + 1], bank_s[m % 2][:, :], AX.X, ALU.max).then_inc(max_set, 1)
                    dve.wait_ge(max_set, 2 * m + 1)
                    dve.tensor_scalar(neg_max[:, c:c + 1], row_max[:, c:c + 1], -1.0, None, ALU.mult
                                      ).then_inc(max_set, 1)
                    dve.wait_ge(e_set, m + 1)
                    dve.reciprocal(inv_sum[:, c:c + 1], row_sum[:, c:c + 1]).then_inc(inv_set, 1)
                    dve.wait_ge(inv_set, m + 1)
                    if m >= 2:
                        dve.wait_ge(pe_pt, m - 1)
                    d = (3 - m % 4) * P
                    dve.scalar_tensor_tensor(prob[:, m % 2, :], e[:, m % 2, :], inv_sum[:, c:c + 1],
                                             decay[:, d:d + SEQ], ALU.mult, ALU.mult).then_inc(prob_set, 1)
                if 5 <= n < 4 * BATCH + 5:
                    m = n - 5
                    dve.wait_ge(pe_o, m + 1)
                    dve.tensor_tensor(x[:, m, :], bank_o[:, 0:DIM], x[:, m, :], ALU.add).then_inc(x_set, 1)

        @block.gpsimd
        def _(pool):
            pool.wait_ge(stats_set, 32)
            pool.wait_ge(half_set, 1)
            pool.tensor_scalar(rstd[:, :], meanvar[:, :, 1], EPS, 1.0, ALU.add, ALU.mult).then_inc(var_set, 1)
            pool.wait_ge(var_set, 1)
            pool.tensor_tensor(rstd[:, :], rstd[:, :], mhalf[:, :], ALU.pow).then_inc(rstd_set, 1)
            for n in range(4 * BATCH):
                T = n % 4
                pool.wait_ge(rotated, n + 1)
                if n >= 4:
                    pool.wait_ge(pe_qk, n - 3)
                pool.tensor_tensor(q_k[:, T, :], cosined[:, T, :], sined[:, T, :], ALU.add).then_inc(qk_set, 1)
def ffn_stack(nc, shared, w):
    xo, ident, rot, mask = shared["x"], shared["ident"], shared["rot"], shared["mask"]
    with ExitStack() as ctx:
        def sb(name, shape):
            return ctx.enter_context(nc.sbuf_tensor(shared["tag"] + name, shape, F32))

        def ps(name):
            return ctx.enter_context(nc.psum_tensor(shared["tag"] + name, [P, 512], F32))

        def sem(name):
            return ctx.enter_context(nc.semaphore(shared["tag"] + name))

        w_qkv = sb("w_qkv", [P, 2, 3 * INNER])
        w_o = sb("w_o", [P, 2, PAIRS, DIM])
        w_1 = sb("w_1", [P, 2, 2 * HID])
        w_2 = sb("w_2", [P, 2, 3, DIM])
        b_1 = sb("b_1", [P, 2, 2 * HID])
        b_2 = sb("b_2", [P, 2, DIM])
        ln_gb = sb("ln_gb", [P, 2, 2])
        xres = sb("xres", [P, 16, DIM])
        xin = sb("xin", [P, 4, DIM])
        xmid = sb("xmid", [P, 4, DIM])
        xmid_b = sb("xmid_b", [P, 4, DIM])
        xshift = sb("xshift", [P, 4 * P + 1])
        mshift = sb("mshift", [P, 4 * P + 1])
        sq = sb("sq", [P, 2, 512])
        rot_c = sb("rot_c", [P, 2, 512])
        rot_s = sb("rot_s", [P, 2, 512])
        roped = sb("roped", [P, 2, 512])
        ssq = sb("ssq", [P, 4, 4, 8])
        rnorm = sb("rnorm", [P, 4, 4, 8])
        nrn8 = sb("nrn8", [P, 4, HEADS])
        q_t = sb("q_t", [P, 2, PAIRS, P])
        k_z = sb("k_z", [P, 4, PAIRS, 2, P])
        v_n = sb("v_n", [P, 4, INNER])
        s_m = sb("s_m", [P, 4, 2, 160])
        prob = sb("prob", [P, 4, 2, 256])
        smax = sb("smax", [P, 4, HEADS])
        nbias = sb("nbias", [P, 4, HEADS])
        psums = sb("psums", [P, 4, HEADS])
        prec = sb("prec", [P, 4, HEADS])
        p_t = sb("p_t", [P, 2, 320])
        o_t = sb("o_t", [P, 2, PAIRS, P])
        stats = sb("stats", [P, 16, 6])
        meanvar = sb("meanvar", [P, 16, 2])
        rstd = sb("rstd", [P, 16, 1])
        mhalf = sb("mhalf", [P, 16])
        x_n = sb("x_n", [P, 2, DIM])
        xn_t = sb("xn_t", [P, 2, DIM])
        h_gate = sb("h_gate", [P, HID])
        h_act = sb("h_act", [P, HID])
        h_lin = sb("h_lin", [P, HID])
        h = sb("h", [P, HID])
        h_t = sb("h_t", [P, 3, P])

        bank_proj = [ps("bank_proj0"), ps("bank_proj1")]
        bank_turn = ps("bank_turn")
        bank_s = [ps("bank_s0"), ps("bank_s1")]
        bank_pt = ps("bank_pt")
        bank_o = ps("bank_o")
        bank_misc = ps("bank_misc")

        passed = {e.engine: sem(f"passed_{n}") for n, e in enumerate((nc.scalar, nc.vector, nc.gpsimd))}
        weights_in = sem("weights_in")
        consts_set = sem("consts_set")
        x_var = sem("x_var")
        x_stats = sem("x_stats")
        x_rstd = sem("x_rstd")
        x_ready = sem("x_ready")
        xin_set = sem("xin_set")
        pe_x = sem("pe_x")
        x_turned = sem("x_turned")
        proj_done = sem("proj_done")
        rot_read = sem("rot_read")
        sq_done = sem("sq_done")
        ssq_done = sem("ssq_done")
        rope_chain = sem("rope_chain")
        ln_chain = sem("ln_chain")
        roped_set = sem("roped_set")
        rn8_set = sem("rn8_set")
        pe_turn = sem("pe_turn")
        turned = sem("turned")
        v_set = sem("v_set")
        pe_s = sem("pe_s")
        masked = sem("masked")
        nbias_set = sem("nbias_set")
        exp_done = sem("exp_done")
        prec_set = sem("prec_set")
        normed = sem("normed")
        pe_pt = sem("pe_pt")
        pt_set = sem("pt_set")
        pe_pv = sem("pe_pv")
        o_set = sem("o_set")
        pe_wo = sem("pe_wo")
        xmid_set = sem("xmid_set")
        xmid_b_set = sem("xmid_b_set")
        pe_m = sem("pe_m")
        m_turned = sem("m_turned")
        pe_ms = sem("pe_ms")
        ln_stats = sem("ln_stats")
        ln_rstd = sem("ln_rstd")
        xn_set = sem("xn_set")
        pe_xn = sem("pe_xn")
        xn_turned = sem("xn_turned")
        pe_w1 = sem("pe_w1")
        hid_read = sem("hid_read")
        gelu_done = sem("gelu_done")
        h_set = sem("h_set")
        pe_h = sem("pe_h")
        h_turned = sem("h_turned")
        pe_w2 = sem("pe_w2")

        def wait(eng, s, per_tile, tile, c):
            n = tile * per_tile + c
            if isinstance(n, int) and (n <= 0 or tile >= TILES):
                return
            eng.wait_ge(s, n)

        def wait_apart(eng, s, per_tile, tile, c):
            wait(eng, s, per_tile, tile, c)
            if not isinstance(tile, int):
                eng.sem_inc(passed[eng.engine], 1)

        def slots(eng, body):
            def where(i, T):
                def tile(lag):
                    return 4 * i + (T - lag)

                def ahead(lag):
                    return i + (T - lag) // 4
                return tile, ahead

            def static(N):
                tile, ahead = where(N // 4, N % 4)
                body(N, N % 4, lambda lag: (N - lag) // 16 % 2, lambda lag: (N - lag) // 4 % 4,
                     lambda lag: 0 <= N - lag < TILES)

            for N in range(8):
                static(N)
            with eng.Fori(2, TILES // 4) as i:
                for T in range(4):
                    def parity(lag, T=T):
                        return (i + (T - lag) // 4) // 4 % 2

                    def row(lag, T=T):
                        return (i + (T - lag) // 4) % 4
                    body(4 * i + T, T, parity, row, lambda lag: True)
            for N in range(TILES, TILES + 6):
                static(N)

        CHUNK_COLS = [INNER, 0, INNER + 512, 512, 2 * INNER, 2 * INNER + 512]

        block = ctx.enter_context(nc.Block())

        @block.sync
        def _(sp):
            for layer in range(DEPTH):
                half = layer % 2
                if layer >= 1:
                    sp.wait_ge(weights_in, 16 * N_LOADS * layer)
                if layer >= 2:
                    sp.wait_ge(x_ready, 16 * layer)
                sp.dma_start(w_qkv[:, half, :], w["Wqkv"][layer]).then_inc(weights_in, 16)
                sp.dma_start(w_o[:, half, :, :], w["Wo"][layer].rearrange("(g p) n -> p g n", p=P)
                             ).then_inc(weights_in, 16)
                sp.dma_start(w_1[:, half, :], w["W1"][layer]).then_inc(weights_in, 16)
                sp.dma_start(w_2[:, half, 0:2, :], w["W2"][layer, 0:2 * P, :].rearrange("(g p) n -> p g n", p=P)
                             ).then_inc(weights_in, 16)
                sp.dma_start(w_2[0:HID - 2 * P, half, 2, :], w["W2"][layer, 2 * P:HID, :]).then_inc(weights_in, 16)
                sp.dma_start(b_1[:, half, :], w["b1"][layer].partition_broadcast(P)).then_inc(weights_in, 16)
                sp.dma_start(b_2[:, half, :], w["b2"][layer].partition_broadcast(P)).then_inc(weights_in, 16)
                sp.dma_start(ln_gb[:, half, 0:1], w["ln_g"][layer].unsqueeze(1)).then_inc(weights_in, 16)
                sp.dma_start(ln_gb[:, half, 1:2], w["ln_b"][layer].unsqueeze(1)).then_inc(weights_in, 16)
            sp.wait_ge(weights_in, 16 * N_LOADS * DEPTH)

        @block.tensor
        def _(pe):
            def turn_x(t, T):
                wait(pe, xin_set, 1, t, 1)
                wait(pe, turned, 4, t - 1, 0)
                pe.transpose(bank_turn[:, 0:P], xin[:, T, :], ident[:, :]).then_inc(pe_x, 1)

            def project(t, T, c, half):
                if c == 0:
                    wait(pe, x_turned, 1, t, 1)
                    if T == 0:
                        pe.wait_ge(weights_in, (t // 16 + 1) * (16 * N_LOADS))
                if c in (0, 1):
                    wait(pe, v_set, 2, t - 1, c + 1)
                elif c in (2, 3):
                    wait(pe, hid_read, 2, t - 3, c - 1)
                    wait(pe, sq_done, 4, t, c - 1)
                else:
                    wait(pe, sq_done, 4, t, c - 1)
                pe.matmul(bank_proj[c % 2][:, :], xshift[:, T * P:(T + 1) * P],
                          w_qkv[:, half, CHUNK_COLS[c]:CHUNK_COLS[c] + 512],
                          start=True, stop=True).then_inc(proj_done, 1)

            def turn_chunk(t, c):
                wait(pe, roped_set, 4, t, c + 1)
                if c == 0:
                    wait(pe, x_turned, 1, t + 1, 1)
                elif c == 2:
                    wait(pe, h_turned, 1, t - 3, 1)
                    wait(pe, turned, 4, t, c)
                else:
                    wait(pe, turned, 4, t, c)
                for g in range(4):
                    last = pe.transpose(bank_turn[:, g * P:(g + 1) * P], roped[:, c % 2, g * P:(g + 1) * P],
                                        ident[:, :])
                last.then_inc(pe_turn, 1)

            def scores(t, T, hp):
                wait(pe, turned, 4, t, 2 if hp < 4 else 4)
                wait(pe, masked, 8, t, hp - 1)
                out = bank_s[hp % 2][:, 0:320].rearrange("p (h c) -> p h c", h=2)
                last = pe.matmul(out[:, :, 32:160], q_t[:, T % 2, hp, :], k_z[:, T, hp, :, :], start=True, stop=True)
                if T > 0:
                    last = pe.matmul(out[:, :, 0:32], q_t[:, T % 2, hp, :], k_z[:, T - 1, hp, :, 96:128],
                                     start=True, stop=True)
                last.then_inc(pe_s, 1)

            def turn_probs(t, T, hp):
                wait(pe, normed, 8, t, hp + 1)
                wait(pe, pt_set, 8, t, hp)
                for j in range(2):
                    last = pe.transpose(bank_pt[:, 160 * j:160 * j + P], prob[:, hp % 4, j, P:2 * P], ident[:, :])
                    if T > 0:
                        last = pe.transpose(bank_pt[:, 160 * j + P:160 * j + 160], prob[0:32, hp % 4, j, 0:P],
                                            ident[0:32, 0:32])
                last.then_inc(pe_pt, 1)

            def weigh_values(t, T, hp):
                wait(pe, pt_set, 8, t, hp + 1)
                if hp == 0:
                    wait(pe, v_set, 2, t, 2)
                if hp % 4 == 0:
                    wait(pe, o_set, 2, t, hp // 4)
                for j in range(2):
                    head = 2 * hp + j
                    out = bank_o[64 * j:64 * j + 64, (hp % 4) * P:(hp % 4 + 1) * P]
                    last = pe.matmul(out, v_n[:, T, 64 * head:64 * head + 64], p_t[:, hp % 2, 160 * j:160 * j + P],
                                     start=True, stop=True)
                    if T > 0:
                        last = pe.matmul(out[:, 0:32], v_n[:, T - 1, 64 * head:64 * head + 64],
                                         p_t[:, hp % 2, 160 * j + P:160 * j + 160], start=False, stop=True,
                                         skip_group_check=True)
                last.then_inc(pe_pv, 1)

            def project_out(t, T, half):
                wait(pe, o_set, 2, t, 2)
                wait(pe, xn_turned, 1, t - 1, 1)
                for g in range(PAIRS):
                    last = pe.matmul(bank_misc[:, 0:DIM], o_t[:, T % 2, g, :], w_o[:, half, g, :],
                                     start=g == 0, stop=g == PAIRS - 1)
                last.then_inc(pe_wo, 1)

            def turn_mid(t, T):
                wait(pe, xmid_set, 1, t, 1)
                pe.transpose(bank_misc[:, 0:P], xmid[:, T, :], ident[:, :]).then_inc(pe_m, 1)

            def turn_mid_back(t, T):
                wait(pe, m_turned, 1, t, 1)
                wait(pe, x_ready, 1, t - 1, 17)
                pe.transpose(bank_misc[:, 0:P], mshift[:, T * P:(T + 1) * P], ident[:, :]).then_inc(pe_ms, 1)

            def turn_xn(t, T):
                wait(pe, xn_set, 1, t, 1)
                pe.transpose(bank_misc[:, 0:P], x_n[:, T % 2, :], ident[:, :]).then_inc(pe_xn, 1)

            def mlp_up(t, T, c, half):
                if c == 0:
                    wait(pe, xn_turned, 1, t, 1)
                wait(pe, sq_done, 4, t + 3, c + 1)
                if isinstance(t, int) and t + 3 >= TILES:
                    wait(pe, v_set, 2, TILES - 1, 2)
                    wait(pe, hid_read, 2, t - 1, c + 1)
                col = HID * (1 - c)
                pe.matmul(bank_proj[c][:, 0:HID], xn_t[:, T % 2, :], w_1[:, half, col:col + HID],
                          start=True, stop=True).then_inc(pe_w1, 1)

            def turn_h(t):
                wait(pe, h_set, 1, t, 1)
                wait(pe, turned, 4, t + 3, 2)
                if isinstance(t, int) and t + 3 >= TILES:
                    wait(pe, turned, 4, TILES - 1, 4)
                    wait(pe, h_turned, 1, t - 1, 1)
                for g in range(3):
                    n = min(P, HID - g * P)
                    last = pe.transpose(bank_turn[0:n, g * P:(g + 1) * P], h[:, g * P:g * P + n], ident[:, :])
                last.then_inc(pe_h, 1)

            def mlp_down(t, half):
                wait(pe, h_turned, 1, t, 1)
                wait(pe, m_turned, 1, t + 1, 1)
                for g in range(3):
                    n = min(P, HID - g * P)
                    last = pe.matmul(bank_misc[:, 0:DIM], h_t[0:n, g, :], w_2[0:n, half, g, :],
                                     start=g == 0, stop=g == 2)
                last.then_inc(pe_w2, 1)

            def slot(N, T, parity, row, runs):
                if runs(1):
                    project(N - 1, (T - 1) % 4, 0, parity(1))
                if runs(3):
                    weigh_values(N - 3, (T - 3) % 4, 4)
                    turn_probs(N - 3, (T - 3) % 4, 6)
                if runs(2):
                    scores(N - 2, (T - 2) % 4, 1)
                if runs(1):
                    project(N - 1, (T - 1) % 4, 1, parity(1))
                if runs(3):
                    weigh_values(N - 3, (T - 3) % 4, 5)
                    turn_probs(N - 3, (T - 3) % 4, 7)
                    weigh_values(N - 3, (T - 3) % 4, 6)
                if runs(0):
                    turn_x(N, T)
                if runs(4):
                    turn_xn(N - 4, (T - 4) % 4)
                if runs(2):
                    scores(N - 2, (T - 2) % 4, 2)
                    scores(N - 2, (T - 2) % 4, 3)
                    turn_probs(N - 2, (T - 2) % 4, 0)
                if runs(3):
                    weigh_values(N - 3, (T - 3) % 4, 7)
                if runs(4):
                    mlp_up(N - 4, (T - 4) % 4, 0, parity(4))
                    mlp_up(N - 4, (T - 4) % 4, 1, parity(4))
                if runs(2):
                    turn_probs(N - 2, (T - 2) % 4, 1)
                if runs(1):
                    project(N - 1, (T - 1) % 4, 2, parity(1))
                if runs(2):
                    weigh_values(N - 2, (T - 2) % 4, 0)
                    turn_probs(N - 2, (T - 2) % 4, 2)
                if runs(1):
                    turn_chunk(N - 1, 0)
                if runs(2):
                    scores(N - 2, (T - 2) % 4, 4)
                    scores(N - 2, (T - 2) % 4, 5)
                if runs(1):
                    project(N - 1, (T - 1) % 4, 3, parity(1))
                if runs(3):
                    project_out(N - 3, (T - 3) % 4, parity(3))
                if runs(2):
                    weigh_values(N - 2, (T - 2) % 4, 1)
                if runs(1):
                    turn_chunk(N - 1, 1)
                if runs(2):
                    turn_probs(N - 2, (T - 2) % 4, 3)
                if runs(1):
                    project(N - 1, (T - 1) % 4, 4, parity(1))
                if runs(4):
                    turn_h(N - 4)
                if runs(2):
                    scores(N - 2, (T - 2) % 4, 6)
                    turn_probs(N - 2, (T - 2) % 4, 4)
                    weigh_values(N - 2, (T - 2) % 4, 2)
                if runs(1):
                    project(N - 1, (T - 1) % 4, 5, parity(1))
                if runs(2):
                    weigh_values(N - 2, (T - 2) % 4, 3)
                if runs(3):
                    turn_mid(N - 3, (T - 3) % 4)
                if runs(1):
                    turn_chunk(N - 1, 2)
                if runs(2):
                    scores(N - 2, (T - 2) % 4, 7)
                    turn_probs(N - 2, (T - 2) % 4, 5)
                if runs(4):
                    mlp_down(N - 4, parity(4))
                if runs(1):
                    scores(N - 1, (T - 1) % 4, 0)
                if runs(3):
                    turn_mid_back(N - 3, (T - 3) % 4)
                if runs(1):
                    turn_chunk(N - 1, 3)

            pe.wait_ge(consts_set, N_CONSTS)
            slots(pe, slot)

        @block.scalar
        def _(act):
            def x_out(t, T):
                wait(act, pe_x, 1, t, 1)
                wait(act, proj_done, 6, t - 3, 6)
                act.copy(xshift[0:64, T * P:(T + 1) * P], bank_turn[0:64, 0:P])
                act.copy(xshift[64:P, T * P + 1:(T + 1) * P + 1], bank_turn[64:P, 0:P]).then_inc(x_turned, 1)

            def square(t, c):
                wait(act, rot_read, 4, t, c + 1)
                wait(act, ssq_done, 4, t, c - 1)
                act.activation(sq[:, c % 2, :], bank_proj[c % 2][:, :], ACT.Square).then_inc(sq_done, 1)

            def turned_out(t, T, c):
                wait(act, pe_turn, 4, t, c + 1)
                g = 4 * (c // 2)
                src = bank_turn[:, :].rearrange("p (g n) -> p g n", g=4)
                if c % 2 == 0:
                    wait(act, pe_s, 8, t - 3, 8)
                    act.copy(k_z[0:64, T, g:g + 4, 0, :], src[0:64])
                    act.copy(k_z[64:P, T, g:g + 4, 1, :], src[64:P]).then_inc(turned, 1)
                else:
                    wait(act, pe_s, 8, t - 2, 8)
                    act.copy(q_t[:, T % 2, g:g + 4, :], src).then_inc(turned, 1)

            def values_out(t, T, c):
                wait(act, proj_done, 6, t, 5 + c)
                wait(act, pe_pv, 8, t - 3, 8)
                act.copy(v_n[:, T, 512 * c:512 * c + 512], bank_proj[c][:, :]).then_inc(v_set, 1)

            def exponent(t, T, hp):
                wait(act, nbias_set, 8, t, hp + 1)
                wait(act, pe_pt, 8, t, hp - 3)
                lo = 0 if T > 0 else 32
                for j in range(2):
                    head = 2 * hp + j
                    last = act.activation(prob[:, hp % 4, j, 96 + lo:256], s_m[:, hp % 4, j, lo:160], ACT.Exp,
                                          bias=nbias[:, T, head:head + 1],
                                          scale=rnorm[:, T, 1 + 2 * (hp // 4), head % 8:head % 8 + 1],
                                          accum_out=psums[:, T, head:head + 1])
                last.then_inc(exp_done, 1)

            def probs_out(t, T, hp):
                wait(act, pe_pt, 8, t, hp + 1)
                wait(act, pe_pv, 8, t, hp - 1)
                if T > 0:
                    act.copy(p_t[:, hp % 2, :], bank_pt[:, 0:320]).then_inc(pt_set, 1)
                else:
                    act.copy(p_t[:, hp % 2, :].rearrange("p (h c) -> p h c", h=2)[:, :, 0:P],
                             bank_pt[:, 0:320].rearrange("p (h c) -> p h c", h=2)[:, :, 0:P]).then_inc(pt_set, 1)

            def heads_out(t, T, c):
                wait(act, pe_pv, 8, t, 4 * c + 4)
                wait(act, pe_wo, 1, t - 2, 1)
                act.copy(o_t[:, T % 2, 4 * c:4 * c + 4, :],
                         bank_o[:, :].rearrange("p (g n) -> p g n", g=4)).then_inc(o_set, 1)

            def mid_out(t, T):
                wait(act, pe_m, 1, t, 1)
                act.copy(mshift[0:64, T * P:(T + 1) * P], bank_misc[0:64, 0:P])
                act.copy(mshift[64:P, T * P + 1:(T + 1) * P + 1], bank_misc[64:P, 0:P]).then_inc(m_turned, 1)

            def xn_out(t, T, half):
                wait_apart(act, pe_xn, 1, t, 1)
                act.activation(xn_t[:, T % 2, :], bank_misc[:, 0:P], ACT.Identity,
                               bias=ln_gb[:, half, 1:2], scale=ln_gb[:, half, 0:1]).then_inc(xn_turned, 1)

            def gelu(t):
                wait(act, hid_read, 2, t, 1)
                act.activation(h_act[:, :], h_gate[:, :], ACT.Gelu).then_inc(gelu_done, 1)

            def h_out(t):
                wait(act, pe_h, 1, t, 1)
                act.copy(h_t[:, 0:2, :], bank_turn[:, 0:2 * P].rearrange("p (g n) -> p g n", g=2))
                act.copy(h_t[0:HID - 2 * P, 2, :], bank_turn[0:HID - 2 * P, 2 * P:3 * P]).then_inc(h_turned, 1)

            def slot(N, T, parity, row, runs):
                if runs(3):
                    probs_out(N - 3, (T - 3) % 4, 6)
                if runs(2):
                    exponent(N - 2, (T - 2) % 4, 0)
                    turned_out(N - 2, (T - 2) % 4, 3)
                if runs(3):
                    probs_out(N - 3, (T - 3) % 4, 7)
                if runs(1):
                    square(N - 1, 0)
                if runs(2):
                    exponent(N - 2, (T - 2) % 4, 1)
                if runs(4):
                    xn_out(N - 4, (T - 4) % 4, parity(4))
                if runs(1):
                    square(N - 1, 1)
                if runs(2):
                    probs_out(N - 2, (T - 2) % 4, 0)
                if runs(0):
                    x_out(N, T)
                if runs(2):
                    exponent(N - 2, (T - 2) % 4, 2)
                if runs(3):
                    heads_out(N - 3, (T - 3) % 4, 1)
                if runs(2):
                    probs_out(N - 2, (T - 2) % 4, 1)
                if runs(4):
                    gelu(N - 4)
                if runs(2):
                    exponent(N - 2, (T - 2) % 4, 3)
                if runs(1):
                    square(N - 1, 2)
                if runs(2):
                    probs_out(N - 2, (T - 2) % 4, 2)
                if runs(1):
                    turned_out(N - 1, (T - 1) % 4, 0)
                if runs(2):
                    exponent(N - 2, (T - 2) % 4, 4)
                if runs(1):
                    square(N - 1, 3)
                    turned_out(N - 1, (T - 1) % 4, 1)
                if runs(2):
                    probs_out(N - 2, (T - 2) % 4, 3)
                if runs(1):
                    values_out(N - 1, (T - 1) % 4, 0)
                if runs(2):
                    exponent(N - 2, (T - 2) % 4, 5)
                if runs(4):
                    h_out(N - 4)
                if runs(2):
                    probs_out(N - 2, (T - 2) % 4, 4)
                    exponent(N - 2, (T - 2) % 4, 6)
                if runs(3):
                    mid_out(N - 3, (T - 3) % 4)
                if runs(1):
                    turned_out(N - 1, (T - 1) % 4, 2)
                    values_out(N - 1, (T - 1) % 4, 1)
                if runs(2):
                    heads_out(N - 2, (T - 2) % 4, 0)
                    probs_out(N - 2, (T - 2) % 4, 5)
                    exponent(N - 2, (T - 2) % 4, 7)

            act.wait_ge(consts_set, N_CONSTS)
            slots(act, slot)

        @block.vector
        def _(dve):
            def rotate(t, T, c, table):
                wait(dve, proj_done, 6, t, c + 1)
                wait(dve, roped_set, 4, t, c - 1)
                kind = 0 if c % 2 else 2
                src = bank_proj[c % 2][:, :]
                cosine = table[:, kind, :].unsqueeze(1).broadcast_to([P, 8, HD])
                sine = table[:, kind + 1, :].rearrange("p (f d) -> p f d", f=2).unsqueeze(1).broadcast_to([P, 8, 2, HD // 2])
                dve.tensor_tensor(rot_c[:, c % 2, :].rearrange("p (h d) -> p h d", h=8),
                                  src.rearrange("p (h d) -> p h d", h=8), cosine, ALU.mult)
                dve.tensor_tensor(rot_s[:, c % 2, :].rearrange("p (h f d) -> p h f d", h=8, f=2),
                                  src.rearrange("p (h f d) -> p h f d", h=8, f=2)[:, :, ::-1, :], sine,
                                  ALU.mult).then_inc(rot_read, 1)

            def sum_squares(t, T, c):
                wait(dve, sq_done, 4, t, c + 1)
                dve.tensor_reduce(ssq[:, T, c, :], sq[:, c % 2, :].rearrange("p (h d) -> p h d", h=8),
                                  AX.X, ALU.add).then_inc(ssq_done, 1)

            def mask_max(t, T, hp):
                wait(dve, pe_s, 8, t, hp + 1)
                wait_apart(dve, exp_done, 8, t, hp - 3)
                lo = 0 if T > 0 else 32
                for j in range(2):
                    head = 2 * hp + j
                    last = dve.tensor_tensor_reduce(s_m[:, hp % 4, j, lo:160],
                                                    bank_s[hp % 2][:, 160 * j + lo:160 * j + 160], mask[:, lo:160],
                                                    1.0, LOWEST, ALU.add, ALU.max, smax[:, T, head:head + 1])
                last.then_inc(masked, 1)

            def reciprocal(t, T, hp):
                wait(dve, exp_done, 8, t, hp + 1)
                dve.reciprocal(prec[:, T, 2 * hp:2 * hp + 2], psums[:, T, 2 * hp:2 * hp + 2]).then_inc(prec_set, 1)

            def normalise(t, T, hp):
                wait(dve, prec_set, 8, t, hp + 1)
                lo = 96 if T > 0 else 128
                for j in range(2):
                    head = 2 * hp + j
                    p = prob[:, hp % 4, j, lo:256]
                    last = dve.tensor_scalar(p, p, prec[:, T, head:head + 1], None, ALU.mult)
                last.then_inc(normed, 1)

            def mid(t, T):
                wait(dve, pe_wo, 1, t, 1)
                dve.tensor_tensor(xmid[:, T, :], bank_misc[:, 0:DIM], xin[:, T, :], ALU.add).then_inc(xmid_set, 1)

            def mid_stats(t, T):
                wait(dve, pe_ms, 1, t, 1)
                dve.bn_stats(stats[:, T, :], bank_misc[:, 0:P]).then_inc(ln_stats, 1)
                wait_apart(dve, ln_stats, 2, t, 1)
                dve.bn_aggr(meanvar[:, T, :], stats[:, T, :]).then_inc(ln_stats, 1)

            def mid_norm(t, T):
                wait(dve, ln_rstd, 1, t, 1)
                dve.tensor_scalar(x_n[:, T % 2, :], bank_misc[:, 0:P], meanvar[:, T, 0:1], rstd[:, T, :],
                                  ALU.subtract, ALU.mult).then_inc(xn_set, 1)

            def hidden(t, c, half):
                out, col = ((h_gate, HID), (h_lin, 0))[c]
                wait(dve, pe_w1, 2, t, c + 1)
                dve.tensor_tensor(out[:, :], bank_proj[c][:, 0:HID], b_1[:, half, col:col + HID],
                                  ALU.add).then_inc(hid_read, 1)

            def finish(t, T, r):
                wait(dve, pe_w2, 1, t, 1)
                wait(dve, xmid_b_set, 1, t, 1)
                dve.tensor_tensor(xres[:, r * 4 + T, :], bank_misc[:, 0:DIM], xmid_b[:, T, :],
                                  ALU.add).then_inc(x_ready, 1)

            def slot(N, T, parity, row, runs):
                if runs(4):
                    mid_stats(N - 4, (T - 4) % 4)
                if runs(2):
                    mask_max(N - 2, (T - 2) % 4, 0)
                if runs(3):
                    reciprocal(N - 3, (T - 3) % 4, 7)
                if runs(1):
                    rotate(N - 1, (T - 1) % 4, 0, rot[:, (N - 1) // 16, (T - 1) % 4, :, :])
                if runs(3):
                    normalise(N - 3, (T - 3) % 4, 7)
                if runs(2):
                    mask_max(N - 2, (T - 2) % 4, 1)
                if runs(4):
                    mid_norm(N - 4, (T - 4) % 4)
                if runs(2):
                    reciprocal(N - 2, (T - 2) % 4, 0)
                    normalise(N - 2, (T - 2) % 4, 0)
                if runs(1):
                    rotate(N - 1, (T - 1) % 4, 1, rot[:, (N - 1) // 16, (T - 1) % 4, :, :])
                if runs(2):
                    mask_max(N - 2, (T - 2) % 4, 2)
                if runs(1):
                    sum_squares(N - 1, (T - 1) % 4, 0)
                if runs(2):
                    reciprocal(N - 2, (T - 2) % 4, 1)
                    normalise(N - 2, (T - 2) % 4, 1)
                if runs(4):
                    hidden(N - 4, 0, parity(4))
                if runs(1):
                    sum_squares(N - 1, (T - 1) % 4, 1)
                if runs(2):
                    reciprocal(N - 2, (T - 2) % 4, 2)
                    mask_max(N - 2, (T - 2) % 4, 3)
                if runs(4):
                    hidden(N - 4, 1, parity(4))
                if runs(2):
                    normalise(N - 2, (T - 2) % 4, 2)
                if runs(1):
                    rotate(N - 1, (T - 1) % 4, 2, rot[:, (N - 1) // 16, (T - 1) % 4, :, :])
                if runs(2):
                    mask_max(N - 2, (T - 2) % 4, 4)
                    reciprocal(N - 2, (T - 2) % 4, 3)
                if runs(1):
                    sum_squares(N - 1, (T - 1) % 4, 2)
                if runs(2):
                    normalise(N - 2, (T - 2) % 4, 3)
                if runs(1):
                    rotate(N - 1, (T - 1) % 4, 3, rot[:, (N - 1) // 16, (T - 1) % 4, :, :])
                if runs(2):
                    mask_max(N - 2, (T - 2) % 4, 5)
                if runs(1):
                    sum_squares(N - 1, (T - 1) % 4, 3)
                if runs(2):
                    reciprocal(N - 2, (T - 2) % 4, 4)
                    normalise(N - 2, (T - 2) % 4, 4)
                    mask_max(N - 2, (T - 2) % 4, 6)
                    reciprocal(N - 2, (T - 2) % 4, 5)
                    normalise(N - 2, (T - 2) % 4, 5)
                if runs(3):
                    mid(N - 3, (T - 3) % 4)
                if runs(2):
                    mask_max(N - 2, (T - 2) % 4, 7)
                    reciprocal(N - 2, (T - 2) % 4, 6)
                if runs(4):
                    finish(N - 4, (T - 4) % 4, row(4))
                if runs(2):
                    normalise(N - 2, (T - 2) % 4, 6)

            dve.memset(mhalf[:, :], -0.5).then_inc(consts_set, 1)
            dve.memset(k_z[0:64, :, :, 1, :], 0.0).then_inc(consts_set, 1)
            dve.memset(k_z[64:P, :, :, 0, :], 0.0).then_inc(consts_set, 1)
            dve.memset(prob[0:32, :, :, 0:96], 0.0).then_inc(consts_set, 1)
            dve.memset(xshift[64:P, 0:1], 0.0).then_inc(consts_set, 1)
            dve.memset(mshift[64:P, 0:1], 0.0).then_inc(consts_set, 1)
            for n in range(16):
                dve.bn_stats(stats[:, n, :], xo[:, n, :]).then_inc(x_stats, 1)
            dve.wait_ge(x_stats, 16)
            for n in range(16):
                dve.bn_aggr(meanvar[:, n, :], stats[:, n, :]).then_inc(x_stats, 1)
            dve.wait_ge(x_rstd, 1)
            for n in range(16):
                dve.tensor_scalar(xres[:, n, :], xo[:, n, :], meanvar[:, n, 0:1], rstd[:, n, :],
                                  ALU.subtract, ALU.mult).then_inc(x_ready, 1)
            slots(dve, slot)
            dve.wait_ge(x_ready, 16 + TILES)
            dve.tensor_tensor(xo[:, :, :], xo[:, :, :], xres[:, :, :], ALU.add)

        @block.gpsimd
        def _(pool):
            def link(t, c, ins):
                ins.then_inc(rope_chain, 1)
                wait_apart(pool, rope_chain, 10, t, c)

            def copy_in(t, T, r):
                wait_apart(pool, x_ready, 1, t, 1)
                pool.tensor_copy(xin[:, T, :], xres[:, r * 4 + T, :]).then_inc(xin_set, 1)

            def rope(t, T, c):
                wait(pool, rot_read, 4, t, c + 1)
                wait(pool, pe_turn, 4, t, c - 1)
                ins = pool.tensor_tensor(roped[:, c % 2, :], rot_c[:, c % 2, :], rot_s[:, c % 2, :], ALU.add)
                if c % 2:
                    ins.then_inc(roped_set, 1)
                else:
                    link(t, 1 if c == 0 else 6, ins)

            def norms(t, T, c):
                wait_apart(pool, ssq_done, 4, t, c + 1)
                n = (2, 4, 7, 9)[c]
                link(t, n, pool.tensor_scalar(ssq[:, T, c, :], ssq[:, T, c, :], 1e-24, 1.0 / 64 if c % 2 else 1.0,
                                              ALU.max, ALU.mult))
                ins = pool.tensor_tensor(rnorm[:, T, c, :], ssq[:, T, c, :], mhalf[:, 0:8], ALU.pow)
                link(t, n + 1, ins)
                if c % 2:
                    head = 8 * (c // 2)
                    pool.tensor_scalar(nrn8[:, T, head:head + 8], rnorm[:, T, c, :], -1.0, 1.0,
                                       ALU.mult, ALU.mult).then_inc(rn8_set, 1)
                else:
                    k = roped[:, c % 2, :].rearrange("p (h d) -> p h d", h=8)
                    pool.tensor_tensor(k, k, rnorm[:, T, c, :].unsqueeze(2).broadcast_to([P, 8, HD]),
                                       ALU.mult).then_inc(roped_set, 1)

            def biases(t, T, hp):
                wait(pool, masked, 8, t, hp + 1)
                wait(pool, rn8_set, 2, t, 1 + hp // 4)
                pool.tensor_tensor(nbias[:, T, 2 * hp:2 * hp + 2], smax[:, T, 2 * hp:2 * hp + 2],
                                   nrn8[:, T, 2 * hp:2 * hp + 2], ALU.mult).then_inc(nbias_set, 1)

            def mid_rstd(t, T):
                wait_apart(pool, ln_stats, 2, t, 2)
                pool.tensor_scalar(rstd[:, T, :], meanvar[:, T, 1:2], EPS, 1.0, ALU.add, ALU.mult).then_inc(ln_chain, 1)
                wait(pool, ln_chain, 1, t, 1)
                pool.tensor_tensor(rstd[:, T, :], rstd[:, T, :], mhalf[:, 0:1], ALU.pow).then_inc(ln_rstd, 1)

            def mid_bias(t, T, half):
                wait_apart(pool, xmid_set, 1, t, 1)
                pool.tensor_tensor(xmid_b[:, T, :], xmid[:, T, :], b_2[:, half, :], ALU.add).then_inc(xmid_b_set, 1)

            def gate(t):
                wait(pool, gelu_done, 1, t, 1)
                wait(pool, hid_read, 2, t, 2)
                pool.tensor_tensor(h[:, :], h_act[:, :], h_lin[:, :], ALU.mult).then_inc(h_set, 1)

            def slot(N, T, parity, row, runs):
                if runs(2):
                    biases(N - 2, (T - 2) % 4, 0)
                if runs(0):
                    copy_in(N, T, row(0))
                if runs(4):
                    mid_rstd(N - 4, (T - 4) % 4)
                if runs(1):
                    rope(N - 1, (T - 1) % 4, 0)
                if runs(2):
                    biases(N - 2, (T - 2) % 4, 1)
                    biases(N - 2, (T - 2) % 4, 2)
                if runs(1):
                    norms(N - 1, (T - 1) % 4, 0)
                if runs(2):
                    biases(N - 2, (T - 2) % 4, 3)
                if runs(1):
                    rope(N - 1, (T - 1) % 4, 1)
                if runs(4):
                    gate(N - 4)
                if runs(1):
                    norms(N - 1, (T - 1) % 4, 1)
                if runs(2):
                    biases(N - 2, (T - 2) % 4, 4)
                if runs(1):
                    rope(N - 1, (T - 1) % 4, 2)
                if runs(2):
                    biases(N - 2, (T - 2) % 4, 5)
                if runs(1):
                    norms(N - 1, (T - 1) % 4, 2)
                if runs(2):
                    biases(N - 2, (T - 2) % 4, 6)
                if runs(1):
                    rope(N - 1, (T - 1) % 4, 3)
                if runs(3):
                    mid_bias(N - 3, (T - 3) % 4, parity(3))
                if runs(2):
                    biases(N - 2, (T - 2) % 4, 7)
                if runs(1):
                    norms(N - 1, (T - 1) % 4, 3)

            pool.wait_ge(consts_set, N_CONSTS)
            pool.wait_ge(x_stats, 32)
            pool.tensor_scalar(rstd[:, :, 0], meanvar[:, :, 1], EPS, 1.0, ALU.add, ALU.mult).then_inc(x_var, 1)
            pool.wait_ge(x_var, 1)
            pool.tensor_tensor(rstd[:, :, 0], rstd[:, :, 0], mhalf[:, :], ALU.pow).then_inc(x_rstd, 1)
            slots(pool, slot)

MATS = ("maa1", "maa2", "r", "k", "v", "o", "gate1", "gate2", "wa1", "wa2", "k1", "k2", "ones", "mean")
VECS = ("maa_x", "maa0", "maa1", "maa2", "maa3", "decay", "faaaa", "aaaaa", "misc_a", "misc_k", "ln_w", "ln_b")
HS = 8
EPS_HEAD = 0.00064
CHUNK = 32


def mixer(nc, shared, ins):
    with ExitStack() as ctx:
        def sb(name, shape):
            return ctx.enter_context(nc.sbuf_tensor("mix_" + name, shape, F32))

        mats = sb("mats", [P, len(MATS), P])
        vecs = sb("vecs", [P, len(VECS)])
        kept = {n: sb("kept_" + n, [P, BATCH, SEQ]) for n in ("r", "wt", "k", "v", "kk", "b", "g")}
        mat = {n: mats[:, i, :] for i, n in enumerate(MATS)}
        vec = {n: vecs[:, i:i + 1] for i, n in enumerate(VECS)}
        mixer_inputs(nc, shared, ins, mats, vecs, mat, vec, kept)
        mixer_scan(nc, ins, kept)
        mixer_output(nc, shared, mat, vec, kept)


def chain_steps(ctx, nc, prefix, steps):
    where = {name: (nc_sem, i, len(names)) for nc_sem, names in (
        (ctx.enter_context(nc.semaphore(f"{prefix}_{engine}_steps")), names) for engine, names in steps.items())
        for i, name in enumerate(names)}

    def done(instruction, name):
        instruction.then_inc(where[name][0], 1)

    def need(engine, b, *names):
        for name in names:
            semaphore, i, each = where[name]
            engine.wait_ge(semaphore, b * each + (i + 1))

    return done, need


IN_STEPS = {
    "pe": ("pe_x", "pe_lo", "pe_log", "pe_r", "pe_gate1", "pe_wa1", "pe_k1", "pe_k", "pe_v", "pe_g", "pe_decay", "pe_a",
           "pe_ma", "pe_kkk", "pe_mk", "pe_ss"),
    "act": ("xc", "lo_t", "gate_t", "low_wa", "low_k", "r_out", "v_out", "g_out", "a", "ma", "mk", "ksq", "e", "ln1",
            "exp_w", "wt", "exp_wmk", "sqrt_ss"),
    "dve": ("x_n", "xx", "mix", "xm_part", "xm", "k0", "z", "nabs", "kk0", "z_min", "w", "w_mk", "a_rest", "k_factor",
            "k_part", "k_out", "ss", "inv_norm", "kk", "kkb_out"),
}
OUT_STEPS = {
    "pe": ("pe_mean", "pe_rk", "pe_var", "pe_out"),
    "act": ("ysq", "std"),
    "dve": ("rk", "yc", "bonus", "var", "inv_std", "normed", "scaled", "summed", "gated"),
}


def mixer_inputs(nc, shared, ins, mats, vecs, mat, vec, kept):
    x, ident = shared["x"], shared["ident"]
    with ExitStack() as ctx:
        def sb(name, shape):
            return ctx.enter_context(nc.sbuf_tensor("mixin_" + name, shape, F32))

        sems = {}

        def sem(name):
            if name not in sems:
                sems[name] = ctx.enter_context(nc.semaphore("mixin_" + name))
            return sems[name]

        mhalf = sb("mhalf", [P, 16])
        stats = sb("stats", [P, 16, 6])
        meanvar = sb("meanvar", [P, 16, 2])
        rstd = sb("rstd", [P, 16])
        x_n = sb("x_n", [P, 4, DIM])
        xc = sb("xc", [P, SEQ + 1])
        xx, mix, lo_t = (sb(n, [P, SEQ]) for n in ("xx", "mix", "lo_t"))
        xm = sb("xm", [P, 4, SEQ])
        gate_t, low_wa, low_k, k0, z, e, w, a, ma, mk = (
            sb(n, [P, SEQ]) for n in ("gate_t", "low_wa", "low_k", "k0", "z", "e", "w", "a", "ma", "mk"))
        nabs, ln1, kk0, ksq, knorm = (sb(n, [P, SEQ]) for n in ("nabs", "ln1", "kk0", "ksq", "knorm"))
        banks = [ctx.enter_context(nc.psum_tensor(f"mixin_bank{n}", [P, 512], F32)) for n in range(8)]

        done, need = chain_steps(ctx, nc, "mixin", IN_STEPS)
        row_free = sem("row_free")

        block = ctx.enter_context(nc.Block())

        @block.sync
        def _(sp):
            sp.dma_start(mats[:, :, :], ins["table_mix"]).then_inc(sem("loaded"), 16)
            sp.dma_start(vecs[:, :], ins["table_vec"]).then_inc(sem("loaded"), 16)

        @block.tensor
        def _(pe):
            pe.wait_ge(sem("loaded"), 32)
            with pe.Fori(0, BATCH) as b:
                pe.wait_ge(row_free, b + 1)
                need(pe, b, "x_n")
                for T in range(4):
                    last = pe.transpose(banks[0][:, T * P:(T + 1) * P], x_n[:, T, :], ident[:, :])
                done(last, "pe_x")

                def product(bank, m, rhs, name, rows=slice(0, P), *names):
                    need(pe, b, *names)
                    done(pe.matmul(banks[bank][:, :], mat[m][rows, :], rhs, start=True, stop=True), name)

                product(1, "maa1", mix[:, :], "pe_lo", slice(0, P), "mix")
                need(pe, b, "lo_t")
                for g in range(4):
                    rows = slice(32 * g, 32 * g + 32)
                    last = pe.matmul(banks[2 + g][:, :], mat["maa2"][rows, :], lo_t[rows, :], start=True, stop=True)
                done(last, "pe_log")
                everything = slice(0, P)
                product(0, "r", xm[:, 0, :], "pe_r", everything, "xm")
                product(1, "gate1", xm[:, 0, :], "pe_gate1")
                product(2, "wa1", xm[:, 1, :], "pe_wa1")
                product(3, "k1", xm[:, 2, :], "pe_k1")
                product(6, "k", xm[:, 2, :], "pe_k")
                product(7, "v", xm[:, 3, :], "pe_v")
                product(4, "gate2", gate_t[:, :], "pe_g", everything, "gate_t")
                product(5, "wa2", low_wa[0:64, :], "pe_decay", slice(0, 64), "low_wa")
                product(0, "wa2", low_wa[64:96, :], "pe_a", slice(64, 96), "r_out")
                product(1, "wa2", low_wa[96:128, :], "pe_ma", slice(96, 128))
                product(3, "k2", low_k[0:32, :], "pe_kkk", slice(0, 32), "low_k")
                product(2, "k2", low_k[32:64, :], "pe_mk", slice(32, 64))
                product(7, "ones", ksq[:, :], "pe_ss", everything, "ksq", "v_out")

        @block.scalar
        def _(act):
            with act.Fori(0, BATCH) as b:
                act.wait_ge(row_free, b + 1)
                need(act, b, "pe_x")
                done(act.copy(xc[:, 1:SEQ + 1], banks[0][:, :]), "xc")
                need(act, b, "pe_lo")
                done(act.activation(lo_t[:, :], banks[1][:, :], ACT.Tanh), "lo_t")
                need(act, b, "pe_gate1")
                done(act.activation(gate_t[:, :], banks[1][:, :], ACT.Tanh), "gate_t")
                need(act, b, "pe_wa1")
                act.activation(low_wa[0:64, :], banks[2][0:64, :], ACT.Tanh)
                done(act.copy(low_wa[64:P, :], banks[2][64:P, :]), "low_wa")
                need(act, b, "pe_k1")
                act.activation(low_k[0:32, :], banks[3][0:32, :], ACT.Tanh)
                done(act.copy(low_k[32:64, :], banks[3][32:64, :]), "low_k")
                need(act, b, "pe_r")
                done(act.copy(kept["r"][:, b, :], banks[0][:, :]), "r_out")
                need(act, b, "pe_v")
                done(act.copy(kept["v"][:, b, :], banks[7][:, :]), "v_out")
                need(act, b, "pe_g")
                done(act.copy(kept["g"][:, b, :], banks[4][:, :]), "g_out")
                for bank, out, v, name in ((0, a, "aaaaa", "a"), (1, ma, "misc_a", "ma"), (2, mk, "misc_k", "mk")):
                    need(act, b, "pe_" + name)
                    done(act.activation(out[:, :], banks[bank][:, :], ACT.Sigmoid, bias=vec[v]), name)
                need(act, b, "kk0")
                done(act.activation(ksq[:, :], kk0[:, :], ACT.Square), "ksq")
                need(act, b, "nabs")
                done(act.activation(e[:, :], nabs[:, :], ACT.Exp), "e")
                need(act, b, "e")
                done(act.activation(ln1[:, :], e[:, :], ACT.Ln, bias=1.0), "ln1")
                need(act, b, "w")
                done(act.activation(e[:, :], w[:, :], ACT.Exp), "exp_w")
                need(act, b, "exp_w")
                done(act.activation(kept["wt"][:, b, :], e[:, :], ACT.Exp, scale=-1.0), "wt")
                need(act, b, "w_mk")
                done(act.activation(mk[:, :], mk[:, :], ACT.Exp), "exp_wmk")
                need(act, b, "ss")
                done(act.activation(knorm[:, :], knorm[:, :], ACT.Sqrt), "sqrt_ss")

        @block.vector
        def _(dve):
            dve.memset(mhalf[:, :], -0.5).then_inc(sem("half"), 1)
            dve.memset(xc[:, 0:1], 0.0).then_inc(sem("half"), 1)
            for n in range(16):
                layernorm_rows(2 * n + 1, dve, stats, meanvar, x[:, n, :], n, sem("stats"))
            dve.wait_ge(sem("rstd"), 1)
            dve.wait_ge(sem("loaded"), 32)
            dve.memset(xx[:, 0:1], 0.0).then_inc(row_free, 1)
            dve.wait_ge(row_free, 1)
            with dve.Fori(0, BATCH) as b:
                def psum(bank):
                    return banks[bank][:, :]

                dve.wait_ge(row_free, b + 1)
                for T in range(4):
                    n = b * 4 + T
                    last = dve.tensor_scalar(x_n[:, T, :], x[:, n, :], meanvar[:, n, 0:1], rstd[:, bass.ds(n, 1)],
                                             ALU.subtract, ALU.mult)
                done(last, "x_n")
                need(dve, b, "xc")
                xt = xc[:, 1:SEQ + 1]
                done(dve.tensor_tensor(xx[:, :], xc[:, 0:SEQ], xt, ALU.subtract), "xx")
                need(dve, b, "xx")
                done(dve.scalar_tensor_tensor(mix[:, :], xx[:, :], vec["maa_x"], xt, ALU.mult, ALU.add), "mix")
                need(dve, b, "pe_log")
                for g in range(4):
                    last = dve.scalar_tensor_tensor(xm[:, g, :], psum(2 + g), vec[f"maa{g}"], xx[:, :],
                                                    ALU.add, ALU.mult)
                done(last, "xm_part")
                need(dve, b, "xm_part")
                done(dve.tensor_tensor(xm[:, :, :], xm[:, :, :], xt.unsqueeze(1).broadcast_to([P, 4, SEQ]), ALU.add),
                     "xm")
                need(dve, b, "pe_k")
                done(dve.tensor_copy(k0[:, :], psum(6)), "k0")
                need(dve, b, "pe_decay")
                done(dve.tensor_scalar(z[:, :], psum(5), vec["decay"], None, ALU.add), "z")
                need(dve, b, "z")
                done(dve.scalar_tensor_tensor(nabs[:, :], z[:, :], -1.0, z[:, :], ALU.mult, ALU.min), "nabs")
                need(dve, b, "pe_kkk", "k0")
                done(dve.tensor_tensor(kk0[:, :], psum(3), k0[:, :], ALU.add), "kk0")
                need(dve, b, "nabs")
                done(dve.tensor_scalar(z[:, :], z[:, :], 0.0, 0.5, ALU.min, ALU.subtract), "z_min")
                need(dve, b, "z_min", "ln1")
                done(dve.tensor_tensor(w[:, :], z[:, :], ln1[:, :], ALU.subtract), "w")
                need(dve, b, "w", "mk")
                done(dve.tensor_tensor(mk[:, :], mk[:, :], w[:, :], ALU.mult), "w_mk")
                need(dve, b, "a", "ma")
                done(dve.scalar_tensor_tensor(nabs[:, :], ma[:, :], 1.0, a[:, :], ALU.subtract, ALU.mult), "a_rest")
                need(dve, b, "a_rest")
                done(dve.tensor_tensor(ma[:, :], ma[:, :], nabs[:, :], ALU.subtract), "k_factor")
                need(dve, b, "k_factor")
                done(dve.tensor_tensor(k0[:, :], k0[:, :], ma[:, :], ALU.mult), "k_part")
                need(dve, b, "k_part", "exp_wmk")
                done(dve.tensor_tensor(kept["k"][:, b, :], k0[:, :], mk[:, :], ALU.mult), "k_out")
                need(dve, b, "pe_ss")
                done(dve.tensor_scalar(knorm[:, :], psum(7), 1e-24, None, ALU.max), "ss")
                need(dve, b, "sqrt_ss")
                done(dve.reciprocal(knorm[:, :], knorm[:, :]), "inv_norm")
                need(dve, b, "inv_norm")
                done(dve.tensor_tensor(kk0[:, :], kk0[:, :], knorm[:, :], ALU.mult), "kk")
                need(dve, b, "kk")
                dve.tensor_copy(kept["kk"][:, b, :], kk0[:, :])
                done(dve.scalar_tensor_tensor(kept["b"][:, b, :], kk0[:, :], -1.0, a[:, :], ALU.mult, ALU.mult),
                     "kkb_out")
                need(dve, b, "kkb_out", "wt", "g_out", "k_out")
                dve.memset(xx[:, 0:1], 0.0).then_inc(row_free, 1)

        @block.gpsimd
        def _(pool):
            pool.wait_ge(sem("stats"), 32)
            pool.wait_ge(sem("half"), 2)
            pool.tensor_scalar(rstd[:, :], meanvar[:, :, 1], EPS, 1.0, ALU.add, ALU.mult).then_inc(sem("var"), 1)
            pool.wait_ge(sem("var"), 1)
            pool.tensor_tensor(rstd[:, :], rstd[:, :], mhalf[:, :], ALU.pow).then_inc(sem("rstd"), 1)


def mixer_scan(nc, ins, kept):
    with ExitStack() as ctx:
        def sb(name, shape):
            return ctx.enter_context(nc.sbuf_tensor("scan_" + name, shape, F32))

        def sem(name):
            return ctx.enter_context(nc.semaphore("scan_" + name))

        names = ("kk", "wt", "b", "k", "r")
        per_bank = 512 // (BATCH * CHUNK)
        fills_each = HS // per_bank
        fills = len(names) * fills_each
        spread = sb("spread", [P, HS, P])
        wide = {n: sb("wide_" + n, [P, 2, HS, BATCH, CHUNK]) for n in names}
        states = sb("states", [P, 2, HS, BATCH, CHUNK + 1])
        s_kk, s_decayed, s_fed, s_rank = (sb(n, [P, HS, BATCH]) for n in ("s_kk", "s_decayed", "s_fed", "s_rank"))
        sa = sb("sa", [P, BATCH])
        banks = [ctx.enter_context(nc.psum_tensor(f"scan_bank{n}", [P, per_bank, BATCH, CHUNK], F32)) for n in range(4)]

        loaded = sem("loaded")
        pe_wide = sem("pe_wide")
        wide_set = sem("wide_set")
        vk_set = sem("vk_set")
        kk_used = sem("kk_used")
        decayed = sem("decayed")
        sa_set = sem("sa_set")
        fed = sem("fed")
        rank_one = sem("rank_one")
        state_set = sem("state_set")
        carried = sem("carried")
        r_used = sem("r_used")
        y_set = sem("y_set")

        block = ctx.enter_context(nc.Block())

        def chunks(eng, body):
            with eng.Fori(0, SEQ // CHUNK // 2) as pair:
                for parity in range(2):
                    body(pair * 2 + parity, parity)

        @block.sync
        def _(sp):
            sp.dma_start(spread[:, :, :], ins["table_spread"]).then_inc(loaded, 16)

        @block.tensor
        def _(pe):
            pe.wait_ge(loaded, 16)

            def spread_chunk(c, parity):
                for f in range(fills):
                    name, j = names[f // fills_each], f % fills_each * per_bank
                    bank = (parity * fills + f) % 4
                    pe.wait_ge(wide_set, c * fills + (f + 1))
                    for n in range(per_bank):
                        last = pe.matmul(banks[bank][:, n, :, :], spread[:, j + n, :],
                                         kept[name][:, :, bass.ds(c * CHUNK, CHUNK)], start=True, stop=True)
                    last.then_inc(pe_wide, 1)

            chunks(pe, spread_chunk)

        @block.scalar
        def _(act):
            act.sem_inc(wide_set, 4)

            def widen(c, parity):
                act.wait_ge(y_set, c + 1)
                for f in range(fills):
                    name, j = names[f // fills_each], f % fills_each * per_bank
                    bank = (parity * fills + f) % 4
                    act.wait_ge(pe_wide, c * fills + (f + 1))
                    act.copy(wide[name][:, parity, j:j + per_bank, :, :], banks[bank][:, :, :, :]).then_inc(wide_set, 1)

            chunks(act, widen)

        @block.vector
        def _(dve):
            dve.memset(states[:, 0, :, :, 0], 0.0).then_inc(state_set, 1)
            dve.wait_ge(state_set, 1)
            dve.sem_inc(carried, 1)

            def recur(c, parity):
                dve.wait_ge(vk_set, c + 1)
                dve.wait_ge(carried, c + 1)
                dve.wait_ge(wide_set, (c + 1) * fills + 4)
                for t in range(CHUNK):
                    n = c * CHUNK + (t + 1)

                    def at(name):
                        return wide[name][:, parity, :, :, t]

                    state = states[:, parity, :, :, t]
                    dve.wait_ge(state_set, n)
                    dve.tensor_tensor(s_kk[:, :, :], state, at("kk"), ALU.mult).then_inc(kk_used, 1)
                    dve.tensor_tensor(s_decayed[:, :, :], state, at("wt"), ALU.mult).then_inc(decayed, 1)
                    dve.wait_ge(kk_used, n)
                    dve.tensor_reduce(sa[:, :], s_kk[:, :, :].rearrange("p j b -> p b j"), AX.X, ALU.add
                                      ).then_inc(sa_set, 1)
                    dve.wait_ge(decayed, n)
                    dve.tensor_tensor(s_fed[:, :, :], s_decayed[:, :, :], at("k"), ALU.add).then_inc(fed, 1)
                    dve.wait_ge(sa_set, n)
                    dve.tensor_tensor(s_rank[:, :, :], sa[:, :].unsqueeze(1).broadcast_to([P, HS, BATCH]), at("b"),
                                      ALU.mult).then_inc(rank_one, 1)
                    dve.wait_ge(rank_one, n)
                    dve.tensor_tensor(states[:, parity, :, :, t + 1], s_fed[:, :, :], s_rank[:, :, :], ALU.add
                                      ).then_inc(state_set, 1)
                dve.wait_ge(state_set, (c + 1) * CHUNK + 1)
                dve.wait_ge(y_set, c + 2)
                dve.tensor_copy(states[:, 1 - parity, :, :, 0], states[:, parity, :, :, CHUNK]).then_inc(carried, 1)

            chunks(dve, recur)

        @block.gpsimd
        def _(pool):
            def feed(c, parity):
                pool.wait_ge(wide_set, c * fills + (fills_each * (names.index("k") + 1) + 4))
                k = wide["k"][:, parity, :, :, :]
                v = kept["v"][:, :, bass.ds(c * CHUNK, CHUNK)].unsqueeze(1).broadcast_to([P, HS, BATCH, CHUNK])
                pool.tensor_tensor(k, k, v, ALU.mult).then_inc(vk_set, 1)

            def read_out(c, parity):
                pool.wait_ge(carried, c + 2)
                r = wide["r"][:, parity, :, :, :]
                pool.tensor_tensor(r, r, states[:, parity, :, :, 1:CHUNK + 1], ALU.mult).then_inc(r_used, 1)
                for n, half in enumerate((4, 2)):
                    pool.wait_ge(r_used, c * 3 + (n + 1))
                    pool.tensor_tensor(r[:, 0:half], r[:, 0:half], r[:, half:2 * half], ALU.add).then_inc(r_used, 1)
                pool.wait_ge(r_used, c * 3 + 3)
                pool.tensor_tensor(kept["kk"][:, :, bass.ds(c * CHUNK, CHUNK)], r[:, 0], r[:, 1], ALU.add
                                   ).then_inc(y_set, 1)

            pool.sem_inc(y_set, 2)
            last = SEQ // CHUNK - 1
            feed(0, 0)
            with pool.Fori(0, last // 2) as pair:
                for parity in range(2):
                    feed(pair * 2 + parity + 1, 1 - parity)
                    read_out(pair * 2 + parity, parity)
            feed(last, 1)
            read_out(last - 1, 0)
            read_out(last, 1)


def mixer_output(nc, shared, mat, vec, kept):
    x = shared["x"]
    with ExitStack() as ctx:
        def sb(name):
            return ctx.enter_context(nc.sbuf_tensor("mixout_" + name, [P, SEQ], F32))

        yc, ysq, ystd, rk, out = (sb(n) for n in ("yc", "ysq", "ystd", "rk", "out"))
        banks = [ctx.enter_context(nc.psum_tensor(f"mixout_bank{n}", [P, 512], F32)) for n in range(4)]

        done, need = chain_steps(ctx, nc, "mixout", OUT_STEPS)
        row_free = ctx.enter_context(nc.semaphore("mixout_row_free"))

        block = ctx.enter_context(nc.Block())

        @block.tensor
        def _(pe):
            with pe.Fori(0, BATCH) as b:
                pe.wait_ge(row_free, b + 1)
                done(pe.matmul(banks[0][:, :], mat["mean"], kept["kk"][:, b, :], start=True, stop=True), "pe_mean")
                need(pe, b, "rk")
                done(pe.matmul(banks[1][:, :], mat["ones"], rk[:, :], start=True, stop=True), "pe_rk")
                need(pe, b, "ysq")
                done(pe.matmul(banks[2][:, :], mat["mean"], ysq[:, :], start=True, stop=True), "pe_var")
                need(pe, b, "gated")
                for T in range(4):
                    last = pe.matmul(banks[3][:, T * P:(T + 1) * P], out[:, T * P:(T + 1) * P], mat["o"],
                                     start=True, stop=True)
                done(last, "pe_out")

        @block.scalar
        def _(act):
            with act.Fori(0, BATCH) as b:
                need(act, b, "yc")
                done(act.activation(ysq[:, :], yc[:, :], ACT.Square), "ysq")
                need(act, b, "var")
                done(act.activation(ystd[:, :], ystd[:, :], ACT.Sqrt), "std")

        @block.vector
        def _(dve):
            dve.memset(out[:, 0:1], 0.0).then_inc(row_free, 1)
            dve.wait_ge(row_free, 1)
            with dve.Fori(0, BATCH) as b:
                dve.wait_ge(row_free, b + 1)
                done(dve.scalar_tensor_tensor(rk[:, :], kept["r"][:, b, :], vec["faaaa"], kept["k"][:, b, :],
                                              ALU.mult, ALU.mult), "rk")
                need(dve, b, "pe_mean")
                done(dve.tensor_tensor(yc[:, :], kept["kk"][:, b, :], banks[0][:, :], ALU.subtract), "yc")
                need(dve, b, "pe_rk")
                done(dve.tensor_tensor(out[:, :], banks[1][:, :], kept["v"][:, b, :], ALU.mult), "bonus")
                need(dve, b, "pe_var")
                done(dve.tensor_scalar(ystd[:, :], banks[2][:, :], EPS_HEAD, None, ALU.add), "var")
                need(dve, b, "std")
                done(dve.reciprocal(ystd[:, :], ystd[:, :]), "inv_std")
                need(dve, b, "inv_std")
                done(dve.tensor_tensor(yc[:, :], yc[:, :], ystd[:, :], ALU.mult), "normed")
                need(dve, b, "normed")
                done(dve.tensor_scalar(yc[:, :], yc[:, :], vec["ln_w"], vec["ln_b"], ALU.mult, ALU.add), "scaled")
                need(dve, b, "scaled", "bonus")
                done(dve.tensor_tensor(yc[:, :], yc[:, :], out[:, :], ALU.add), "summed")
                need(dve, b, "summed")
                done(dve.tensor_tensor(out[:, :], yc[:, :], kept["g"][:, b, :], ALU.mult), "gated")
                need(dve, b, "pe_out")
                rows = x[:, bass.ds(b * 4, 4), :]
                dve.tensor_tensor(rows, banks[3][:, :].rearrange("p (t d) -> p t d", t=4), rows, ALU.add
                                  ).then_inc(row_free, 1)


def setup(nc, shared, x_dram, tables, scales):
    with ExitStack() as ctx:
        base = ctx.enter_context(nc.sbuf_tensor("rot_base", [P, 4, 4, HD], F32))
        qk_scale = ctx.enter_context(nc.sbuf_tensor("qk_scale", [P, 2, DEPTH, HD], F32))
        loaded = ctx.enter_context(nc.semaphore("setup_loaded"))
        block = ctx.enter_context(nc.Block())

        @block.sync
        def _(sp):
            for b in range(BATCH):
                sp.dma_start(shared["x"][:, 4 * b:4 * b + 4, :], x_dram[b].rearrange("(t p) d -> p t d", p=P)
                             ).then_inc(loaded, 16)
            sp.dma_start(shared["ident"][:, :], tables["ident"]).then_inc(loaded, 16)
            sp.dma_start(shared["mask"][:, :], tables["mask"]).then_inc(loaded, 16)
            sp.dma_start(base[:, :, :, :], tables["rot"]).then_inc(loaded, 16)
            for n in range(2):
                sp.dma_start(qk_scale[:, n, :, :], scales[n].partition_broadcast(P)).then_inc(loaded, 16)

        @block.vector
        def _(dve):
            dve.wait_ge(loaded, 16 * 9)
            for layer in range(DEPTH):
                for kind in range(4):
                    s = qk_scale[:, kind // 2, layer, :].rearrange("p (f d) -> p f d", f=2)
                    if kind % 2:
                        s = s[:, ::-1, :]
                    dve.tensor_tensor(shared["rot"][:, layer, :, kind, :].rearrange("p t (f d) -> p t f d", f=2),
                                      base[:, :, kind, :].rearrange("p t (f d) -> p t f d", f=2),
                                      s.unsqueeze(1).broadcast_to([P, 4, 2, HD // 2]), ALU.mult)


def store(nc, shared, out):
    with ExitStack() as ctx:
        stored = ctx.enter_context(nc.semaphore("stored"))
        block = ctx.enter_context(nc.Block())

        @block.sync
        def _(sp):
            for b in range(BATCH):
                sp.dma_start(out[b].rearrange("(t p) d -> p t d", p=P), shared["x"][:, 4 * b:4 * b + 4, :]
                             ).then_inc(stored, 16)
            sp.wait_ge(stored, 16 * BATCH)


def program(nc, ins, out, phases=("retention", "stack0", "mixer", "stack1")):
    with ExitStack() as ctx:
        def sb(name, shape):
            return ctx.enter_context(nc.sbuf_tensor(name, shape, F32))

        shared = {
            "x": sb("x_outer", [P, 16, DIM]),
            "ident": sb("ident", [P, P]),
            "mask": sb("band", [P, 160]),
            "rot": sb("rot_tables", [P, DEPTH, 4, 4, HD]),
        }
        tables = {k: ins["table_" + k] for k in ("ident", "mask", "rot")}
        setup(nc, shared, ins["L0_attn_a_X"], tables, (ins["L0_ffn_q_scale"], ins["L0_ffn_k_scale"]))
        stack_weights = {k: ins["L0_ffn_" + k] for k in ("Wqkv", "Wo", "W1", "W2", "b1", "b2", "ln_g", "ln_b")}
        for phase in phases:
            if phase == "retention":
                retention(nc, shared, ins)
            elif phase == "mixer":
                mixer(nc, shared, ins)
            else:
                ffn_stack(nc, {**shared, "tag": phase + "_"}, stack_weights)
        store(nc, shared, out)


def shape_tables():
    f = np.float32
    t = {"ident": np.eye(P, dtype=f)}
    ahead = np.arange(P)[:, None] - (np.arange(P + WINDOW)[None, :] - WINDOW)
    t["mask"] = np.where((ahead >= 0) & (ahead <= WINDOW), f(0), f(-1e30)).astype(f)
    pos = np.arange(SEQ, dtype=f)
    half = np.arange(0, HD, 2, dtype=f)
    freq = (f(1.0) / np.power(f(10000.0), half / f(HD))).astype(f)
    angle = (pos[:, None] * freq[None, :]).astype(f)
    scale = np.power(((half + f(0.4 * HD)) / f(1.4 * HD)).astype(f)[None, :],
                     ((pos - f(SEQ // 2)) / f(WINDOW // 2)).astype(f)[:, None]).astype(f)
    cos, sin = (np.concatenate([g(angle.astype(np.float64))] * 2, -1).astype(f) for g in (np.cos, np.sin))
    scale = np.concatenate([scale, scale], -1)
    sin = sin * np.where(np.arange(HD) < HD // 2, f(-1), f(1))
    kinds = np.stack([cos * scale, sin * scale, cos / scale, sin / scale], 1).astype(f)
    t["rot"] = np.ascontiguousarray(kinds.reshape(4, P, 4, HD).transpose(1, 0, 2, 3))
    half = DIM // 2
    power = pos / f(SEQ)
    scale = np.power(((np.arange(0, DIM, 2, dtype=f) + f(0.4 * DIM)) / f(1.4 * DIM)).astype(f)[None, :],
                     power[:, None]).astype(f)
    freq = (f(1.0) / np.power(f(10000.0), (np.arange(half, dtype=f) / f(half)))).astype(f)
    angle = (pos[:, None] * freq[None, :]).astype(f).astype(np.float64)
    rows = []
    for g in (np.cos, np.sin):
        both = [np.repeat((g(angle).astype(f) * sc).astype(f), 2, -1) for sc in (scale, f(1.0) / scale)]
        rows.append(np.concatenate(both, -1))
    rows[1] = rows[1] * np.where(np.arange(2 * DIM) % 2 == 0, f(-1), f(1))
    t["xpos"] = np.ascontiguousarray(np.stack(rows, 1).reshape(4, P, 2, 2 * DIM).transpose(1, 0, 2, 3)).astype(f)
    offset = np.abs(np.arange(P)[:, None] - np.arange(7 * P)[None, :] + 3 * P)
    t["decay"] = np.power(f(0.9), offset.astype(f)).astype(f)
    head, item = np.arange(P) // HS, np.arange(P) % HS
    same = head[:, None] == head[None, :]
    t["ones"] = same.astype(f)
    t["mean"] = (same / HS).astype(f)
    t["spread"] = np.stack([same & (item[:, None] == i) for i in range(HS)], 1).astype(f)
    t["gather"] = np.stack([same & (item[None, :] == i) for i in range(HS)], 1).astype(f)
    return t


def arrange(inputs):
    f = np.float32
    got = {k: np.asarray(v) for k, v in inputs.items()}
    mixer_in = {k[len("L0_attn_b_"):]: got[k] for k in got if k.startswith("L0_attn_b_")}
    ins = {k: v for k, v in got.items() if not k.startswith("L0_attn_b_")}
    t = shape_tables()

    def placed(parts, by_column):
        m = np.zeros((P, P), f)
        for at, part in parts:
            if by_column:
                m[:, at:at + part.shape[1]] = part
            else:
                m[at:at + part.shape[0], :] = part
        return m

    w = mixer_in
    mats = {
        "maa1": w["maa_w1"].T, "maa2": w["maa_w2"].reshape(P, P),
        "r": w["Wr"].T, "k": w["Wk"].T, "v": w["Wv"].T, "o": w["Wo"].T,
        "gate1": w["gate_w1"].T, "gate2": w["gate_w2"],
        "wa1": placed(((0, w["decay_w1"].T), (64, w["aaa_w1"].T), (96, w["ma_w1"].T)), True),
        "wa2": placed(((0, w["decay_w2"]), (64, w["aaa_w2"]), (96, w["ma_w2"])), False),
        "k1": placed(((0, w["kkk_w1"].T), (32, w["mk_w1"].T)), True),
        "k2": placed(((0, w["kkk_w2"]), (32, w["mk_w2"])), False),
        "ones": t.pop("ones"), "mean": t.pop("mean"),
    }
    vecs = {
        "maa_x": w["time_maa_x"], **{f"maa{g}": w["time_maa"][g, 0, 0] for g in range(4)},
        "decay": w["time_decay"], "faaaa": w["time_faaaa"], "aaaaa": w["time_aaaaa"],
        "misc_a": w["time_misc_a"], "misc_k": w["time_misc_k"], "ln_w": w["ln_w"], "ln_b": w["ln_b"],
    }
    t["mix"] = np.stack([mats[n] for n in MATS], 1)
    t["vec"] = np.stack([vecs[n] for n in VECS], 1)
    ins.update({"table_" + k: np.ascontiguousarray(v) for k, v in t.items()})
    return ins


def kernel(**inputs):
    import concourse.bacc as bacc
    from concourse.bass_utils import run_bass_kernel_spmd

    nc = bacc.Bacc("TRN2", target_bir_lowering=False, num_devices=1)
    arrays = arrange(inputs)
    ins = {k: nc.dram_tensor(k, v.shape, mybir.dt.from_np(v.dtype), kind="ExternalInput").ap()
           for k, v in arrays.items()}
    out = nc.dram_tensor("out", (BATCH, SEQ, DIM), F32, kind="ExternalOutput").ap()
    program(nc, ins, out)
    return run_bass_kernel_spmd(nc, [arrays], core_ids=[0]).results[0]["out"]
```

```python
from contextlib import ExitStack

import numpy as np

import concourse.bass as bass
from concourse import mybir

F32 = mybir.dt.float32
ALU = mybir.AluOpType
ACT = mybir.ActivationFunctionType
AX = mybir.AxisListType

P = 128
DIM = 128
BATCH, SEQ = 4, 512
EPS = 1e-5
LOWEST = -3.0e38
DEPTH, HEADS, HD, WINDOW = 6, 16, 64, 32
INNER = HEADS * HD
PAIRS = HEADS // 2
HID = DIM * 4 * 2 // 3
TILES = DEPTH * BATCH * SEQ // P
N_LOADS = 9
N_CONSTS = 7




def layernorm_rows(eng_wait, dve, stats, meanvar, src, n, stats_sem):
    dve.bn_stats(stats[:, n, :], src).then_inc(stats_sem, 1)
    dve.wait_ge(stats_sem, eng_wait)
    dve.bn_aggr(meanvar[:, n, :], stats[:, n, :]).then_inc(stats_sem, 1)


def retention(nc, shared, ins):
    x, ident = shared["x"], shared["ident"]
    with ExitStack() as ctx:
        def sb(name, shape):
            return ctx.enter_context(nc.sbuf_tensor("ret_" + name, shape, F32))

        def ps(name):
            return ctx.enter_context(nc.psum_tensor("ret_" + name, [P, 512], F32))

        def sem(name):
            return ctx.enter_context(nc.semaphore("ret_" + name))

        w_qkv = sb("w_qkv", [P, 3 * DIM])
        xpos = sb("xpos", [P, 4, 2, 2 * DIM])
        decay = sb("decay", [P, 7 * P])
        mhalf = sb("mhalf", [P, 16])
        stats = sb("stats", [P, 16, 6])
        meanvar = sb("meanvar", [P, 16, 2])
        rstd = sb("rstd", [P, 16])
        x_n = sb("x_n", [P, 4, DIM])
        xn_t = sb("xn_t", [P, 4, P])
        cosined = sb("cosined", [P, 4, 2 * DIM])
        sined = sb("sined", [P, 4, 2 * DIM])
        q_k = sb("q_k", [P, 4, 2 * DIM])
        v = sb("v", [P, 3, 4, DIM])
        q_t = sb("q_t", [P, 2, 4, P])
        k_t = sb("k_t", [P, 2, 4, P])
        row_max = sb("row_max", [P, 4])
        neg_max = sb("neg_max", [P, 4])
        row_sum = sb("row_sum", [P, 4])
        inv_sum = sb("inv_sum", [P, 4])
        e = sb("e", [P, 2, SEQ])
        prob = sb("prob", [P, 2, SEQ])
        p_t = sb("p_t", [P, 2, SEQ])

        bank_x = ps("bank_x")
        bank_qkv = [ps("bank_qkv0"), ps("bank_qkv1")]
        bank_turn = ps("bank_turn")
        bank_s = [ps("bank_s0"), ps("bank_s1")]
        bank_pt = ps("bank_pt")
        bank_o = ps("bank_o")

        loaded = sem("loaded")
        stats_set = sem("stats_set")
        var_set = sem("var_set")
        rstd_set = sem("rstd_set")
        xn_set = sem("xn_set")
        pe_xn = sem("pe_xn")
        xn_turned = sem("xn_turned")
        pe_qkv = sem("pe_qkv")
        v_set = sem("v_set")
        rotated = sem("rotated")
        qk_set = sem("qk_set")
        pe_qk = sem("pe_qk")
        qk_turned = sem("qk_turned")
        pe_s = sem("pe_s")
        max_set = sem("max_set")
        e_set = sem("e_set")
        inv_set = sem("inv_set")
        prob_set = sem("prob_set")
        pe_pt = sem("pe_pt")
        pt_set = sem("pt_set")
        pe_o = sem("pe_o")
        x_set = sem("x_set")

        block = ctx.enter_context(nc.Block())

        @block.sync
        def _(sp):
            for n, name in enumerate(("W_Q", "W_K", "W_V")):
                sp.dma_start(w_qkv[:, n * DIM:(n + 1) * DIM], ins["L0_attn_a_" + name]).then_inc(loaded, 16)
            sp.dma_start(xpos[:, :, :, :], ins["table_xpos"]).then_inc(loaded, 16)
            sp.dma_start(decay[:, :], ins["table_decay"]).then_inc(loaded, 16)

        @block.tensor
        def _(pe):
            pe.wait_ge(loaded, 16 * 5)

            def project(n):
                T = n % 4
                pe.wait_ge(xn_set, n + 1)
                if n:
                    pe.wait_ge(xn_turned, n)
                pe.transpose(bank_x[:, 0:P], x_n[:, T, :], ident[:, :]).then_inc(pe_xn, 1)
                pe.wait_ge(xn_turned, n + 1)
                if n >= 2:
                    pe.wait_ge(v_set, n - 1)
                pe.matmul(bank_qkv[n % 2][:, 0:3 * DIM], xn_t[:, T, :], w_qkv[:, :],
                          start=True, stop=True).then_inc(pe_qkv, 1)

            def turn(n):
                T = n % 4
                pe.wait_ge(qk_set, n + 1)
                if n:
                    pe.wait_ge(qk_turned, n)
                pe.transpose(bank_turn[:, 0:P], q_k[:, T, 0:P], ident[:, :])
                pe.transpose(bank_turn[:, P:2 * P], q_k[:, T, P:2 * P], ident[:, :]).then_inc(pe_qk, 1)

            def scores(n):
                b, T = n // 4 % 2, n % 4
                pe.wait_ge(qk_turned, n - T + 4)
                if n >= 2:
                    pe.wait_ge(e_set, n - 1)
                pe.matmul(bank_s[n % 2][:, :], q_t[:, b, T, :], k_t[:, b, :, :], start=True, stop=True
                          ).then_inc(pe_s, 1)

            def attend(n):
                pe.wait_ge(prob_set, n + 1)
                if n:
                    pe.wait_ge(pt_set, n)
                for j in range(4):
                    last = pe.transpose(bank_pt[:, j * P:(j + 1) * P], prob[:, n % 2, j * P:(j + 1) * P], ident[:, :])
                last.then_inc(pe_pt, 1)
                pe.wait_ge(pt_set, n + 1)
                if n:
                    pe.wait_ge(x_set, n)
                for j in range(4):
                    last = pe.matmul(bank_o[:, 0:DIM], p_t[:, n % 2, j * P:(j + 1) * P], v[:, n // 4 % 3, j, :],
                                     start=j == 0, stop=j == 3)
                last.then_inc(pe_o, 1)

            for n in range(4 * BATCH + 6):
                if n < 4 * BATCH:
                    project(n)
                if 1 <= n <= 4 * BATCH:
                    turn(n - 1)
                if 4 <= n < 4 * BATCH + 4:
                    scores(n - 4)
                if 5 <= n < 4 * BATCH + 5:
                    attend(n - 5)

        @block.scalar
        def _(act):
            for n in range(4 * BATCH + 6):
                if n < 4 * BATCH:
                    T, b = n % 4, n // 4 % 2
                    act.wait_ge(pe_xn, n + 1)
                    act.copy(xn_t[:, T, :], bank_x[:, 0:P]).then_inc(xn_turned, 1)
                    act.wait_ge(rotated, n + 1)
                    if n >= 12:
                        act.wait_ge(pe_o, n - n % 4 - 8)
                    act.copy(v[:, n // 4 % 3, T, :], bank_qkv[n % 2][:, 2 * DIM:3 * DIM]).then_inc(v_set, 1)
                if 1 <= n <= 4 * BATCH:
                    m = n - 1
                    act.wait_ge(pe_qk, m + 1)
                    act.copy(q_t[:, m // 4 % 2, m % 4, :], bank_turn[:, 0:P])
                    act.copy(k_t[:, m // 4 % 2, m % 4, :], bank_turn[:, P:2 * P]).then_inc(qk_turned, 1)
                if 4 <= n < 4 * BATCH + 4:
                    m = n - 4
                    act.wait_ge(max_set, 2 * m + 2)
                    if m >= 2:
                        act.wait_ge(prob_set, m - 1)
                    act.activation(e[:, m % 2, :], bank_s[m % 2][:, :], ACT.Exp, bias=neg_max[:, m % 4:m % 4 + 1],
                                   accum_out=row_sum[:, m % 4:m % 4 + 1]).then_inc(e_set, 1)
                if 5 <= n < 4 * BATCH + 5:
                    m = n - 5
                    act.wait_ge(pe_pt, m + 1)
                    if m >= 2:
                        act.wait_ge(pe_o, m - 1)
                    act.copy(p_t[:, m % 2, :], bank_pt[:, :]).then_inc(pt_set, 1)

        @block.vector
        def _(dve):
            dve.memset(mhalf[:, :], -0.5).then_inc(stats_set, 1)
            for n in range(16):
                layernorm_rows(2 * n + 2, dve, stats, meanvar, x[:, n, :], n, stats_set)
            dve.wait_ge(rstd_set, 1)
            dve.wait_ge(loaded, 16 * 5)
            for n in range(4 * BATCH + 6):
                if n < 4 * BATCH:
                    T = n % 4
                    if n >= 4:
                        dve.wait_ge(pe_xn, n - 3)
                    dve.tensor_scalar(x_n[:, T, :], x[:, n, :], meanvar[:, n, 0:1], rstd[:, n:n + 1],
                                      ALU.subtract, ALU.mult).then_inc(xn_set, 1)
                    dve.wait_ge(pe_qkv, n + 1)
                    if n >= 4:
                        dve.wait_ge(qk_set, n - 3)
                    src = bank_qkv[n % 2][:, 0:2 * DIM]
                    dve.tensor_tensor(cosined[:, T, :], src, xpos[:, T, 0, :], ALU.mult)
                    dve.tensor_tensor(sined[:, T, :].rearrange("p (n f) -> p n f", f=2),
                                      src.rearrange("p (n f) -> p n f", f=2)[:, :, ::-1],
                                      xpos[:, T, 1, :].rearrange("p (n f) -> p n f", f=2),
                                      ALU.mult).then_inc(rotated, 1)
                if 4 <= n < 4 * BATCH + 4:
                    m = n - 4
                    c = m % 4
                    dve.wait_ge(pe_s, m + 1)
                    dve.tensor_reduce(row_max[:, c:c + 1], bank_s[m % 2][:, :], AX.X, ALU.max).then_inc(max_set, 1)
                    dve.wait_ge(max_set, 2 * m + 1)
                    dve.tensor_scalar(neg_max[:, c:c + 1], row_max[:, c:c + 1], -1.0, None, ALU.mult
                                      ).then_inc(max_set, 1)
                    dve.wait_ge(e_set, m + 1)
                    dve.reciprocal(inv_sum[:, c:c + 1], row_sum[:, c:c + 1]).then_inc(inv_set, 1)
                    dve.wait_ge(inv_set, m + 1)
                    if m >= 2:
                        dve.wait_ge(pe_pt, m - 1)
                    d = (3 - m % 4) * P
                    dve.scalar_tensor_tensor(prob[:, m % 2, :], e[:, m % 2, :], inv_sum[:, c:c + 1],
                                             decay[:, d:d + SEQ], ALU.mult, ALU.mult).then_inc(prob_set, 1)
                if 5 <= n < 4 * BATCH + 5:
                    m = n - 5
                    dve.wait_ge(pe_o, m + 1)
                    dve.tensor_tensor(x[:, m, :], bank_o[:, 0:DIM], x[:, m, :], ALU.add).then_inc(x_set, 1)

        @block.gpsimd
        def _(pool):
            pool.wait_ge(stats_set, 33)
            pool.tensor_scalar(rstd[:, :], meanvar[:, :, 1], EPS, 1.0, ALU.add, ALU.mult).then_inc(var_set, 1)
            pool.wait_ge(var_set, 1)
            pool.tensor_tensor(rstd[:, :], rstd[:, :], mhalf[:, :], ALU.pow).then_inc(rstd_set, 1)
            for n in range(4 * BATCH):
                T = n % 4
                pool.wait_ge(rotated, n + 1)
                if n >= 4:
                    pool.wait_ge(pe_qk, n - 3)
                pool.tensor_tensor(q_k[:, T, :], cosined[:, T, :], sined[:, T, :], ALU.add).then_inc(qk_set, 1)
def ffn_stack(nc, shared, w):
    xo, ident, rot, mask = shared["x"], shared["ident"], shared["rot"], shared["mask"]
    with ExitStack() as ctx:
        def sb(name, shape):
            return ctx.enter_context(nc.sbuf_tensor(shared["tag"] + name, shape, F32))

        def ps(name):
            return ctx.enter_context(nc.psum_tensor(shared["tag"] + name, [P, 512], F32))

        def sem(name):
            return ctx.enter_context(nc.semaphore(shared["tag"] + name))

        w_qkv = sb("w_qkv", [P, 2, 3 * INNER])
        w_v = sb("w_v", [P, 2, PAIRS, HD])
        w_o = sb("w_o", [P, 2, PAIRS, DIM])
        w_1 = sb("w_1", [P, 2, 2 * HID])
        w_2 = sb("w_2", [P, 2, 3, DIM])
        b_1 = sb("b_1", [P, 2, 2 * HID])
        b_2 = sb("b_2", [P, 2, DIM])
        ln_gb = sb("ln_gb", [P, 2, 2])
        xres = sb("xres", [P, 16, DIM])
        xin = sb("xin", [P, 4, DIM])
        xmid = sb("xmid", [P, 4, DIM])
        xmid_b = sb("xmid_b", [P, 4, DIM])
        xshift = sb("xshift", [P, 4 * P + 1])
        mshift = sb("mshift", [P, 4 * P + 1])
        sq = sb("sq", [P, 2, 512])
        rot_c = sb("rot_c", [P, 2, 512])
        rot_s = sb("rot_s", [P, 2, 512])
        roped = sb("roped", [P, 2, 512])
        ssq = sb("ssq", [P, 4, 4, 8])
        rnorm = sb("rnorm", [P, 4, 4, 8])
        nrn8 = sb("nrn8", [P, 4, HEADS])
        q_t = sb("q_t", [P, 2, PAIRS, P])
        k_z = sb("k_z", [P, 2, PAIRS, 2, P])
        v_w = sb("v_w", [P, 2, 4, PAIRS, 2, HD])
        s_m = sb("s_m", [P, 4, 2, 2 * WINDOW])
        prob = sb("prob", [P, 4, 2, 2 * WINDOW])
        smax = sb("smax", [P, 4, HEADS])
        nbias = sb("nbias", [P, 4, HEADS])
        psums = sb("psums", [P, 4, HEADS])
        prec = sb("prec", [P, 4, HEADS])
        p_t = sb("p_t", [P, 2, 2, P])
        o_n = sb("o_n", [P, 2, PAIRS * HD])
        o_t = sb("o_t", [P, 2, PAIRS, P])
        stats = sb("stats", [P, 16, 6])
        meanvar = sb("meanvar", [P, 16, 2])
        rstd = sb("rstd", [P, 16, 1])
        mhalf = sb("mhalf", [P, 16])
        x_n = sb("x_n", [P, 2, DIM])
        xn_t = sb("xn_t", [P, 2, DIM])
        h_gate = sb("h_gate", [P, 2, HID])
        h_act = sb("h_act", [P, 2, HID])
        h_lin = sb("h_lin", [P, 2, HID])
        h = sb("h", [P, HID])
        h_t = sb("h_t", [P, 3, P])

        bank_proj = [ps("bank_proj0"), ps("bank_proj1"), ps("bank_proj2")]
        bank_turn = ps("bank_turn")
        bank_s = ps("bank_s")
        bank_pt = ps("bank_pt")
        bank_o = ps("bank_o")
        bank_misc = ps("bank_misc")

        passed = {e.engine: sem(f"passed_{n}") for n, e in enumerate((nc.scalar, nc.vector, nc.gpsimd))}
        weights_in = sem("weights_in")
        consts_set = sem("consts_set")
        x_var = sem("x_var")
        x_stats = sem("x_stats")
        x_rstd = sem("x_rstd")
        x_ready = sem("x_ready")
        xin_set = sem("xin_set")
        pe_x = sem("pe_x")
        x_turned = sem("x_turned")
        proj_done = sem("proj_done")
        rot_read = sem("rot_read")
        sq_done = sem("sq_done")
        ssq_done = sem("ssq_done")
        rope_chain = sem("rope_chain")
        ln_chain = sem("ln_chain")
        roped_set = sem("roped_set")
        rn8_set = sem("rn8_set")
        pe_turn = sem("pe_turn")
        turned = sem("turned")
        wv_set = sem("wv_set")
        v_set = [sem("v_set0"), sem("v_set1")]
        pe_s = sem("pe_s")
        masked = sem("masked")
        nbias_set = sem("nbias_set")
        exp_done = sem("exp_done")
        prec_set = sem("prec_set")
        o_normed = sem("o_normed")
        pe_oh = sem("pe_oh")
        pe_pt = sem("pe_pt")
        pt_set = sem("pt_set")
        pe_pv = sem("pe_pv")
        o_set = sem("o_set")
        pe_wo = sem("pe_wo")
        xmid_set = sem("xmid_set")
        xmid_b_set = sem("xmid_b_set")
        pe_m = sem("pe_m")
        m_turned = sem("m_turned")
        pe_ms = sem("pe_ms")
        ln_stats = sem("ln_stats")
        ln_rstd = sem("ln_rstd")
        xn_set = sem("xn_set")
        pe_xn = sem("pe_xn")
        xn_turned = sem("xn_turned")
        pe_w1 = sem("pe_w1")
        hid_read = sem("hid_read")
        gelu_done = sem("gelu_done")
        h_set = sem("h_set")
        pe_h = sem("pe_h")
        h_turned = sem("h_turned")
        pe_w2 = sem("pe_w2")

        def wait(eng, s, per_tile, tile, c):
            n = tile * per_tile + c
            if isinstance(n, int) and (n <= 0 or tile >= TILES):
                return
            eng.wait_ge(s, n)

        def wait_apart(eng, s, per_tile, tile, c):
            wait(eng, s, per_tile, tile, c)
            if not isinstance(tile, int):
                eng.sem_inc(passed[eng.engine], 1)

        def slots(eng, body):
            def static(N):
                body(N, N % 4, lambda lag: (N - lag) // 16 % 2, lambda lag: (N - lag) // 4 % 4,
                     lambda lag: 0 <= N - lag < TILES)

            for N in range(8):
                static(N)
            with eng.Fori(2, TILES // 4) as i:
                for T in range(4):
                    def parity(lag, T=T):
                        return (i + (T - lag) // 4) // 4 % 2

                    def row(lag, T=T):
                        return (i + (T - lag) // 4) % 4
                    body(4 * i + T, T, parity, row, lambda lag: True)
            for N in range(TILES, TILES + 7):
                static(N)

        CHUNK_COLS = [INNER, 0, INNER + 512, 512]

        block = ctx.enter_context(nc.Block())

        @block.sync
        def _(sp):
            for layer in range(DEPTH):
                half = layer % 2
                if layer >= 1:
                    sp.wait_ge(weights_in, 16 * N_LOADS * layer)
                if layer >= 2:
                    sp.wait_ge(x_ready, 16 * layer)
                sp.dma_start(w_qkv[:, half, :], w["Wqkv"][layer]).then_inc(weights_in, 16)
                sp.dma_start(w_o[:, half, :, :], w["Wo"][layer].rearrange("(g p) n -> p g n", p=P)
                             ).then_inc(weights_in, 16)
                sp.dma_start(w_1[:, half, :], w["W1"][layer]).then_inc(weights_in, 16)
                sp.dma_start(w_2[:, half, 0:2, :], w["W2"][layer, 0:2 * P, :].rearrange("(g p) n -> p g n", p=P)
                             ).then_inc(weights_in, 16)
                sp.dma_start(w_2[0:HID - 2 * P, half, 2, :], w["W2"][layer, 2 * P:HID, :]).then_inc(weights_in, 16)
                sp.dma_start(b_1[:, half, :], w["b1"][layer].partition_broadcast(P)).then_inc(weights_in, 16)
                sp.dma_start(b_2[:, half, :], w["b2"][layer].partition_broadcast(P)).then_inc(weights_in, 16)
                sp.dma_start(ln_gb[:, half, 0:1], w["ln_g"][layer].unsqueeze(1)).then_inc(weights_in, 16)
                sp.dma_start(ln_gb[:, half, 1:2], w["ln_b"][layer].unsqueeze(1)).then_inc(weights_in, 16)
            sp.wait_ge(weights_in, 16 * N_LOADS * DEPTH)

        @block.tensor
        def _(pe):
            def turn_x(t, T):
                wait(pe, xin_set, 1, t, 1)
                wait(pe, turned, 4, t - 1, 0)
                pe.transpose(bank_turn[:, 0:P], xin[:, T, :], ident[:, :]).then_inc(pe_x, 1)

            def project(t, T, c, half):
                if c == 0:
                    wait(pe, x_turned, 1, t, 1)
                    if T == 0:
                        pe.wait_ge(weights_in, (t // 16 + 1) * (16 * N_LOADS))
                if c in (0, 1):
                    wait(pe, v_set[c], 2, t - 1, 2)
                elif c == 2:
                    wait(pe, hid_read, 2, t - 3, 1)
                    wait(pe, v_set[1], 2, t - 1, 1)
                elif c == 3:
                    wait(pe, hid_read, 2, t - 3, 2)
                    wait(pe, sq_done, 4, t, 1)
                elif c < 7:
                    wait(pe, sq_done, 4, t, c - 2)
                else:
                    wait(pe, v_set[0], 2, t, 1)
                if c < 4:
                    pe.matmul(bank_proj[c % 3][:, :], xshift[:, T * P:(T + 1) * P],
                              w_qkv[:, half, CHUNK_COLS[c]:CHUNK_COLS[c] + 512],
                              start=True, stop=True).then_inc(proj_done, 1)
                    return
                first = T * P + (c - 5) * WINDOW
                parts = [(0, 2 * WINDOW, first)] if first >= 0 else [(0, WINDOW, 0), (WINDOW, WINDOW, 0)]
                if c == 4:
                    wait(pe, wv_set, 1, t // 4, 1)
                for row, count, token in parts:
                    for j in range(2):
                        out = bank_proj[c % 3][64 * j + row:64 * j + row + count, :]
                        last = pe.matmul(out, xshift[:, token:token + count], w_v[:, j, :, :], start=True, stop=True)
                last.then_inc(proj_done, 1)

            def turn_chunk(t, c):
                wait(pe, roped_set, 4, t, c + 1)
                if c == 0:
                    wait(pe, x_turned, 1, t + 1, 1)
                elif c == 2:
                    wait(pe, h_turned, 1, t - 4, 1)
                    wait(pe, turned, 4, t, c)
                else:
                    wait(pe, turned, 4, t, c)
                for g in range(4):
                    last = pe.transpose(bank_turn[:, g * P:(g + 1) * P], roped[:, c % 2, g * P:(g + 1) * P],
                                        ident[:, :])
                last.then_inc(pe_turn, 1)

            def scores(t, T, g):
                wait(pe, turned, 4, t, 2 * g + 2)
                wait(pe, masked, 8, t, 4 * g)
                for hp in range(4 * g, 4 * g + 4):
                    out = bank_s[:, P * (hp % 4):P * (hp % 4 + 1)].rearrange("p (h c) -> p h c", h=2)
                    for n in range(4):
                        rows = slice(WINDOW * n, WINDOW * (n + 1))
                        q = q_t[:, T % 2, hp, rows]
                        if n:
                            last = pe.matmul(out[rows, :, :], q, k_z[:, T % 2, hp, :, WINDOW * (n - 1):WINDOW * (n + 1)],
                                             start=True, stop=True)
                            continue
                        before = k_z[:, (T - 1) % 2, hp, :, 3 * WINDOW:4 * WINDOW] if T > 0 else k_z[:, T % 2, hp, :, rows]
                        pe.matmul(out[rows, :, 0:WINDOW], q, before, start=True, stop=True)
                        pe.matmul(out[rows, :, WINDOW:2 * WINDOW], q, k_z[:, T % 2, hp, :, rows], start=True, stop=True)
                last.then_inc(pe_s, 1)

            def turn_probs(t, T, k):
                wait(pe, exp_done, 8, t, 2 * k + 2)
                wait(pe, pt_set, 4, t, k)
                if k == 3:
                    wait(pe, o_set, 2, t, 1)
                elif k == 1:
                    wait(pe, o_set, 2, t - 1, 2)
                for n in range(2):
                    last = pe.transpose(bank_pt[:, P * n:P * (n + 1)], prob[:, (2 * k + n) % 4, :, :], ident[:, :])
                last.then_inc(pe_pt, 1)

            def weigh_values(t, T, k):
                if k == 0:
                    wait(pe, v_set[0], 2, t, 2)
                    wait(pe, v_set[1], 2, t, 2)
                if k % 2 == 0:
                    wait(pe, o_normed, 2, t, k // 2)
                wait(pe, pt_set, 4, t, k + 1)
                for hp in (2 * k, 2 * k + 1):
                    for n in range(4):
                        rows = slice(WINDOW * n, WINDOW * (n + 1))
                        last = pe.matmul(bank_o[rows, P * (hp % 4):P * (hp % 4 + 1)], p_t[:, k % 2, hp % 2, rows],
                                         v_w[:, T % 2, n, hp, :, :], start=True, stop=True)
                last.then_inc(pe_pv, 1)

            def turn_heads(t, T, c):
                wait(pe, o_normed, 2, t, c + 1)
                if c == 0:
                    wait(pe, pt_set, 4, t, 3)
                elif isinstance(t, int) and t + 1 >= TILES:
                    wait(pe, pt_set, 4, t, 4)
                else:
                    wait(pe, pt_set, 4, t + 1, 1)
                for g in range(4):
                    last = pe.transpose(bank_pt[:, P * g:P * (g + 1)], o_n[:, c, P * g:P * (g + 1)], ident[:, :])
                last.then_inc(pe_oh, 1)

            def project_out(t, T, half):
                wait(pe, o_set, 2, t, 2)
                wait(pe, xn_turned, 1, t - 1, 1)
                for g in range(PAIRS):
                    last = pe.matmul(bank_misc[:, 0:DIM], o_t[:, T % 2, g, :], w_o[:, half, g, :],
                                     start=g == 0, stop=g == PAIRS - 1)
                last.then_inc(pe_wo, 1)

            def turn_mid(t, T):
                wait(pe, xmid_set, 1, t, 1)
                pe.transpose(bank_misc[:, 0:P], xmid[:, T, :], ident[:, :]).then_inc(pe_m, 1)

            def turn_mid_back(t, T):
                wait(pe, m_turned, 1, t, 1)
                wait(pe, x_ready, 1, t - 2, 17)
                pe.transpose(bank_misc[:, 0:P], mshift[:, T * P:(T + 1) * P], ident[:, :]).then_inc(pe_ms, 1)

            def turn_xn(t, T):
                wait(pe, xn_set, 1, t, 1)
                pe.transpose(bank_misc[:, 0:P], x_n[:, T % 2, :], ident[:, :]).then_inc(pe_xn, 1)

            def mlp_up(t, T, c, half):
                if c == 0:
                    wait(pe, xn_turned, 1, t, 1)
                if c == 0:
                    wait(pe, v_set[1], 2, t + 2, 1)
                else:
                    wait(pe, sq_done, 4, t + 3, 1)
                if isinstance(t, int) and t + 3 >= TILES:
                    wait(pe, v_set[1 - c], 2, TILES - 1, 1 + c)
                    wait(pe, hid_read, 2, t - 1, c + 1)
                col = HID * (1 - c)
                pe.matmul(bank_proj[(2, 0)[c]][:, 0:HID], xn_t[:, T % 2, :], w_1[:, half, col:col + HID],
                          start=True, stop=True).then_inc(pe_w1, 1)

            def turn_h(t):
                wait(pe, h_set, 1, t, 1)
                wait(pe, turned, 4, t + 4, 2)
                if isinstance(t, int) and t + 4 >= TILES:
                    wait(pe, turned, 4, TILES - 1, 4)
                    wait(pe, h_turned, 1, t - 1, 1)
                for g in range(3):
                    n = min(P, HID - g * P)
                    last = pe.transpose(bank_turn[0:n, g * P:(g + 1) * P], h[:, g * P:g * P + n], ident[:, :])
                last.then_inc(pe_h, 1)

            def mlp_down(t, half):
                wait(pe, h_turned, 1, t, 1)
                wait(pe, m_turned, 1, t + 2, 1)
                if isinstance(t, int) and t + 2 >= TILES:
                    wait(pe, x_ready, 1, t - 1, 17)
                    wait(pe, xn_turned, 1, TILES - 1, 1)
                for g in range(3):
                    n = min(P, HID - g * P)
                    last = pe.matmul(bank_misc[:, 0:DIM], h_t[0:n, g, :], w_2[0:n, half, g, :],
                                     start=g == 0, stop=g == 2)
                last.then_inc(pe_w2, 1)

            def slot(N, T, parity, row, runs):
                if runs(1):
                    project(N - 1, (T - 1) % 4, 0, parity(1))
                if runs(4):
                    turn_mid_back(N - 4, (T - 4) % 4)
                if runs(3):
                    turn_heads(N - 3, (T - 3) % 4, 0)
                    weigh_values(N - 3, (T - 3) % 4, 2)
                if runs(2):
                    turn_chunk(N - 2, 3)
                if runs(1):
                    project(N - 1, (T - 1) % 4, 1, parity(1))
                if runs(3):
                    turn_probs(N - 3, (T - 3) % 4, 3)
                if runs(4):
                    turn_xn(N - 4, (T - 4) % 4)
                if runs(3):
                    weigh_values(N - 3, (T - 3) % 4, 3)
                if runs(4):
                    mlp_up(N - 4, (T - 4) % 4, 0, parity(4))
                if runs(0):
                    turn_x(N, T)
                if runs(2):
                    turn_probs(N - 2, (T - 2) % 4, 0)
                if runs(4):
                    mlp_up(N - 4, (T - 4) % 4, 1, parity(4))
                if runs(1):
                    project(N - 1, (T - 1) % 4, 2, parity(1))
                if runs(3):
                    turn_heads(N - 3, (T - 3) % 4, 1)
                if runs(2):
                    scores(N - 2, (T - 2) % 4, 1)
                    weigh_values(N - 2, (T - 2) % 4, 0)
                if runs(1):
                    turn_chunk(N - 1, 0)
                    project(N - 1, (T - 1) % 4, 3, parity(1))
                    project(N - 1, (T - 1) % 4, 4, parity(1))
                    turn_chunk(N - 1, 1)
                    project(N - 1, (T - 1) % 4, 5, parity(1))
                if runs(2):
                    turn_probs(N - 2, (T - 2) % 4, 1)
                if runs(1):
                    project(N - 1, (T - 1) % 4, 6, parity(1))
                if runs(5):
                    turn_h(N - 5)
                if runs(3):
                    project_out(N - 3, (T - 3) % 4, parity(3))
                if runs(1):
                    project(N - 1, (T - 1) % 4, 7, parity(1))
                if runs(2):
                    weigh_values(N - 2, (T - 2) % 4, 1)
                if runs(1):
                    turn_chunk(N - 1, 2)
                if runs(3):
                    turn_mid(N - 3, (T - 3) % 4)
                if runs(1):
                    scores(N - 1, (T - 1) % 4, 0)
                if runs(2):
                    turn_probs(N - 2, (T - 2) % 4, 2)
                if runs(5):
                    mlp_down(N - 5, parity(5))

            pe.wait_ge(consts_set, N_CONSTS)
            slots(pe, slot)

        @block.scalar
        def _(act):
            def x_out(t, T):
                wait(act, pe_x, 1, t, 1)
                wait(act, proj_done, 8, t - 3, 8)
                act.copy(xshift[0:64, T * P:(T + 1) * P], bank_turn[0:64, 0:P])
                act.copy(xshift[64:P, T * P + 1:(T + 1) * P + 1], bank_turn[64:P, 0:P]).then_inc(x_turned, 1)

            def square(t, c):
                wait(act, rot_read, 4, t, c + 1)
                wait(act, ssq_done, 4, t, c - 1)
                act.activation(sq[:, c % 2, :], bank_proj[c % 3][:, :], ACT.Square).then_inc(sq_done, 1)

            def turned_out(t, T, c):
                wait(act, pe_turn, 4, t, c + 1)
                g = 4 * (c // 2)
                src = bank_turn[:, :].rearrange("p (g n) -> p g n", g=4)
                if c % 2 == 0:
                    wait(act, pe_s, 2, t - 1, 2)
                    act.copy(k_z[0:64, T % 2, g:g + 4, 0, :], src[0:64])
                    act.copy(k_z[64:P, T % 2, g:g + 4, 1, :], src[64:P]).then_inc(turned, 1)
                else:
                    wait(act, pe_s, 2, t - 2, 2)
                    act.copy(q_t[:, T % 2, g:g + 4, :], src).then_inc(turned, 1)

            def values_out(t, T, c):
                wait(act, proj_done, 8, t, 5 + c)
                wait(act, pe_pv, 4, t - 2, 4)
                for j in range(2):
                    rows = slice(64 * j, 64 * j + 64)
                    last = act.copy(v_w[rows, T % 2, c, :, j, :],
                           bank_proj[(4 + c) % 3][rows, :].rearrange("p (g d) -> p g d", d=HD))
                last.then_inc(v_set[c % 2], 1)

            def exponent(t, T, hp):
                wait(act, nbias_set, 8, t, hp + 1)
                wait(act, pe_pt, 4, t, hp // 2 - 1)
                for j in range(2):
                    head = 2 * hp + j
                    last = act.activation(prob[:, hp % 4, j, :], s_m[:, hp % 4, j, :], ACT.Exp,
                                          bias=nbias[:, T, head:head + 1],
                                          scale=rnorm[:, T, 1 + 2 * (hp // 4), head % 8:head % 8 + 1],
                                          accum_out=psums[:, T, head:head + 1])
                last.then_inc(exp_done, 1)

            def probs_out(t, T, k):
                wait(act, pe_pt, 4, t, k + 1)
                wait(act, pe_pv, 4, t, k - 1)
                act.copy(p_t[:, k % 2, :, :], bank_pt[:, 0:2 * P].rearrange("p (n c) -> p n c", n=2)).then_inc(pt_set, 1)

            def heads_out(t, T, c):
                wait(act, pe_oh, 2, t, c + 1)
                wait(act, pe_wo, 1, t - 2, 1)
                act.copy(o_t[:, T % 2, 4 * c:4 * c + 4, :],
                         bank_pt[:, :].rearrange("p (g n) -> p g n", g=4)).then_inc(o_set, 1)

            def mid_out(t, T):
                wait(act, pe_m, 1, t, 1)
                act.copy(mshift[0:64, T * P:(T + 1) * P], bank_misc[0:64, 0:P])
                act.copy(mshift[64:P, T * P + 1:(T + 1) * P + 1], bank_misc[64:P, 0:P]).then_inc(m_turned, 1)

            def xn_out(t, T, half):
                wait_apart(act, pe_xn, 1, t, 1)
                act.activation(xn_t[:, T % 2, :], bank_misc[:, 0:P], ACT.Identity,
                               bias=ln_gb[:, half, 1:2], scale=ln_gb[:, half, 0:1]).then_inc(xn_turned, 1)

            def gelu(t, T):
                if T % 2:
                    for n in range(2):
                        wait(act, hid_read, 2, t - 1 + n, 1)
                        wait(act, h_set, 1, t - 3 + n, 1)
                        act.activation(h_act[:, n, :], h_gate[:, n, :], ACT.Gelu).then_inc(gelu_done, 1)

            def slot(N, T, parity, row, runs):
                if runs(3):
                    heads_out(N - 3, (T - 3) % 4, 0)
                if runs(2):
                    turned_out(N - 2, (T - 2) % 4, 3)
                if runs(1):
                    square(N - 1, 0)
                if runs(3):
                    probs_out(N - 3, (T - 3) % 4, 3)
                if runs(4):
                    xn_out(N - 4, (T - 4) % 4, parity(4))
                if runs(2):
                    exponent(N - 2, (T - 2) % 4, 1)
                if runs(1):
                    square(N - 1, 1)
                if runs(0):
                    x_out(N, T)
                if runs(2):
                    exponent(N - 2, (T - 2) % 4, 2)
                    probs_out(N - 2, (T - 2) % 4, 0)
                if runs(4):
                    gelu(N - 4, (T - 4) % 4)
                if runs(2):
                    exponent(N - 2, (T - 2) % 4, 3)
                if runs(1):
                    square(N - 1, 2)
                    turned_out(N - 1, (T - 1) % 4, 0)
                if runs(2):
                    exponent(N - 2, (T - 2) % 4, 4)
                if runs(3):
                    heads_out(N - 3, (T - 3) % 4, 1)
                if runs(1):
                    square(N - 1, 3)
                    turned_out(N - 1, (T - 1) % 4, 1)
                if runs(2):
                    probs_out(N - 2, (T - 2) % 4, 1)
                if runs(1):
                    values_out(N - 1, (T - 1) % 4, 0)
                    values_out(N - 1, (T - 1) % 4, 2)
                if runs(2):
                    exponent(N - 2, (T - 2) % 4, 5)
                if runs(3):
                    mid_out(N - 3, (T - 3) % 4)
                if runs(2):
                    exponent(N - 2, (T - 2) % 4, 6)
                    probs_out(N - 2, (T - 2) % 4, 2)
                    exponent(N - 2, (T - 2) % 4, 7)
                if runs(1):
                    turned_out(N - 1, (T - 1) % 4, 2)
                    exponent(N - 1, (T - 1) % 4, 0)

            act.wait_ge(consts_set, N_CONSTS)
            slots(act, slot)

        @block.vector
        def _(dve):
            def rotate(t, T, c, table):
                wait(dve, proj_done, 8, t, c + 1)
                wait(dve, roped_set, 4, t, c - 1)
                kind = 0 if c % 2 else 2
                src = bank_proj[c % 3][:, :]
                cosine = table[:, kind, :].unsqueeze(1).broadcast_to([P, 8, HD])
                sine = table[:, kind + 1, :].rearrange("p (f d) -> p f d", f=2).unsqueeze(1).broadcast_to([P, 8, 2, HD // 2])
                dve.tensor_tensor(rot_c[:, c % 2, :].rearrange("p (h d) -> p h d", h=8),
                                  src.rearrange("p (h d) -> p h d", h=8), cosine, ALU.mult)
                dve.tensor_tensor(rot_s[:, c % 2, :].rearrange("p (h f d) -> p h f d", h=8, f=2),
                                  src.rearrange("p (h f d) -> p h f d", h=8, f=2)[:, :, ::-1, :], sine,
                                  ALU.mult).then_inc(rot_read, 1)

            def sum_squares(t, T, c):
                wait(dve, sq_done, 4, t, c + 1)
                dve.tensor_reduce(ssq[:, T, c, :], sq[:, c % 2, :].rearrange("p (h d) -> p h d", h=8),
                                  AX.X, ALU.add).then_inc(ssq_done, 1)

            def mask_max(t, T, hp):
                wait(dve, pe_s, 2, t, hp // 4 + 1)
                wait_apart(dve, exp_done, 8, t, hp - 3)
                first = 0 if T > 0 else 2 * WINDOW
                for j in range(2):
                    head = 2 * hp + j
                    last = dve.tensor_tensor_reduce(s_m[:, hp % 4, j, :],
                                                    bank_s[:, P * (hp % 4) + 2 * WINDOW * j:P * (hp % 4) + 2 * WINDOW * (j + 1)],
                                                    mask[:, first:first + 2 * WINDOW],
                                                    1.0, LOWEST, ALU.add, ALU.max, smax[:, T, head:head + 1])
                last.then_inc(masked, 1)

            def biases(t, T, hp):
                wait(dve, masked, 8, t, hp + 1)
                wait(dve, rn8_set, 2, t, 1 + hp // 4)
                dve.tensor_tensor(nbias[:, T, 2 * hp:2 * hp + 2], smax[:, T, 2 * hp:2 * hp + 2],
                                  nrn8[:, T, 2 * hp:2 * hp + 2], ALU.mult).then_inc(nbias_set, 1)

            def reciprocal(t, T, hp):
                wait(dve, exp_done, 8, t, hp + 1)
                dve.reciprocal(prec[:, T, 2 * hp:2 * hp + 2], psums[:, T, 2 * hp:2 * hp + 2]).then_inc(prec_set, 1)

            def norm_heads(t, T, c):
                wait(dve, pe_pv, 4, t, 2 * c + 2)
                wait(dve, prec_set, 8, t, 4 * c + 4)
                wait(dve, pe_oh, 2, t - 1, c + 1)
                dve.tensor_tensor(o_n[:, c, :].rearrange("p (h d) -> p h d", h=8),
                                  bank_o[:, :].rearrange("p (h d) -> p h d", h=8),
                                  prec[:, T, 8 * c:8 * c + 8].unsqueeze(2).broadcast_to([P, 8, HD]),
                                  ALU.mult).then_inc(o_normed, 1)

            def mid(t, T):
                wait(dve, pe_wo, 1, t, 1)
                dve.tensor_tensor(xmid[:, T, :], bank_misc[:, 0:DIM], xin[:, T, :], ALU.add).then_inc(xmid_set, 1)

            def mid_stats(t, T):
                wait(dve, pe_ms, 1, t, 1)
                dve.bn_stats(stats[:, T, :], bank_misc[:, 0:P]).then_inc(ln_stats, 1)
                wait_apart(dve, ln_stats, 2, t, 1)
                dve.bn_aggr(meanvar[:, T, :], stats[:, T, :]).then_inc(ln_stats, 1)

            def mid_norm(t, T):
                wait(dve, ln_rstd, 1, t, 1)
                dve.tensor_scalar(x_n[:, T % 2, :], bank_misc[:, 0:P], meanvar[:, T, 0:1], rstd[:, T, :],
                                  ALU.subtract, ALU.mult).then_inc(xn_set, 1)

            def hidden(t, T, c, half):
                out, col = ((h_gate, HID), (h_lin, 0))[c]
                wait(dve, pe_w1, 2, t, c + 1)
                wait(dve, (gelu_done, h_set)[c], 1, t - 2, 1)
                dve.tensor_tensor(out[:, T % 2, :], bank_proj[(2, 0)[c]][:, 0:HID], b_1[:, half, col:col + HID],
                                  ALU.add).then_inc(hid_read, 1)

            def value_weights(t, T, half):
                if T == 0:
                    dve.wait_ge(weights_in, (t // 16 + 1) * (16 * N_LOADS))
                    wait(dve, proj_done, 8, t - 1, 8)
                    columns = w_qkv[:, half, 2 * INNER:3 * INNER].rearrange("p (g j d) -> p j g d", j=2, d=HD)
                    dve.tensor_copy(w_v[:, :, :, :], columns).then_inc(wv_set, 1)

            def values_out(t, T, c):
                wait(dve, proj_done, 8, t, 5 + c)
                wait(dve, pe_pv, 4, t - 2, 4)
                for j in range(2):
                    rows = slice(64 * j, 64 * j + 64)
                    last = dve.tensor_copy(v_w[rows, T % 2, c, :, j, :],
                           bank_proj[(4 + c) % 3][rows, :].rearrange("p (g d) -> p g d", d=HD))
                last.then_inc(v_set[c % 2], 1)

            def h_out(t):
                wait(dve, pe_h, 1, t, 1)
                dve.tensor_copy(h_t[:, 0:2, :], bank_turn[:, 0:2 * P].rearrange("p (g n) -> p g n", g=2))
                dve.tensor_copy(h_t[0:HID - 2 * P, 2, :], bank_turn[0:HID - 2 * P, 2 * P:3 * P]).then_inc(h_turned, 1)

            def finish(t, T, r):
                wait(dve, pe_w2, 1, t, 1)
                wait(dve, xmid_b_set, 1, t, 1)
                dve.tensor_tensor(xres[:, r * 4 + T, :], bank_misc[:, 0:DIM], xmid_b[:, T, :],
                                  ALU.add).then_inc(x_ready, 1)

            def slot(N, T, parity, row, runs):
                if runs(2):
                    values_out(N - 2, (T - 2) % 4, 3)
                if runs(3):
                    reciprocal(N - 3, (T - 3) % 4, 6)
                if runs(6):
                    finish(N - 6, (T - 6) % 4, row(6))
                if runs(2):
                    mask_max(N - 2, (T - 2) % 4, 0)
                    biases(N - 2, (T - 2) % 4, 0)
                if runs(4):
                    mid_stats(N - 4, (T - 4) % 4)
                if runs(1):
                    rotate(N - 1, (T - 1) % 4, 0, rot[:, (N - 1) // 16, (T - 1) % 4, :, :])
                if runs(3):
                    reciprocal(N - 3, (T - 3) % 4, 7)
                if runs(2):
                    mask_max(N - 2, (T - 2) % 4, 1)
                    reciprocal(N - 2, (T - 2) % 4, 0)
                if runs(1):
                    value_weights(N - 1, (T - 1) % 4, parity(1))
                if runs(2):
                    biases(N - 2, (T - 2) % 4, 1)
                if runs(4):
                    mid_norm(N - 4, (T - 4) % 4)
                if runs(1):
                    rotate(N - 1, (T - 1) % 4, 1, rot[:, (N - 1) // 16, (T - 1) % 4, :, :])
                if runs(2):
                    mask_max(N - 2, (T - 2) % 4, 2)
                if runs(1):
                    sum_squares(N - 1, (T - 1) % 4, 0)
                if runs(2):
                    mask_max(N - 2, (T - 2) % 4, 3)
                    biases(N - 2, (T - 2) % 4, 2)
                if runs(3):
                    norm_heads(N - 3, (T - 3) % 4, 1)
                if runs(4):
                    hidden(N - 4, (T - 4) % 4, 0, parity(4))
                if runs(2):
                    biases(N - 2, (T - 2) % 4, 3)
                    reciprocal(N - 2, (T - 2) % 4, 1)
                if runs(1):
                    sum_squares(N - 1, (T - 1) % 4, 1)
                if runs(2):
                    reciprocal(N - 2, (T - 2) % 4, 2)
                if runs(4):
                    hidden(N - 4, (T - 4) % 4, 1, parity(4))
                if runs(1):
                    rotate(N - 1, (T - 1) % 4, 2, rot[:, (N - 1) // 16, (T - 1) % 4, :, :])
                if runs(2):
                    mask_max(N - 2, (T - 2) % 4, 4)
                    biases(N - 2, (T - 2) % 4, 4)
                if runs(1):
                    sum_squares(N - 1, (T - 1) % 4, 2)
                if runs(2):
                    reciprocal(N - 2, (T - 2) % 4, 3)
                if runs(1):
                    rotate(N - 1, (T - 1) % 4, 3, rot[:, (N - 1) // 16, (T - 1) % 4, :, :])
                if runs(2):
                    mask_max(N - 2, (T - 2) % 4, 5)
                if runs(1):
                    sum_squares(N - 1, (T - 1) % 4, 3)
                if runs(5):
                    h_out(N - 5)
                if runs(2):
                    biases(N - 2, (T - 2) % 4, 5)
                    reciprocal(N - 2, (T - 2) % 4, 4)
                if runs(1):
                    values_out(N - 1, (T - 1) % 4, 1)
                if runs(2):
                    mask_max(N - 2, (T - 2) % 4, 6)
                    mask_max(N - 2, (T - 2) % 4, 7)
                    biases(N - 2, (T - 2) % 4, 6)
                if runs(3):
                    mid(N - 3, (T - 3) % 4)
                if runs(2):
                    reciprocal(N - 2, (T - 2) % 4, 5)
                    biases(N - 2, (T - 2) % 4, 7)
                    norm_heads(N - 2, (T - 2) % 4, 0)

            dve.memset(mhalf[:, :], -0.5).then_inc(consts_set, 1)
            dve.memset(xshift[64:P, 0:1], 0.0).then_inc(consts_set, 1)
            dve.memset(mshift[64:P, 0:1], 0.0).then_inc(consts_set, 1)
            for n in range(16):
                dve.bn_stats(stats[:, n, :], xo[:, n, :]).then_inc(x_stats, 1)
            dve.wait_ge(x_stats, 16)
            for n in range(16):
                dve.bn_aggr(meanvar[:, n, :], stats[:, n, :]).then_inc(x_stats, 1)
            dve.memset(k_z[0:64, :, :, 1, :], 0.0).then_inc(consts_set, 1)
            dve.memset(k_z[64:P, :, :, 0, :], 0.0).then_inc(consts_set, 1)
            dve.memset(v_w[0:64, :, :, :, 1, :], 0.0).then_inc(consts_set, 1)
            dve.memset(v_w[64:P, :, :, :, 0, :], 0.0).then_inc(consts_set, 1)
            dve.wait_ge(x_rstd, 1)
            for n in range(16):
                dve.tensor_scalar(xres[:, n, :], xo[:, n, :], meanvar[:, n, 0:1], rstd[:, n, :],
                                  ALU.subtract, ALU.mult).then_inc(x_ready, 1)
            slots(dve, slot)
            dve.wait_ge(x_ready, 16 + TILES)
            dve.tensor_tensor(xo[:, :, :], xo[:, :, :], xres[:, :, :], ALU.add)

        @block.gpsimd
        def _(pool):
            def link(t, c, ins):
                ins.then_inc(rope_chain, 1)
                wait_apart(pool, rope_chain, 10, t, c)

            def copy_in(t, T, r):
                wait_apart(pool, x_ready, 1, t, 1)
                pool.tensor_copy(xin[:, T, :], xres[:, r * 4 + T, :]).then_inc(xin_set, 1)

            def rope(t, T, c):
                wait(pool, rot_read, 4, t, c + 1)
                wait(pool, pe_turn, 4, t, c - 1)
                ins = pool.tensor_tensor(roped[:, c % 2, :], rot_c[:, c % 2, :], rot_s[:, c % 2, :], ALU.add)
                if c % 2:
                    ins.then_inc(roped_set, 1)
                else:
                    link(t, 1 if c == 0 else 6, ins)

            def norms(t, T, c):
                wait_apart(pool, ssq_done, 4, t, c + 1)
                n = (2, 4, 7, 9)[c]
                link(t, n, pool.tensor_scalar(ssq[:, T, c, :], ssq[:, T, c, :], 1e-24, 1.0 / 64 if c % 2 else 1.0,
                                              ALU.max, ALU.mult))
                ins = pool.tensor_tensor(rnorm[:, T, c, :], ssq[:, T, c, :], mhalf[:, 0:8], ALU.pow)
                link(t, n + 1, ins)
                if c % 2:
                    head = 8 * (c // 2)
                    pool.tensor_scalar(nrn8[:, T, head:head + 8], rnorm[:, T, c, :], -1.0, 1.0,
                                       ALU.mult, ALU.mult).then_inc(rn8_set, 1)
                else:
                    k = roped[:, c % 2, :].rearrange("p (h d) -> p h d", h=8)
                    pool.tensor_tensor(k, k, rnorm[:, T, c, :].unsqueeze(2).broadcast_to([P, 8, HD]),
                                       ALU.mult).then_inc(roped_set, 1)

            def mid_rstd(t, T):
                wait_apart(pool, ln_stats, 2, t, 2)
                pool.tensor_scalar(rstd[:, T, :], meanvar[:, T, 1:2], EPS, 1.0, ALU.add, ALU.mult).then_inc(ln_chain, 1)
                wait(pool, ln_chain, 1, t, 1)
                pool.tensor_tensor(rstd[:, T, :], rstd[:, T, :], mhalf[:, 0:1], ALU.pow).then_inc(ln_rstd, 1)

            def mid_bias(t, T, half):
                wait_apart(pool, xmid_set, 1, t, 1)
                pool.tensor_tensor(xmid_b[:, T, :], xmid[:, T, :], b_2[:, half, :], ALU.add).then_inc(xmid_b_set, 1)

            def gate(t, T):
                wait(pool, gelu_done, 1, t, 1)
                wait(pool, hid_read, 2, t, 2)
                wait(pool, pe_h, 1, t - 1, 1)
                pool.tensor_tensor(h[:, :], h_act[:, T % 2, :], h_lin[:, T % 2, :], ALU.mult).then_inc(h_set, 1)

            def slot(N, T, parity, row, runs):
                if runs(2):
                    rope(N - 2, (T - 2) % 4, 3)
                    norms(N - 2, (T - 2) % 4, 3)
                if runs(4):
                    mid_rstd(N - 4, (T - 4) % 4)
                if runs(1):
                    rope(N - 1, (T - 1) % 4, 0)
                if runs(0):
                    copy_in(N, T, row(0))
                if runs(1):
                    norms(N - 1, (T - 1) % 4, 0)
                    rope(N - 1, (T - 1) % 4, 1)
                    norms(N - 1, (T - 1) % 4, 1)
                if runs(5):
                    gate(N - 5, (T - 5) % 4)
                if runs(1):
                    rope(N - 1, (T - 1) % 4, 2)
                if runs(5):
                    mid_bias(N - 5, (T - 5) % 4, parity(5))
                if runs(1):
                    norms(N - 1, (T - 1) % 4, 2)

            pool.wait_ge(consts_set, 1)
            pool.wait_ge(x_stats, 32)
            pool.tensor_scalar(rstd[:, :, 0], meanvar[:, :, 1], EPS, 1.0, ALU.add, ALU.mult).then_inc(x_var, 1)
            pool.wait_ge(x_var, 1)
            pool.tensor_tensor(rstd[:, :, 0], rstd[:, :, 0], mhalf[:, :], ALU.pow).then_inc(x_rstd, 1)
            slots(pool, slot)

MATS = ("maa1", "maa2", "r", "k", "v", "o", "gate1", "gate2", "wa1", "wa2", "k1", "k2", "ones", "mean")
VECS = ("maa_x", "maa0", "maa1", "maa2", "maa3", "decay", "faaaa", "aaaaa", "misc_a", "misc_k", "ln_w", "ln_b")
HS = 8
EPS_HEAD = 0.00064
CHUNK = 32


def mixer(nc, shared, ins):
    with ExitStack() as ctx:
        def sb(name, shape):
            return ctx.enter_context(nc.sbuf_tensor("mix_" + name, shape, F32))

        mats = sb("mats", [P, len(MATS), P])
        vecs = sb("vecs", [P, len(VECS)])
        kept = {n: sb("kept_" + n, [P, BATCH, SEQ]) for n in ("r", "wt", "k", "v", "kk", "b", "g")}
        mat = {n: mats[:, i, :] for i, n in enumerate(MATS)}
        vec = {n: vecs[:, i:i + 1] for i, n in enumerate(VECS)}
        mixer_inputs(nc, shared, ins, mats, vecs, mat, vec, kept)
        mixer_scan(nc, ins, kept)
        mixer_output(nc, shared, mat, vec, kept)


def chain_steps(ctx, nc, prefix, steps):
    where = {name: (nc_sem, i, len(names)) for nc_sem, names in (
        (ctx.enter_context(nc.semaphore(f"{prefix}_{engine}_steps")), names) for engine, names in steps.items())
        for i, name in enumerate(names)}

    def done(instruction, name):
        instruction.then_inc(where[name][0], 1)

    def need(engine, b, *names):
        for name in names:
            semaphore, i, each = where[name]
            engine.wait_ge(semaphore, b * each + (i + 1))

    return done, need


IN_STEPS = {
    "pe": ("pe_x", "pe_lo", "pe_log", "pe_r", "pe_gate1", "pe_wa1", "pe_k1", "pe_k", "pe_v", "pe_g", "pe_decay", "pe_a",
           "pe_ma", "pe_kkk", "pe_mk", "pe_ss"),
    "act": ("xc", "lo_t", "gate_t", "low_wa", "low_k", "r_out", "v_out", "g_out", "a", "ma", "mk", "ksq", "e", "ln1",
            "exp_w", "wt", "exp_wmk", "sqrt_ss"),
    "dve": ("x_n", "xx", "mix", "xm_part", "xm", "k0", "z", "nabs", "kk0", "z_min", "w", "w_mk", "a_rest", "k_factor",
            "k_part", "k_out", "ss", "inv_norm", "kk", "kkb_out"),
}
OUT_STEPS = {
    "pe": ("pe_mean", "pe_rk", "pe_var", "pe_out"),
    "act": ("ysq", "std"),
    "dve": ("rk", "yc", "bonus", "var", "inv_std", "normed", "scaled", "summed", "gated"),
}


def mixer_inputs(nc, shared, ins, mats, vecs, mat, vec, kept):
    x, ident = shared["x"], shared["ident"]
    with ExitStack() as ctx:
        def sb(name, shape):
            return ctx.enter_context(nc.sbuf_tensor("mixin_" + name, shape, F32))

        sems = {}

        def sem(name):
            if name not in sems:
                sems[name] = ctx.enter_context(nc.semaphore("mixin_" + name))
            return sems[name]

        mhalf = sb("mhalf", [P, 16])
        stats = sb("stats", [P, 16, 6])
        meanvar = sb("meanvar", [P, 16, 2])
        rstd = sb("rstd", [P, 16])
        x_n = sb("x_n", [P, 4, DIM])
        xc = sb("xc", [P, SEQ + 1])
        xx, mix, lo_t = (sb(n, [P, SEQ]) for n in ("xx", "mix", "lo_t"))
        xm = sb("xm", [P, 4, SEQ])
        gate_t, low_wa, low_k, k0, z, e, w, a, ma, mk = (
            sb(n, [P, SEQ]) for n in ("gate_t", "low_wa", "low_k", "k0", "z", "e", "w", "a", "ma", "mk"))
        nabs, ln1, kk0, ksq, knorm = (sb(n, [P, SEQ]) for n in ("nabs", "ln1", "kk0", "ksq", "knorm"))
        banks = [ctx.enter_context(nc.psum_tensor(f"mixin_bank{n}", [P, 512], F32)) for n in range(8)]

        done, need = chain_steps(ctx, nc, "mixin", IN_STEPS)
        row_free = sem("row_free")

        block = ctx.enter_context(nc.Block())

        @block.sync
        def _(sp):
            sp.dma_start(mats[:, :, :], ins["table_mix"]).then_inc(sem("loaded"), 16)
            sp.dma_start(vecs[:, :], ins["table_vec"]).then_inc(sem("loaded"), 16)

        @block.tensor
        def _(pe):
            pe.wait_ge(sem("loaded"), 32)
            with pe.Fori(0, BATCH) as b:
                pe.wait_ge(row_free, b + 1)
                need(pe, b, "x_n")
                for T in range(4):
                    last = pe.transpose(banks[0][:, T * P:(T + 1) * P], x_n[:, T, :], ident[:, :])
                done(last, "pe_x")

                def product(bank, m, rhs, name, rows=slice(0, P), *names):
                    need(pe, b, *names)
                    done(pe.matmul(banks[bank][:, :], mat[m][rows, :], rhs, start=True, stop=True), name)

                product(1, "maa1", mix[:, :], "pe_lo", slice(0, P), "mix")
                need(pe, b, "lo_t")
                for g in range(4):
                    rows = slice(32 * g, 32 * g + 32)
                    last = pe.matmul(banks[2 + g][:, :], mat["maa2"][rows, :], lo_t[rows, :], start=True, stop=True)
                done(last, "pe_log")
                everything = slice(0, P)
                product(0, "r", xm[:, 0, :], "pe_r", everything, "xm")
                product(1, "gate1", xm[:, 0, :], "pe_gate1")
                product(2, "wa1", xm[:, 1, :], "pe_wa1")
                product(3, "k1", xm[:, 2, :], "pe_k1")
                product(6, "k", xm[:, 2, :], "pe_k")
                product(7, "v", xm[:, 3, :], "pe_v")
                product(4, "gate2", gate_t[:, :], "pe_g", everything, "gate_t")
                product(5, "wa2", low_wa[0:64, :], "pe_decay", slice(0, 64), "low_wa")
                product(0, "wa2", low_wa[64:96, :], "pe_a", slice(64, 96), "r_out")
                product(1, "wa2", low_wa[96:128, :], "pe_ma", slice(96, 128))
                product(3, "k2", low_k[0:32, :], "pe_kkk", slice(0, 32), "low_k")
                product(2, "k2", low_k[32:64, :], "pe_mk", slice(32, 64))
                product(7, "ones", ksq[:, :], "pe_ss", everything, "ksq", "v_out")

        @block.scalar
        def _(act):
            with act.Fori(0, BATCH) as b:
                act.wait_ge(row_free, b + 1)
                need(act, b, "pe_x")
                done(act.copy(xc[:, 1:SEQ + 1], banks[0][:, :]), "xc")
                need(act, b, "pe_lo")
                done(act.activation(lo_t[:, :], banks[1][:, :], ACT.Tanh), "lo_t")
                need(act, b, "pe_gate1")
                done(act.activation(gate_t[:, :], banks[1][:, :], ACT.Tanh), "gate_t")
                need(act, b, "pe_wa1")
                act.activation(low_wa[0:64, :], banks[2][0:64, :], ACT.Tanh)
                done(act.copy(low_wa[64:P, :], banks[2][64:P, :]), "low_wa")
                need(act, b, "pe_k1")
                act.activation(low_k[0:32, :], banks[3][0:32, :], ACT.Tanh)
                done(act.copy(low_k[32:64, :], banks[3][32:64, :]), "low_k")
                need(act, b, "pe_r")
                done(act.copy(kept["r"][:, b, :], banks[0][:, :]), "r_out")
                need(act, b, "pe_v")
                done(act.copy(kept["v"][:, b, :], banks[7][:, :]), "v_out")
                need(act, b, "pe_g")
                done(act.copy(kept["g"][:, b, :], banks[4][:, :]), "g_out")
                for bank, out, v, name in ((0, a, "aaaaa", "a"), (1, ma, "misc_a", "ma"), (2, mk, "misc_k", "mk")):
                    need(act, b, "pe_" + name)
                    done(act.activation(out[:, :], banks[bank][:, :], ACT.Sigmoid, bias=vec[v]), name)
                need(act, b, "kk0")
                done(act.activation(ksq[:, :], kk0[:, :], ACT.Square), "ksq")
                need(act, b, "nabs")
                done(act.activation(e[:, :], nabs[:, :], ACT.Exp), "e")
                need(act, b, "e")
                done(act.activation(ln1[:, :], e[:, :], ACT.Ln, bias=1.0), "ln1")
                need(act, b, "w")
                done(act.activation(e[:, :], w[:, :], ACT.Exp), "exp_w")
                need(act, b, "exp_w")
                done(act.activation(kept["wt"][:, b, :], e[:, :], ACT.Exp, scale=-1.0), "wt")
                need(act, b, "w_mk")
                done(act.activation(mk[:, :], mk[:, :], ACT.Exp), "exp_wmk")
                need(act, b, "ss")
                done(act.activation(knorm[:, :], knorm[:, :], ACT.Sqrt), "sqrt_ss")

        @block.vector
        def _(dve):
            dve.memset(mhalf[:, :], -0.5).then_inc(sem("stats"), 1)
            dve.memset(xc[:, 0:1], 0.0).then_inc(sem("stats"), 1)
            for n in range(16):
                layernorm_rows(2 * n + 3, dve, stats, meanvar, x[:, n, :], n, sem("stats"))
            dve.wait_ge(sem("rstd"), 1)
            dve.wait_ge(sem("loaded"), 32)
            dve.memset(xx[:, 0:1], 0.0).then_inc(row_free, 1)
            dve.wait_ge(row_free, 1)
            with dve.Fori(0, BATCH) as b:
                def psum(bank):
                    return banks[bank][:, :]

                dve.wait_ge(row_free, b + 1)
                for T in range(4):
                    n = b * 4 + T
                    last = dve.tensor_scalar(x_n[:, T, :], x[:, n, :], meanvar[:, n, 0:1], rstd[:, bass.ds(n, 1)],
                                             ALU.subtract, ALU.mult)
                done(last, "x_n")
                need(dve, b, "xc")
                xt = xc[:, 1:SEQ + 1]
                done(dve.tensor_tensor(xx[:, :], xc[:, 0:SEQ], xt, ALU.subtract), "xx")
                need(dve, b, "xx")
                done(dve.scalar_tensor_tensor(mix[:, :], xx[:, :], vec["maa_x"], xt, ALU.mult, ALU.add), "mix")
                need(dve, b, "pe_log")
                for g in range(4):
                    last = dve.scalar_tensor_tensor(xm[:, g, :], psum(2 + g), vec[f"maa{g}"], xx[:, :],
                                                    ALU.add, ALU.mult)
                done(last, "xm_part")
                need(dve, b, "xm_part")
                done(dve.tensor_tensor(xm[:, :, :], xm[:, :, :], xt.unsqueeze(1).broadcast_to([P, 4, SEQ]), ALU.add),
                     "xm")
                need(dve, b, "pe_k")
                done(dve.tensor_copy(k0[:, :], psum(6)), "k0")
                need(dve, b, "pe_decay")
                done(dve.tensor_scalar(z[:, :], psum(5), vec["decay"], None, ALU.add), "z")
                need(dve, b, "z")
                done(dve.scalar_tensor_tensor(nabs[:, :], z[:, :], -1.0, z[:, :], ALU.mult, ALU.min), "nabs")
                need(dve, b, "pe_kkk", "k0")
                done(dve.tensor_tensor(kk0[:, :], psum(3), k0[:, :], ALU.add), "kk0")
                need(dve, b, "nabs")
                done(dve.tensor_scalar(z[:, :], z[:, :], 0.0, 0.5, ALU.min, ALU.subtract), "z_min")
                need(dve, b, "z_min", "ln1")
                done(dve.tensor_tensor(w[:, :], z[:, :], ln1[:, :], ALU.subtract), "w")
                need(dve, b, "w", "mk")
                done(dve.tensor_tensor(mk[:, :], mk[:, :], w[:, :], ALU.mult), "w_mk")
                need(dve, b, "a", "ma")
                done(dve.scalar_tensor_tensor(nabs[:, :], ma[:, :], 1.0, a[:, :], ALU.subtract, ALU.mult), "a_rest")
                need(dve, b, "a_rest")
                done(dve.tensor_tensor(ma[:, :], ma[:, :], nabs[:, :], ALU.subtract), "k_factor")
                need(dve, b, "k_factor")
                done(dve.tensor_tensor(k0[:, :], k0[:, :], ma[:, :], ALU.mult), "k_part")
                need(dve, b, "k_part", "exp_wmk")
                done(dve.tensor_tensor(kept["k"][:, b, :], k0[:, :], mk[:, :], ALU.mult), "k_out")
                need(dve, b, "pe_ss")
                done(dve.tensor_scalar(knorm[:, :], psum(7), 1e-24, None, ALU.max), "ss")
                need(dve, b, "sqrt_ss")
                done(dve.reciprocal(knorm[:, :], knorm[:, :]), "inv_norm")
                need(dve, b, "inv_norm")
                done(dve.tensor_tensor(kk0[:, :], kk0[:, :], knorm[:, :], ALU.mult), "kk")
                need(dve, b, "kk")
                dve.tensor_copy(kept["kk"][:, b, :], kk0[:, :])
                done(dve.scalar_tensor_tensor(kept["b"][:, b, :], kk0[:, :], -1.0, a[:, :], ALU.mult, ALU.mult),
                     "kkb_out")
                need(dve, b, "kkb_out", "wt", "g_out", "k_out")
                dve.memset(xx[:, 0:1], 0.0).then_inc(row_free, 1)

        @block.gpsimd
        def _(pool):
            pool.wait_ge(sem("stats"), 34)
            pool.tensor_scalar(rstd[:, :], meanvar[:, :, 1], EPS, 1.0, ALU.add, ALU.mult).then_inc(sem("var"), 1)
            pool.wait_ge(sem("var"), 1)
            pool.tensor_tensor(rstd[:, :], rstd[:, :], mhalf[:, :], ALU.pow).then_inc(sem("rstd"), 1)


def mixer_scan(nc, ins, kept):
    with ExitStack() as ctx:
        def sb(name, shape):
            return ctx.enter_context(nc.sbuf_tensor("scan_" + name, shape, F32))

        def sem(name):
            return ctx.enter_context(nc.semaphore("scan_" + name))

        names = ("kk", "wt", "b", "k", "r")
        per_bank = 512 // (BATCH * CHUNK)
        fills_each = HS // per_bank
        fills = len(names) * fills_each
        spread = sb("spread", [P, HS, P])
        wide = {n: sb("wide_" + n, [P, 2, HS, BATCH, CHUNK]) for n in names}
        states = sb("states", [P, 2, HS, BATCH, CHUNK + 1])
        s_kk, s_decayed, s_fed, s_rank = (sb(n, [P, HS, BATCH]) for n in ("s_kk", "s_decayed", "s_fed", "s_rank"))
        sa = sb("sa", [P, BATCH])
        banks = [ctx.enter_context(nc.psum_tensor(f"scan_bank{n}", [P, per_bank, BATCH, CHUNK], F32)) for n in range(4)]

        loaded = sem("loaded")
        pe_wide = sem("pe_wide")
        wide_set = sem("wide_set")
        vk_set = sem("vk_set")
        kk_used = sem("kk_used")
        decayed = sem("decayed")
        sa_set = sem("sa_set")
        rank_one = sem("rank_one")
        state_set = sem("state_set")
        carried = sem("carried")
        r_used = sem("r_used")
        y_set = sem("y_set")

        block = ctx.enter_context(nc.Block())

        def chunks(eng, body):
            with eng.Fori(0, SEQ // CHUNK // 2) as pair:
                for parity in range(2):
                    body(pair * 2 + parity, parity)

        @block.sync
        def _(sp):
            sp.dma_start(spread[:, :, :], ins["table_spread"]).then_inc(loaded, 16)

        @block.tensor
        def _(pe):
            pe.wait_ge(loaded, 16)

            def spread_chunk(c, parity):
                for f in range(fills):
                    name, j = names[f // fills_each], f % fills_each * per_bank
                    bank = (parity * fills + f) % 4
                    pe.wait_ge(wide_set, c * fills + (f + 1))
                    for n in range(per_bank):
                        last = pe.matmul(banks[bank][:, n, :, :], spread[:, j + n, :],
                                         kept[name][:, :, bass.ds(c * CHUNK, CHUNK)], start=True, stop=True)
                    last.then_inc(pe_wide, 1)

            chunks(pe, spread_chunk)

        @block.scalar
        def _(act):
            act.sem_inc(wide_set, 4)

            def widen(c, parity):
                act.wait_ge(y_set, c + 1)
                for f in range(fills):
                    name, j = names[f // fills_each], f % fills_each * per_bank
                    bank = (parity * fills + f) % 4
                    act.wait_ge(pe_wide, c * fills + (f + 1))
                    act.copy(wide[name][:, parity, j:j + per_bank, :, :], banks[bank][:, :, :, :]).then_inc(wide_set, 1)

            chunks(act, widen)

        @block.vector
        def _(dve):
            dve.memset(states[:, 0, :, :, 0], 0.0).then_inc(state_set, 1)
            dve.wait_ge(state_set, 1)
            dve.sem_inc(carried, 1)

            def recur(c, parity):
                dve.wait_ge(vk_set, c + 1)
                dve.wait_ge(carried, c + 1)
                dve.wait_ge(wide_set, (c + 1) * fills + 4)
                for t in range(CHUNK):
                    n = c * CHUNK + (t + 1)

                    def at(name):
                        return wide[name][:, parity, :, :, t]

                    state = states[:, parity, :, :, t]
                    dve.wait_ge(state_set, n)
                    dve.tensor_tensor(s_kk[:, :, :], state, at("kk"), ALU.mult).then_inc(kk_used, 1)
                    dve.tensor_tensor(s_decayed[:, :, :], state, at("wt"), ALU.mult).then_inc(decayed, 1)
                    dve.wait_ge(kk_used, n)
                    dve.tensor_reduce(sa[:, :], s_kk[:, :, :].rearrange("p j b -> p b j"), AX.X, ALU.add
                                      ).then_inc(sa_set, 1)
                    dve.wait_ge(decayed, n)
                    dve.tensor_tensor(s_fed[:, :, :], s_decayed[:, :, :], at("k"), ALU.add)
                    dve.wait_ge(sa_set, n)
                    dve.tensor_tensor(s_rank[:, :, :], sa[:, :].unsqueeze(1).broadcast_to([P, HS, BATCH]), at("b"),
                                      ALU.mult).then_inc(rank_one, 1)
                    dve.wait_ge(rank_one, n)
                    dve.tensor_tensor(states[:, parity, :, :, t + 1], s_fed[:, :, :], s_rank[:, :, :], ALU.add
                                      ).then_inc(state_set, 1)
                dve.wait_ge(state_set, (c + 1) * CHUNK + 1)
                dve.wait_ge(y_set, c + 2)
                dve.tensor_copy(states[:, 1 - parity, :, :, 0], states[:, parity, :, :, CHUNK]).then_inc(carried, 1)

            chunks(dve, recur)

        @block.gpsimd
        def _(pool):
            def feed(c, parity):
                pool.wait_ge(wide_set, c * fills + (fills_each * (names.index("k") + 1) + 4))
                k = wide["k"][:, parity, :, :, :]
                v = kept["v"][:, :, bass.ds(c * CHUNK, CHUNK)].unsqueeze(1).broadcast_to([P, HS, BATCH, CHUNK])
                pool.tensor_tensor(k, k, v, ALU.mult).then_inc(vk_set, 1)

            def read_out(c, parity):
                pool.wait_ge(carried, c + 2)
                r = wide["r"][:, parity, :, :, :]
                pool.tensor_tensor(r, r, states[:, parity, :, :, 1:CHUNK + 1], ALU.mult).then_inc(r_used, 1)
                for n, half in enumerate((4, 2)):
                    pool.wait_ge(r_used, c * 3 + (n + 1))
                    pool.tensor_tensor(r[:, 0:half], r[:, 0:half], r[:, half:2 * half], ALU.add).then_inc(r_used, 1)
                pool.wait_ge(r_used, c * 3 + 3)
                pool.tensor_tensor(kept["kk"][:, :, bass.ds(c * CHUNK, CHUNK)], r[:, 0], r[:, 1], ALU.add
                                   ).then_inc(y_set, 1)

            pool.sem_inc(y_set, 2)
            last = SEQ // CHUNK - 1
            feed(0, 0)
            with pool.Fori(0, last // 2) as pair:
                for parity in range(2):
                    feed(pair * 2 + parity + 1, 1 - parity)
                    read_out(pair * 2 + parity, parity)
            feed(last, 1)
            read_out(last - 1, 0)
            read_out(last, 1)


def mixer_output(nc, shared, mat, vec, kept):
    x = shared["x"]
    with ExitStack() as ctx:
        def sb(name):
            return ctx.enter_context(nc.sbuf_tensor("mixout_" + name, [P, SEQ], F32))

        yc, ysq, ystd, rk, out = (sb(n) for n in ("yc", "ysq", "ystd", "rk", "out"))
        banks = [ctx.enter_context(nc.psum_tensor(f"mixout_bank{n}", [P, 512], F32)) for n in range(4)]

        done, need = chain_steps(ctx, nc, "mixout", OUT_STEPS)
        row_free = ctx.enter_context(nc.semaphore("mixout_row_free"))

        block = ctx.enter_context(nc.Block())

        @block.tensor
        def _(pe):
            with pe.Fori(0, BATCH) as b:
                pe.wait_ge(row_free, b + 1)
                done(pe.matmul(banks[0][:, :], mat["mean"], kept["kk"][:, b, :], start=True, stop=True), "pe_mean")
                need(pe, b, "rk")
                done(pe.matmul(banks[1][:, :], mat["ones"], rk[:, :], start=True, stop=True), "pe_rk")
                need(pe, b, "ysq")
                done(pe.matmul(banks[2][:, :], mat["mean"], ysq[:, :], start=True, stop=True), "pe_var")
                need(pe, b, "gated")
                for T in range(4):
                    last = pe.matmul(banks[3][:, T * P:(T + 1) * P], out[:, T * P:(T + 1) * P], mat["o"],
                                     start=True, stop=True)
                done(last, "pe_out")

        @block.scalar
        def _(act):
            with act.Fori(0, BATCH) as b:
                need(act, b, "yc")
                done(act.activation(ysq[:, :], yc[:, :], ACT.Square), "ysq")
                need(act, b, "var")
                done(act.activation(ystd[:, :], ystd[:, :], ACT.Sqrt), "std")

        @block.vector
        def _(dve):
            dve.memset(out[:, 0:1], 0.0).then_inc(row_free, 1)
            dve.wait_ge(row_free, 1)
            with dve.Fori(0, BATCH) as b:
                dve.wait_ge(row_free, b + 1)
                done(dve.scalar_tensor_tensor(rk[:, :], kept["r"][:, b, :], vec["faaaa"], kept["k"][:, b, :],
                                              ALU.mult, ALU.mult), "rk")
                need(dve, b, "pe_mean")
                done(dve.tensor_tensor(yc[:, :], kept["kk"][:, b, :], banks[0][:, :], ALU.subtract), "yc")
                need(dve, b, "pe_rk")
                done(dve.tensor_tensor(out[:, :], banks[1][:, :], kept["v"][:, b, :], ALU.mult), "bonus")
                need(dve, b, "pe_var")
                done(dve.tensor_scalar(ystd[:, :], banks[2][:, :], EPS_HEAD, None, ALU.add), "var")
                need(dve, b, "std")
                done(dve.reciprocal(ystd[:, :], ystd[:, :]), "inv_std")
                need(dve, b, "inv_std")
                done(dve.tensor_tensor(yc[:, :], yc[:, :], ystd[:, :], ALU.mult), "normed")
                need(dve, b, "normed")
                done(dve.tensor_scalar(yc[:, :], yc[:, :], vec["ln_w"], vec["ln_b"], ALU.mult, ALU.add), "scaled")
                need(dve, b, "scaled", "bonus")
                done(dve.tensor_tensor(yc[:, :], yc[:, :], out[:, :], ALU.add), "summed")
                need(dve, b, "summed")
                done(dve.tensor_tensor(out[:, :], yc[:, :], kept["g"][:, b, :], ALU.mult), "gated")
                need(dve, b, "pe_out")
                rows = x[:, bass.ds(b * 4, 4), :]
                dve.tensor_tensor(rows, banks[3][:, :].rearrange("p (t d) -> p t d", t=4), rows, ALU.add
                                  ).then_inc(row_free, 1)


def setup(nc, shared, x_dram, tables, scales):
    with ExitStack() as ctx:
        base = ctx.enter_context(nc.sbuf_tensor("rot_base", [P, 4, 4, HD], F32))
        qk_scale = ctx.enter_context(nc.sbuf_tensor("qk_scale", [P, 2, DEPTH, HD], F32))
        loaded = ctx.enter_context(nc.semaphore("setup_loaded"))
        block = ctx.enter_context(nc.Block())

        @block.sync
        def _(sp):
            for b in range(BATCH):
                sp.dma_start(shared["x"][:, 4 * b:4 * b + 4, :], x_dram[b].rearrange("(t p) d -> p t d", p=P)
                             ).then_inc(loaded, 16)
            sp.dma_start(shared["ident"][:, :], tables["ident"]).then_inc(loaded, 16)
            sp.dma_start(shared["mask"][:, :], tables["mask"]).then_inc(loaded, 16)
            sp.dma_start(base[:, :, :, :], tables["rot"]).then_inc(loaded, 16)
            for n in range(2):
                sp.dma_start(qk_scale[:, n, :, :], scales[n].partition_broadcast(P)).then_inc(loaded, 16)

        @block.vector
        def _(dve):
            dve.wait_ge(loaded, 16 * 9)
            for layer in range(DEPTH):
                for kind in range(4):
                    s = qk_scale[:, kind // 2, layer, :].rearrange("p (f d) -> p f d", f=2)
                    if kind % 2:
                        s = s[:, ::-1, :]
                    dve.tensor_tensor(shared["rot"][:, layer, :, kind, :].rearrange("p t (f d) -> p t f d", f=2),
                                      base[:, :, kind, :].rearrange("p t (f d) -> p t f d", f=2),
                                      s.unsqueeze(1).broadcast_to([P, 4, 2, HD // 2]), ALU.mult)


def store(nc, shared, out):
    with ExitStack() as ctx:
        stored = ctx.enter_context(nc.semaphore("stored"))
        block = ctx.enter_context(nc.Block())

        @block.sync
        def _(sp):
            for b in range(BATCH):
                sp.dma_start(out[b].rearrange("(t p) d -> p t d", p=P), shared["x"][:, 4 * b:4 * b + 4, :]
                             ).then_inc(stored, 16)
            sp.wait_ge(stored, 16 * BATCH)


def program(nc, ins, out, phases=("retention", "stack0", "mixer", "stack1")):
    with ExitStack() as ctx:
        def sb(name, shape):
            return ctx.enter_context(nc.sbuf_tensor(name, shape, F32))

        shared = {
            "x": sb("x_outer", [P, 16, DIM]),
            "ident": sb("ident", [P, P]),
            "mask": sb("band", [P, 4 * WINDOW]),
            "rot": sb("rot_tables", [P, DEPTH, 4, 4, HD]),
        }
        tables = {k: ins["table_" + k] for k in ("ident", "mask", "rot")}
        setup(nc, shared, ins["L0_attn_a_X"], tables, (ins["L0_ffn_q_scale"], ins["L0_ffn_k_scale"]))
        stack_weights = {k: ins["L0_ffn_" + k] for k in ("Wqkv", "Wo", "W1", "W2", "b1", "b2", "ln_g", "ln_b")}
        for phase in phases:
            if phase == "retention":
                retention(nc, shared, ins)
            elif phase == "mixer":
                mixer(nc, shared, ins)
            else:
                ffn_stack(nc, {**shared, "tag": phase + "_"}, stack_weights)
        store(nc, shared, out)


def shape_tables():
    f = np.float32
    t = {"ident": np.eye(P, dtype=f)}
    q = np.arange(P)[:, None] % WINDOW
    c = np.arange(2 * WINDOW)[None, :]
    seen = (c >= q) & (c <= q + WINDOW)
    seen = np.concatenate([seen, seen & ((np.arange(P)[:, None] >= WINDOW) | (c >= WINDOW))], 1)
    t["mask"] = np.where(seen, f(0), f(-1e30)).astype(f)
    pos = np.arange(SEQ, dtype=f)
    half = np.arange(0, HD, 2, dtype=f)
    freq = (f(1.0) / np.power(f(10000.0), half / f(HD))).astype(f)
    angle = (pos[:, None] * freq[None, :]).astype(f)
    scale = np.power(((half + f(0.4 * HD)) / f(1.4 * HD)).astype(f)[None, :],
                     ((pos - f(SEQ // 2)) / f(WINDOW // 2)).astype(f)[:, None]).astype(f)
    cos, sin = (np.concatenate([g(angle.astype(np.float64))] * 2, -1).astype(f) for g in (np.cos, np.sin))
    scale = np.concatenate([scale, scale], -1)
    sin = sin * np.where(np.arange(HD) < HD // 2, f(-1), f(1))
    kinds = np.stack([cos * scale, sin * scale, cos / scale, sin / scale], 1).astype(f)
    t["rot"] = np.ascontiguousarray(kinds.reshape(4, P, 4, HD).transpose(1, 0, 2, 3))
    half = DIM // 2
    power = pos / f(SEQ)
    scale = np.power(((np.arange(0, DIM, 2, dtype=f) + f(0.4 * DIM)) / f(1.4 * DIM)).astype(f)[None, :],
                     power[:, None]).astype(f)
    freq = (f(1.0) / np.power(f(10000.0), (np.arange(half, dtype=f) / f(half)))).astype(f)
    angle = (pos[:, None] * freq[None, :]).astype(f).astype(np.float64)
    rows = []
    for g in (np.cos, np.sin):
        both = [np.repeat((g(angle).astype(f) * sc).astype(f), 2, -1) for sc in (scale, f(1.0) / scale)]
        rows.append(np.concatenate(both, -1))
    rows[1] = rows[1] * np.where(np.arange(2 * DIM) % 2 == 0, f(-1), f(1))
    t["xpos"] = np.ascontiguousarray(np.stack(rows, 1).reshape(4, P, 2, 2 * DIM).transpose(1, 0, 2, 3)).astype(f)
    offset = np.abs(np.arange(P)[:, None] - np.arange(7 * P)[None, :] + 3 * P)
    t["decay"] = np.power(f(0.9), offset.astype(f)).astype(f)
    head, item = np.arange(P) // HS, np.arange(P) % HS
    same = head[:, None] == head[None, :]
    t["ones"] = same.astype(f)
    t["mean"] = (same / HS).astype(f)
    t["spread"] = np.stack([same & (item[:, None] == i) for i in range(HS)], 1).astype(f)
    t["gather"] = np.stack([same & (item[None, :] == i) for i in range(HS)], 1).astype(f)
    return t


def arrange(inputs):
    f = np.float32
    got = {k: np.asarray(v) for k, v in inputs.items()}
    mixer_in = {k[len("L0_attn_b_"):]: got[k] for k in got if k.startswith("L0_attn_b_")}
    ins = {k: v for k, v in got.items() if not k.startswith("L0_attn_b_")}
    t = shape_tables()

    def placed(parts, by_column):
        m = np.zeros((P, P), f)
        for at, part in parts:
            if by_column:
                m[:, at:at + part.shape[1]] = part
            else:
                m[at:at + part.shape[0], :] = part
        return m

    w = mixer_in
    mats = {
        "maa1": w["maa_w1"].T, "maa2": w["maa_w2"].reshape(P, P),
        "r": w["Wr"].T, "k": w["Wk"].T, "v": w["Wv"].T, "o": w["Wo"].T,
        "gate1": w["gate_w1"].T, "gate2": w["gate_w2"],
        "wa1": placed(((0, w["decay_w1"].T), (64, w["aaa_w1"].T), (96, w["ma_w1"].T)), True),
        "wa2": placed(((0, w["decay_w2"]), (64, w["aaa_w2"]), (96, w["ma_w2"])), False),
        "k1": placed(((0, w["kkk_w1"].T), (32, w["mk_w1"].T)), True),
        "k2": placed(((0, w["kkk_w2"]), (32, w["mk_w2"])), False),
        "ones": t.pop("ones"), "mean": t.pop("mean"),
    }
    vecs = {
        "maa_x": w["time_maa_x"], **{f"maa{g}": w["time_maa"][g, 0, 0] for g in range(4)},
        "decay": w["time_decay"], "faaaa": w["time_faaaa"], "aaaaa": w["time_aaaaa"],
        "misc_a": w["time_misc_a"], "misc_k": w["time_misc_k"], "ln_w": w["ln_w"], "ln_b": w["ln_b"],
    }
    t["mix"] = np.stack([mats[n] for n in MATS], 1)
    t["vec"] = np.stack([vecs[n] for n in VECS], 1)
    ins.update({"table_" + k: np.ascontiguousarray(v) for k, v in t.items()})
    return ins


def kernel(**inputs):
    import concourse.bacc as bacc
    from concourse.bass_utils import run_bass_kernel_spmd

    nc = bacc.Bacc("TRN2", target_bir_lowering=False, num_devices=1)
    arrays = arrange(inputs)
    ins = {k: nc.dram_tensor(k, v.shape, mybir.dt.from_np(v.dtype), kind="ExternalInput").ap()
           for k, v in arrays.items()}
    out = nc.dram_tensor("out", (BATCH, SEQ, DIM), F32, kind="ExternalOutput").ap()
    program(nc, ins, out)
    return run_bass_kernel_spmd(nc, [arrays], core_ids=[0]).results[0]["out"]
```
